# Optimizing a Trainium2 kernel written in Bass

```python
import numpy as np
import jax
import jax.numpy as jnp

def _softmax(x, axis=-1):
    return jax.nn.softmax(x, axis=axis)

def _gelu(x):
    return jax.nn.gelu(x, approximate=True)

def _silu(x):
    return jax.nn.silu(x)

def _sigmoid(x):
    return jax.nn.sigmoid(x)

def _layernorm(x, axis=-1, eps=1e-05):
    m = jnp.mean(x, axis=axis, keepdims=True)
    v = jnp.var(x, axis=axis, keepdims=True)
    return (x - m) / jnp.sqrt(v + eps)

def _scatter_add(tgt, idx, src, axis=0):
    return tgt.at[idx].add(src)

def _segment_sum(src, seg, n):
    return jax.ops.segment_sum(src, seg, n)
kernel_name = 'mk_early_fusion_d2_tok_img768_r4_f1f5f2'

def setup_inputs(seed: int=0):
    np.random.seed(seed)
    _w = jnp.asarray

    def _rec_inputs():
        import jax
        import jax.numpy as jnp
        _rk = jax.random.key(seed)
        x = -0.00016672 + 0.999947 * jax.random.normal(jax.random.fold_in(_rk, 1), (16, 3, 96, 96), jnp.float32)
        txt = 0.000200627 + 0.144369 * jax.random.normal(jax.random.fold_in(_rk, 2), (16, 512, 192), jnp.float32)
        return (x, txt)
    x, txt = _rec_inputs()

    def _L0_tok_setup():
        import jax, jax.numpy as jnp
        import numpy as np
        P = 16
        EPS = 1e-05
        key = jax.random.key(seed)
        ks = jax.random.split(key, 6)
        B, C, H = (64, 3, 96)
        E = 192
        L = (H // P) ** 2
        patch_dim = C * P * P
        return {'x': jax.random.normal(ks[0], (B, C, H, H), dtype=jnp.float32), 'ln_w': jnp.ones((C, H, H), dtype=jnp.float32), 'ln_b': jnp.zeros((C, H, H), dtype=jnp.float32), 'conv_w': jax.random.normal(ks[1], (C, C, 1, 1), dtype=jnp.float32) * 0.1, 'conv_b': jax.random.normal(ks[2], (C,), dtype=jnp.float32) * 0.1, 'proj_w': jax.random.normal(ks[3], (E, patch_dim), dtype=jnp.float32) * 0.02, 'proj_b': jax.random.normal(ks[4], (E,), dtype=jnp.float32) * 0.02, 'pos_emb': jax.random.normal(ks[5], (1, L, E), dtype=jnp.float32) * 0.02}
    _L0_tok_all = _L0_tok_setup()
    _L0_tok_in = {k: v for k, v in _L0_tok_all.items() if k in ('ln_w', 'ln_b', 'conv_w', 'conv_b', 'proj_w', 'proj_b', 'pos_emb')}
    del _L0_tok_all

    def _L0_attn_setup():
        import math
        import jax, jax.numpy as jnp
        import numpy as np
        NUM_HEADS = 12
        EPS = 0.0001

        def softmax_kernel_features(data, proj, is_query):
            d = data.shape[-1]
            data_normalizer = 1.0 / math.sqrt(math.sqrt(d))
            ratio = 1.0 / math.sqrt(proj.shape[0])
            data_dash = jnp.einsum('bhnd,md->bhnm', data_normalizer * data, proj)
            diag_data = jnp.sum(jnp.square(data), axis=-1, keepdims=True) * 0.5 * data_normalizer * data_normalizer
            if is_query:
                stab = jnp.max(data_dash, axis=-1, keepdims=True)
            else:
                stab = jnp.max(data_dash)
            return ratio * (jnp.exp(data_dash - diag_data - stab) + EPS)
        key = jax.random.key(seed)
        k0, k1, k2, k3, k4 = jax.random.split(key, 5)
        B, N, C, H = (8, 1024, 192, NUM_HEADS)
        hd = C // H
        m = int(hd * math.log(hd))
        x = jax.random.normal(k0, (B, N, C), dtype=jnp.float32)
        W_qkv = jax.random.normal(k1, (C, 3 * C), dtype=jnp.float32) / math.sqrt(C)
        W_proj = jax.random.normal(k2, (C, C), dtype=jnp.float32) / math.sqrt(C)
        b_proj = jnp.zeros((C,), dtype=jnp.float32)
        proj_mat = jax.random.normal(k3, (m, hd), dtype=jnp.float32)
        return {'x': x, 'W_qkv': W_qkv, 'W_proj': W_proj, 'b_proj': b_proj, 'proj_mat': proj_mat}
    _L0_attn_all = _L0_attn_setup()
    _L0_attn_in = {k: v for k, v in _L0_attn_all.items() if k in ('W_qkv', 'W_proj', 'b_proj', 'proj_mat')}
    del _L0_attn_all

    def _L0_ffn_setup():
        import jax, jax.numpy as jnp
        import numpy as np
        import math
        B, T, C = (8, 512, 192)
        E = 3
        HD = C // E
        TOPK = 2
        NGLOB = 4

        def _masked_softmax(att, mask):
            att = jnp.where(mask, -jnp.inf, att)
            return jax.nn.softmax(att, axis=-1)
        key = jax.random.key(seed)
        ks = jax.random.split(key, 16)
        s = 0.02
        return {'x': jax.random.normal(ks[0], (B, T, C), jnp.float32), 'Wqk': jax.random.normal(ks[1], (C, 2 * C), jnp.float32) * s, 'bqk': jnp.zeros((2 * C,), jnp.float32), 'Wv': jax.random.normal(ks[2], (E, C, HD), jnp.float32) * s, 'bv': jnp.zeros((E, HD), jnp.float32), 'conv_w': jax.random.normal(ks[3], (HD, 1, 3), jnp.float32) * s, 'conv_b': jnp.zeros((HD,), jnp.float32), 'glob': jax.random.normal(ks[4], (NGLOB, HD), jnp.float32) * 0.02, 'pos_bias': jnp.zeros((64, 64), jnp.float32), 'Wg1': jax.random.normal(ks[5], (C, 32), jnp.float32) * s, 'bg1': jnp.zeros((32,), jnp.float32), 'Wg2': jax.random.normal(ks[6], (32, E), jnp.float32) * s, 'bg2': jnp.zeros((E,), jnp.float32), 'Wp': jax.random.normal(ks[7], (C, C), jnp.float32) * s, 'bp': jnp.zeros((C,), jnp.float32)}
    _L0_ffn_all = _L0_ffn_setup()
    _L0_ffn_in = {k: v for k, v in _L0_ffn_all.items() if k in ('Wqk', 'bqk', 'Wv', 'bv', 'conv_w', 'conv_b', 'glob', 'pos_bias', 'Wg1', 'bg1', 'Wg2', 'bg2', 'Wp', 'bp')}
    del _L0_ffn_all

    def _L1_attn_setup():
        import jax, jax.numpy as jnp
        import numpy as np
        N_HEADS = 12
        key = jax.random.key(seed)
        ks = jax.random.split(key, 13)
        B, N, D, H = (8, 256, 192, N_HEADS)
        s = 0.05
        return {'x': jax.random.normal(ks[0], (B, N, D), jnp.float32), 'wq': jax.random.normal(ks[1], (D, D), jnp.float32) * s, 'bq': jax.random.normal(ks[2], (D,), jnp.float32) * s, 'wk': jax.random.normal(ks[3], (D, D), jnp.float32) * s, 'bk': jax.random.normal(ks[4], (D,), jnp.float32) * s, 'wv': jax.random.normal(ks[5], (D, D), jnp.float32) * s, 'bv': jax.random.normal(ks[6], (D,), jnp.float32) * s, 'wo': jax.random.normal(ks[7], (D, D), jnp.float32) * s, 'bo': jax.random.normal(ks[8], (D,), jnp.float32) * s, 'th1_w': jax.random.normal(ks[9], (H, H), jnp.float32) * (1.0 / H ** 0.5), 'th1_b': jax.random.normal(ks[10], (H,), jnp.float32) * s, 'th2_w': jax.random.normal(ks[11], (H, H), jnp.float32) * (1.0 / H ** 0.5), 'th2_b': jax.random.normal(ks[12], (H,), jnp.float32) * s}
    _L1_attn_all = _L1_attn_setup()
    _L1_attn_in = {k: v for k, v in _L1_attn_all.items() if k in ('wq', 'bq', 'wk', 'bk', 'wv', 'bv', 'wo', 'bo', 'th1_w', 'th1_b', 'th2_w', 'th2_b')}
    del _L1_attn_all

    def _L1_ffn_setup():
        import jax, jax.numpy as jnp
        import numpy as np
        D_MODEL = 192
        D_FF = 768
        N_EXPERTS = 9
        key = jax.random.key(seed)
        ks = jax.random.split(key, 7)
        scale = 0.02
        return {'x': jax.random.normal(ks[0], (2, 256, D_MODEL), jnp.float32), 'Ws': jax.random.normal(ks[1], (D_MODEL, N_EXPERTS), jnp.float32) * scale, 'bs': jnp.zeros((N_EXPERTS,), jnp.float32), 'W1': jax.random.normal(ks[2], (N_EXPERTS, D_MODEL, D_FF), jnp.float32) * scale, 'b1': jnp.zeros((N_EXPERTS, D_FF), jnp.float32), 'W2': jax.random.normal(ks[3], (N_EXPERTS, D_FF, D_MODEL), jnp.float32) * scale, 'b2': jnp.zeros((N_EXPERTS, D_MODEL), jnp.float32)}
    _L1_ffn_all = _L1_ffn_setup()
    _L1_ffn_in = {k: v for k, v in _L1_ffn_all.items() if k in ('Ws', 'bs', 'W1', 'b1', 'W2', 'b2')}
    del _L1_ffn_all
    return {'x': x, 'txt': txt, 'L0_tok_ln_w': _L0_tok_in['ln_w'], 'L0_tok_ln_b': _L0_tok_in['ln_b'], 'L0_tok_conv_w': _L0_tok_in['conv_w'], 'L0_tok_conv_b': _L0_tok_in['conv_b'], 'L0_tok_proj_w': _L0_tok_in['proj_w'], 'L0_tok_proj_b': _L0_tok_in['proj_b'], 'L0_tok_pos_emb': _L0_tok_in['pos_emb'], 'L0_attn_W_qkv': _L0_attn_in['W_qkv'], 'L0_attn_W_proj': _L0_attn_in['W_proj'], 'L0_attn_b_proj': _L0_attn_in['b_proj'], 'L0_attn_proj_mat': _L0_attn_in['proj_mat'], 'L0_ffn_Wqk': _L0_ffn_in['Wqk'], 'L0_ffn_bqk': _L0_ffn_in['bqk'], 'L0_ffn_Wv': _L0_ffn_in['Wv'], 'L0_ffn_bv': _L0_ffn_in['bv'], 'L0_ffn_conv_w': _L0_ffn_in['conv_w'], 'L0_ffn_conv_b': _L0_ffn_in['conv_b'], 'L0_ffn_glob': _L0_ffn_in['glob'], 'L0_ffn_pos_bias': _L0_ffn_in['pos_bias'], 'L0_ffn_Wg1': _L0_ffn_in['Wg1'], 'L0_ffn_bg1': _L0_ffn_in['bg1'], 'L0_ffn_Wg2': _L0_ffn_in['Wg2'], 'L0_ffn_bg2': _L0_ffn_in['bg2'], 'L0_ffn_Wp': _L0_ffn_in['Wp'], 'L0_ffn_bp': _L0_ffn_in['bp'], 'L1_attn_wq': _L1_attn_in['wq'], 'L1_attn_bq': _L1_attn_in['bq'], 'L1_attn_wk': _L1_attn_in['wk'], 'L1_attn_bk': _L1_attn_in['bk'], 'L1_attn_wv': _L1_attn_in['wv'], 'L1_attn_bv': _L1_attn_in['bv'], 'L1_attn_wo': _L1_attn_in['wo'], 'L1_attn_bo': _L1_attn_in['bo'], 'L1_attn_th1_w': _L1_attn_in['th1_w'], 'L1_attn_th1_b': _L1_attn_in['th1_b'], 'L1_attn_th2_w': _L1_attn_in['th2_w'], 'L1_attn_th2_b': _L1_attn_in['th2_b'], 'L1_ffn_Ws': _L1_ffn_in['Ws'], 'L1_ffn_bs': _L1_ffn_in['bs'], 'L1_ffn_W1': _L1_ffn_in['W1'], 'L1_ffn_b1': _L1_ffn_in['b1'], 'L1_ffn_W2': _L1_ffn_in['W2'], 'L1_ffn_b2': _L1_ffn_in['b2']}

def reference(x, txt, L0_tok_ln_w, L0_tok_ln_b, L0_tok_conv_w, L0_tok_conv_b, L0_tok_proj_w, L0_tok_proj_b, L0_tok_pos_emb, L0_attn_W_qkv, L0_attn_W_proj, L0_attn_b_proj, L0_attn_proj_mat, L0_ffn_Wqk, L0_ffn_bqk, L0_ffn_Wv, L0_ffn_bv, L0_ffn_conv_w, L0_ffn_conv_b, L0_ffn_glob, L0_ffn_pos_bias, L0_ffn_Wg1, L0_ffn_bg1, L0_ffn_Wg2, L0_ffn_bg2, L0_ffn_Wp, L0_ffn_bp, L1_attn_wq, L1_attn_bq, L1_attn_wk, L1_attn_bk, L1_attn_wv, L1_attn_bv, L1_attn_wo, L1_attn_bo, L1_attn_th1_w, L1_attn_th1_b, L1_attn_th2_w, L1_attn_th2_b, L1_ffn_Ws, L1_ffn_bs, L1_ffn_W1, L1_ffn_b1, L1_ffn_W2, L1_ffn_b2):
    import jax
    import jax.numpy as jnp

    def _L0_tok_ref(x, ln_w, ln_b, conv_w, conv_b, proj_w, proj_b, pos_emb):
        import jax, jax.numpy as jnp
        import numpy as np
        P = 16
        EPS = 1e-05
        B, C, H, W = x.shape
        mu = jnp.mean(x, axis=(1, 2, 3), keepdims=True)
        var = jnp.var(x, axis=(1, 2, 3), keepdims=True)
        xn = (x - mu) * jax.lax.rsqrt(var + EPS) * ln_w + ln_b
        w = conv_w[:, :, 0, 0]
        xc = jnp.einsum('bchw,oc->bohw', xn, w) + conv_b[None, :, None, None]
        hp, wp = (H // P, W // P)
        patches = xc.reshape(B, C, hp, P, wp, P)
        patches = patches.transpose(0, 2, 4, 1, 3, 5).reshape(B, hp * wp, C * P * P)
        tokens = jnp.einsum('bld,ed->ble', patches, proj_w) + proj_b
        return tokens + pos_emb

    def _L0_attn_ref(x, W_qkv, W_proj, b_proj, proj_mat):
        import math
        import jax, jax.numpy as jnp
        import numpy as np
        NUM_HEADS = 12
        EPS = 0.0001

        def softmax_kernel_features(data, proj, is_query):
            d = data.shape[-1]
            data_normalizer = 1.0 / math.sqrt(math.sqrt(d))
            ratio = 1.0 / math.sqrt(proj.shape[0])
            data_dash = jnp.einsum('bhnd,md->bhnm', data_normalizer * data, proj)
            diag_data = jnp.sum(jnp.square(data), axis=-1, keepdims=True) * 0.5 * data_normalizer * data_normalizer
            if is_query:
                stab = jnp.max(data_dash, axis=-1, keepdims=True)
            else:
                stab = jnp.max(data_dash)
            return ratio * (jnp.exp(data_dash - diag_data - stab) + EPS)
        B, N, C = x.shape
        H = NUM_HEADS
        hd = C // H
        qkv = (x @ W_qkv).reshape(B, N, 3, H, hd)
        qkv = jnp.transpose(qkv, (2, 0, 3, 1, 4))
        q, k, v = (qkv[0], qkv[1], qkv[2])
        q1 = softmax_kernel_features(q, proj_mat, is_query=True)
        k1 = softmax_kernel_features(k, proj_mat, is_query=False)
        kv = jnp.einsum('bhnm,bhnd->bhmd', k1, v)
        ksum = jnp.sum(k1, axis=2)
        z = 1.0 / jnp.einsum('bhnm,bhm->bhn', q1, ksum)
        out = jnp.einsum('bhnm,bhmd->bhnd', q1, kv) * z[..., None]
        out = jnp.transpose(out, (0, 2, 1, 3)).reshape(B, N, C)
        return out @ W_proj + b_proj

    def _L0_ffn_ref(x, Wqk, bqk, Wv, bv, conv_w, conv_b, glob, pos_bias, Wg1, bg1, Wg2, bg2, Wp, bp):
        import jax, jax.numpy as jnp
        import numpy as np
        import math
        B, T, C = (8, 512, 192)
        E = 3
        HD = C // E
        TOPK = 2
        NGLOB = 4

        def _masked_softmax(att, mask):
            att = jnp.where(mask, -jnp.inf, att)
            return jax.nn.softmax(att, axis=-1)
        Bx, Tx, Cx = x.shape
        scale = 1.0 / math.sqrt(HD)
        gate = jax.nn.softmax(jax.nn.relu(x @ Wg1 + bg1) @ Wg2 + bg2, axis=-1)
        top_w, top_i = jax.lax.top_k(gate, TOPK)
        top_w = jax.nn.softmax(top_w, axis=-1)
        qk = x @ Wqk + bqk
        q, k = (qk[..., :Cx], qk[..., Cx:])
        q = q.reshape(Bx, Tx, E, HD)
        k = k.reshape(Bx, Tx, E, HD)
        rows = jnp.arange(Tx)[:, None]
        ys = []
        for e in range(E):
            qe = q[:, :, e]
            ke = k[:, :, e]
            ve = x @ Wv[e] + bv[e]
            if e == 0:
                qc = jnp.transpose(qe, (0, 2, 1))
                qc = jax.lax.conv_general_dilated(qc, conv_w, window_strides=(1,), padding=((1, 1),), feature_group_count=HD, dimension_numbers=('NCH', 'OIH', 'NCH'))
                qe = jnp.transpose(qc + conv_b[None, :, None], (0, 2, 1))
            elif e == 1:
                gb = jnp.broadcast_to(glob[None], (Bx, NGLOB, HD))
                ke = jnp.concatenate([ke, gb], axis=1)
                ve = jnp.concatenate([ve, gb], axis=1)
            att = jnp.einsum('btd,bsd->bts', qe, ke) * scale
            if e == 2 and Tx <= 64:
                att = att + pos_bias[:Tx, :Tx][None]
            S = att.shape[-1]
            mask = jnp.arange(S)[None, :] > rows
            att = _masked_softmax(att, mask[None])
            ys.append(jnp.einsum('bts,bsd->btd', att, ve))
        ys = jnp.stack(ys, axis=2)
        w_e = jnp.sum(jax.nn.one_hot(top_i, E, dtype=x.dtype) * top_w[..., None], axis=-2)
        combined = (ys * w_e[..., None]).reshape(Bx, Tx, Cx)
        return combined @ Wp + bp

    def _L1_attn_ref(x, wq, bq, wk, bk, wv, bv, wo, bo, th1_w, th1_b, th2_w, th2_b):
        import jax, jax.numpy as jnp
        import numpy as np
        N_HEADS = 12
        B, N, D = x.shape
        H = N_HEADS
        hd = D // H
        scale = hd ** (-0.5)

        def split_heads(y):
            return y.reshape(B, N, H, hd).transpose(0, 2, 1, 3)
        q = split_heads(x @ wq.T + bq)
        k = split_heads(x @ wk.T + bk)
        v = split_heads(x @ wv.T + bv)
        attn = jnp.einsum('bhnd,bhmd->bhnm', q, k) * scale
        attn = jnp.einsum('gh,bhnm->bgnm', th1_w, attn) + th1_b[None, :, None, None]
        attn = jax.nn.softmax(attn, axis=-1)
        attn = jnp.einsum('gh,bhnm->bgnm', th2_w, attn) + th2_b[None, :, None, None]
        out = jnp.einsum('bhnm,bhmd->bhnd', attn, v)
        out = out.transpose(0, 2, 1, 3).reshape(B, N, D)
        return out @ wo.T + bo

    def _L1_ffn_ref(x, Ws, bs, W1, b1, W2, b2):
        import jax, jax.numpy as jnp
        import numpy as np
        D_MODEL = 192
        D_FF = 768
        N_EXPERTS = 9
        B, S, d = x.shape
        xt = x.reshape(-1, d)
        route_prob = jax.nn.softmax(xt @ Ws + bs, axis=-1)
        p = jnp.max(route_prob, axis=-1)
        routes = jnp.argmax(route_prob, axis=-1)
        h = jax.nn.gelu(jnp.einsum('td,edf->tef', xt, W1) + b1, approximate=False)
        out = jnp.einsum('tef,efd->ted', h, W2) + b2
        common = out[:, 0, :]
        sel = jnp.take_along_axis(out, routes[:, None, None], axis=1)[:, 0, :]
        scaling = (p / jax.lax.stop_gradient(p))[:, None]
        pe = p[:, None]
        final = jnp.where((routes == 0)[:, None], common * scaling, pe * sel + (1.0 - pe) * common)
        return final.reshape(B, S, d)
    h = _L0_tok_ref(x, L0_tok_ln_w, L0_tok_ln_b, L0_tok_conv_w, L0_tok_conv_b, L0_tok_proj_w, L0_tok_proj_b, L0_tok_pos_emb)
    h = jnp.concatenate([h, txt], axis=1)
    h = h + _L0_attn_ref(_layernorm(h, axis=-1), L0_attn_W_qkv, L0_attn_W_proj, L0_attn_b_proj, L0_attn_proj_mat)
    h = h + _L0_ffn_ref(_layernorm(h, axis=-1), L0_ffn_Wqk, L0_ffn_bqk, L0_ffn_Wv, L0_ffn_bv, L0_ffn_conv_w, L0_ffn_conv_b, L0_ffn_glob, L0_ffn_pos_bias, L0_ffn_Wg1, L0_ffn_bg1, L0_ffn_Wg2, L0_ffn_bg2, L0_ffn_Wp, L0_ffn_bp)
    h = h + _L1_attn_ref(_layernorm(h, axis=-1), L1_attn_wq, L1_attn_bq, L1_attn_wk, L1_attn_bk, L1_attn_wv, L1_attn_bv, L1_attn_wo, L1_attn_bo, L1_attn_th1_w, L1_attn_th1_b, L1_attn_th2_w, L1_attn_th2_b)
    h = h + _L1_ffn_ref(_layernorm(h, axis=-1), L1_ffn_Ws, L1_ffn_bs, L1_ffn_W1, L1_ffn_b1, L1_ffn_W2, L1_ffn_b2)
    return h

_drawn_inputs = setup_inputs


def setup_inputs(seed=0):
    import zlib

    import numpy as np

    out = dict(_drawn_inputs(seed))
    spreads = {'L0_tok_ln_w': (1.0, 0.6),
     'L0_tok_ln_b': (0.0, 0.8),
     'L0_attn_b_proj': (0.0, 0.1),
     'L0_ffn_bqk': (0.0, 0.8),
     'L0_ffn_bv': (0.0, 0.1),
     'L0_ffn_conv_b': (0.0, 2.0),
     'L0_ffn_pos_bias': (0.0, 0.1),
     'L0_ffn_bg1': (0.0, 0.8),
     'L0_ffn_bg2': (0.0, 0.432),
     'L0_ffn_bp': (0.0, 0.1),
     'L1_ffn_bs': (0.0, 0.8),
     'L1_ffn_b1': (0.0, 0.8),
     'L1_ffn_b2': (0.0, 0.618)}
    factors = {'L0_tok_pos_emb': 4.559,
     'L0_ffn_Wqk': 8.0,
     'L0_ffn_conv_w': 41.38,
     'L0_ffn_Wg1': 8.0,
     'L0_ffn_Wg2': 8.0,
     'L1_attn_wq': 8.0,
     'L1_attn_bq': 8.0,
     'L1_attn_wk': 8.0,
     'L1_attn_bk': 64.0,
     'L1_attn_bo': 7.817,
     'L1_attn_th1_w': 8.0,
     'L1_attn_th1_b': 64.0,
     'L1_ffn_Ws': 8.0,
     'L1_ffn_W1': 5.732,
     'L1_ffn_W2': 5.192}
    for name, (base, spread) in spreads.items():
        noise = np.random.default_rng([zlib.crc32(name.encode()), seed]).standard_normal(out[name].shape)
        drawn = base * np.exp(spread * noise) if base else spread * noise
        out[name] = jnp.asarray(drawn.astype(out[name].dtype))
    for name, factor in factors.items():
        out[name] = (out[name] * factor).astype(out[name].dtype)
    return out
```

```python
from contextlib import ExitStack

import concourse.bass as bass
from concourse import mybir
from concourse.alu_op_type import AluOpType as ALU

ACT = mybir.ActivationFunctionType
AX = mybir.AxisListType
F32 = mybir.dt.float32

B = 16
IMG, PATCH, CH = 96, 16, 3
SIDE = IMG // PATCH
NPATCH = SIDE * SIDE
PIX = CH * PATCH * PATCH
NTXT = 512
N = NPATCH + NTXT
R = 110
T = 5
NP = R * T
LAST = N - R * (T - 1)
D = 192
C = 96
KC = D // C
H = 12
HD = D // H
M = 44
HM = H * M // KC
E0 = 3
HD0 = D // E0
HID = 32
E1 = 9
FF = 768
FC = FF // 128
NEG = -1.0e30

QT = 10
QG = 8
NG = 7
NQ = QT * QG * NG
HQ = H * QT


def rows(t):
    return LAST if t == T - 1 else R


class Signal:

    def __init__(self, nc, name, per, primed=False):
        self.sem, self.per, self.first = nc.alloc_semaphore(name), per, int(primed)

    def prime(self, eng):
        eng.sem_inc(self.sem, self.per)

    def now(self, turn, k):
        return turn * self.per + (self.first * self.per + k)

    def before(self, turn, k):
        assert self.first and k >= 1
        return turn * self.per + k


class Chain:

    def __init__(self, eng, marks, turn):
        self.eng, self.marks, self.turn, self.n = eng, marks, turn, 0

    def __call__(self, ins):
        self.n += 1
        ins.then_inc(self.marks.sem, 1)
        self.eng.wait_ge(self.marks.sem, self.marks.now(self.turn, self.n))

    def end(self):
        assert self.n == self.marks.per, (self.n, self.marks.per)


def stand(k, eng):
    eng.sem_inc(k.passed, 1)


class Core:
    pass


def chunked(w):
    return w.rearrange("(c p) n -> p c n", c=KC)


def row(v):
    return v.rearrange("(a n) -> a n", a=1)



def setup(k, A):
    nc = k.nc
    k.X = nc.alloc_sbuf_tensor("X", [R, B * T, D], F32)
    k.ident = nc.alloc_sbuf_tensor("ident", [128, 128], F32)
    k.causal = nc.alloc_sbuf_tensor("causal", [R, R], F32)
    k.mhalf = nc.alloc_sbuf_tensor("mhalf", [128, 16], F32)
    k.passed = nc.alloc_semaphore("passed")
    k.PS = nc.alloc_psum_tensor("PS", [128, 8, 512], F32)
    zeroed = nc.alloc_semaphore("zeroed")
    k.text_in = nc.alloc_semaphore("text_in")
    filled = nc.alloc_semaphore("filled")
    with nc.Block() as block:
        @block.gpsimd
        def _(pool):
            pool.memset(k.ident[:], 0.0).then_inc(filled, 1)
            pool.memset(k.causal[:], 0.0).then_inc(filled, 1)
            pool.memset(k.mhalf[:], -0.5)
            pool.wait_ge(filled, 2)
            pool.affine_select(out=k.ident[:], in_=k.ident[:], compare_op=ALU.not_equal, fill=1.0,
                               base=0, pattern=[[-1, 128]], channel_multiplier=1)
            pool.affine_select(out=k.causal[:], in_=k.causal[:], compare_op=ALU.is_ge, fill=NEG,
                               base=0, pattern=[[-1, R]], channel_multiplier=1)

        @block.vector
        def _(dve):
            dve.memset(k.X[C:R, T - 1::T, :], 0.0).then_inc(zeroed, 1)

        @block.sync
        def _(sp):
            txt = A["txt"].rearrange("b n d -> n b d")
            sp.dma_start(k.X[NPATCH:R, 0::T, :], txt[0:R - NPATCH]).then_inc(k.text_in, 16)
            for t in range(1, T):
                if t == T - 1:
                    sp.wait_ge(zeroed, 1)
                n0 = t * R - NPATCH
                sp.dma_start(k.X[0:rows(t), t::T, :], txt[n0:n0 + rows(t)]).then_inc(k.text_in, 16)
            sp.wait_ge(k.text_in, 16 * T)



def patch_tokens(k, A):
    nc, X, PS = k.nc, k.X, k.PS
    KP = PIX // 128
    with ExitStack() as ctx:
        def sb(name, shape):
            return ctx.enter_context(nc.sbuf_tensor(name, shape, F32))

        projT = sb("tk_projT", [128, KP, D])
        weff = sb("tk_weff", [128, KP, D])
        cw = sb("tk_cw", [128, CH * CH])
        cb = sb("tk_cb", [128, CH])
        cbw = sb("tk_cbw", [128, KP, NPATCH])
        posb = sb("tk_posb", [NPATCH, D])
        pb = sb("tk_pb", [NPATCH, D])
        lnw = sb("tk_lnw", [NPATCH, PIX])
        lnb = sb("tk_lnb", [NPATCH, PIX])
        mean_of = sb("tk_mean_of", [NPATCH, NPATCH])
        img = sb("tk_img", [NPATCH, B, PIX])
        xn = sb("tk_xn", [NPATCH, PIX])
        xT = sb("tk_xT", [128, KP, NPATCH])
        st = sb("tk_st", [NPATCH, 2, 6])
        mv = sb("tk_mv", [NPATCH, 2])
        avg = sb("tk_avg", [NPATCH, 2])
        var = sb("tk_var", [NPATCH, 2])
        rstd = sb("tk_rstd", [NPATCH, 1])

        w_in = nc.alloc_semaphore("tk_w_in")
        img_in = nc.alloc_semaphore("tk_img_in")
        biased = nc.alloc_semaphore("tk_biased")
        copied = nc.alloc_semaphore("tk_copied")
        made = nc.alloc_semaphore("tk_made")

        NW = 16 * 7

        with nc.Block() as block:
            @block.sync
            def _(sp):
                sp.dma_start(projT[:], A["tok_proj_wT"].rearrange("(q p) n -> p q n", p=128)).then_inc(w_in, 16)
                sp.dma_start(cw[:], row(A["L0_tok_conv_w"].rearrange("o c y x -> (o c y x)"))
                             .broadcast_to([128, CH * CH])).then_inc(w_in, 16)
                sp.dma_start(cb[:], row(A["L0_tok_conv_b"]).broadcast_to([128, CH])).then_inc(w_in, 16)
                sp.dma_start(pb[:], row(A["L0_tok_proj_b"]).broadcast_to([NPATCH, D])).then_inc(w_in, 16)
                sp.dma_start(posb[:], A["L0_tok_pos_emb"][0]).then_inc(w_in, 16)
                sp.dma_start(lnw[:], A["tok_ln_w_patches"]).then_inc(w_in, 16)
                sp.dma_start(lnb[:], A["tok_ln_b_patches"]).then_inc(w_in, 16)
                sp.wait_ge(w_in, NW)

            @block.scalar
            def _(act):
                act.dma_start(img[:], A["x_patches"].rearrange("b p n -> p b n")).then_inc(img_in, 16)
                act.wait_ge(img_in, 16)

            @block.gpsimd
            def _(pool):
                pool.memset(mean_of[:], 1.0 / NPATCH)

            @block.tensor
            def _(pe):
                pe.wait_ge(made, 1)
                for q in range(KP):
                    ins = pe.matmul(PS[0:NPATCH, 6, 0:D], cbw[:, q, :], projT[:, q, :],
                                    start=q == 0, stop=q == KP - 1)
                ins.then_inc(biased, 1)

            @block.vector
            def _(dve):
                dve.memset(cbw[:], 0.0).then_inc(copied, 1)
                dve.wait_ge(w_in, NW)
                dve.wait_ge(copied, 1)
                for q in range(KP):
                    ins = dve.tensor_scalar(cbw[:, q, :], cbw[:, q, :], cb[:, q // 2:q // 2 + 1], None, ALU.add)
                ins.then_inc(made, 1)
                n = 1
                for c in range(CH):
                    w = weff[:, 2 * c:2 * c + 2, :]
                    for o in range(CH):
                        s = cw[:, o * CH + c:o * CH + c + 1]
                        p = projT[:, 2 * o:2 * o + 2, :]
                        if o == 0:
                            dve.tensor_scalar(w, p, s, None, ALU.mult).then_inc(copied, 1)
                        else:
                            dve.scalar_tensor_tensor(w, p, s, w, ALU.mult, ALU.add).then_inc(copied, 1)
                        n += 1
                        dve.wait_ge(copied, n)
                dve.tensor_tensor(posb[:], posb[:], pb[:], ALU.add).then_inc(copied, 1)
                dve.wait_ge(copied, n + 1)
                dve.wait_ge(biased, 1)
                dve.tensor_tensor(posb[:], PS[0:NPATCH, 6, 0:D], posb[:], ALU.add).then_inc(copied, 1)

        dv = Signal(nc, "tk_dve", 12)
        stats = Signal(nc, "tk_stats", 1)
        averaged = Signal(nc, "tk_averaged", 1)
        varr = Signal(nc, "tk_varr", 1)
        powed = Signal(nc, "tk_powed", 1)
        normed = Signal(nc, "tk_normed", 1)
        tr = Signal(nc, "tk_tr", 1)
        trc = Signal(nc, "tk_trc", 1)
        prod = Signal(nc, "tk_prod", 1)
        added = Signal(nc, "tk_added", 1, primed=True)
        with nc.Block() as block:
            @block.vector
            def _(dve):
                added.prime(dve)
                with dve.Fori(0, B) as b:
                    step = Chain(dve, dv, b)
                    im = img[:, b, :]
                    dve.bn_stats(st[:, 0, :], im[:, 0:PIX // 2])
                    step(dve.bn_stats(st[:, 1, :], im[:, PIX // 2:PIX]))
                    stand(k, dve)
                    step(dve.bn_aggr(mv[:], st[:]))
                    step(dve.scalar_tensor_tensor(mv[:, 1:2], mv[:, 0:1], mv[:, 0:1], mv[:, 1:2], ALU.mult, ALU.add))
                    dve.sem_inc(stats.sem, 1)
                    dve.wait_ge(averaged.sem, averaged.now(b, 1))
                    step(dve.tensor_copy(avg[:], PS[0:NPATCH, 7, 0:2]))
                    step(dve.tensor_tensor(var[:, 0:1], avg[:, 0:1], avg[:, 0:1], ALU.mult))
                    step(dve.tensor_tensor(var[:, 1:2], avg[:, 1:2], var[:, 0:1], ALU.subtract))
                    step(dve.tensor_scalar(var[:, 1:2], var[:, 1:2], 1e-5, None, ALU.add))
                    dve.sem_inc(varr.sem, 1)
                    dve.wait_ge(powed.sem, powed.now(b, 1))
                    step(dve.tensor_scalar(xn[:], im, avg[:, 0:1], rstd[:, 0:1], ALU.subtract, ALU.mult))
                    step(dve.tensor_tensor(xn[:], xn[:], lnw[:], ALU.mult))
                    step(dve.tensor_tensor(xn[:], xn[:], lnb[:], ALU.add))
                    dve.sem_inc(normed.sem, 1)
                    dve.wait_ge(tr.sem, tr.now(b, 1))
                    step(dve.tensor_copy(xT[:], PS[:, 0, 0:KP * NPATCH].rearrange("p (q n) -> p q n", n=NPATCH)))
                    dve.sem_inc(trc.sem, 1)
                    dve.wait_ge(prod.sem, prod.now(b, 1))
                    step(dve.tensor_tensor(X[0:NPATCH, b * T, :], PS[0:NPATCH, 1, 0:D], posb[:], ALU.add))
                    dve.sem_inc(added.sem, 1)
                    step.end()

            @block.gpsimd
            def _(pool):
                with pool.Fori(0, B) as b:
                    pool.wait_ge(varr.sem, varr.now(b, 1))
                    pool.tensor_tensor(rstd[:], var[:, 1:2], k.mhalf[0:NPATCH, 0:1], ALU.pow).then_inc(powed.sem, 1)

            @block.tensor
            def _(pe):
                with pe.Fori(0, B) as b:
                    pe.wait_ge(stats.sem, stats.now(b, 1))
                    stand(k, pe)
                    pe.matmul(PS[0:NPATCH, 7, 0:2], mean_of[:], mv[:], start=True, stop=True).then_inc(averaged.sem, 1)
                    pe.wait_ge(normed.sem, normed.now(b, 1))
                    stand(k, pe)
                    for q in range(KP):
                        ins = pe.transpose(PS[:, 0, q * NPATCH:(q + 1) * NPATCH], xn[:, q * 128:(q + 1) * 128],
                                           k.ident[0:NPATCH, 0:NPATCH])
                    ins.then_inc(tr.sem, 1)
                    pe.wait_ge(trc.sem, trc.now(b, 1))
                    pe.wait_ge(added.sem, added.before(b, 1))
                    for q in range(KP):
                        ins = pe.matmul(PS[0:NPATCH, 1, 0:D], xT[:, q, :], weff[:, q, :],
                                        start=q == 0, stop=q == KP - 1)
                    ins.then_inc(prod.sem, 1)


class Norm:

    def __init__(self, k, ctx, name):
        nc = k.nc
        self.k = k
        def sb(n, shape):
            return ctx.enter_context(nc.sbuf_tensor(name + n, shape, F32))
        self.st = sb("st", [R, T, 6])
        self.mv = sb("mv", [R, T, 2])
        self.ve = sb("ve", [R, T])
        self.rstd = sb("rstd", [R, T])
        self.xn = sb("xn", [R, T, D])
        self.xT = sb("xT", [C + 1, KC, NP])
        self.dv = Signal(nc, name + "nd", 3)
        self.var_ready = Signal(nc, name + "var", 1)
        self.rstd_ready = Signal(nc, name + "rstd", 1)
        self.xn_ready = Signal(nc, name + "xn", T)
        self.turned = Signal(nc, name + "turned", 3, primed=True)
        self.xT_ready = Signal(nc, name + "xT", 3)

    def dve(self, dve, b):
        k = self.k
        step = Chain(dve, self.dv, b)
        for t in range(T):
            ins = dve.bn_stats(self.st[:, t, :], k.X[:, b * T + t, :])
        step(ins)
        stand(k, dve)
        for t in range(T):
            ins = dve.bn_aggr(self.mv[:, t, :], self.st[:, t, :])
        step(ins)
        step(dve.tensor_scalar(self.ve[:], self.mv[:, :, 1], 1e-5, None, ALU.add))
        step.end()
        dve.sem_inc(self.var_ready.sem, 1)
        dve.wait_ge(self.rstd_ready.sem, self.rstd_ready.now(b, 1))
        dve.wait_ge(self.turned.sem, self.turned.before(b, 3))
        for t in range(T):
            dve.tensor_scalar(self.xn[:, t, :], k.X[:, b * T + t, :], self.mv[:, t, 0:1], self.rstd[:, t:t + 1],
                              ALU.subtract, ALU.mult).then_inc(self.xn_ready.sem, 1)

    def pool(self, pool, b):
        pool.wait_ge(self.var_ready.sem, self.var_ready.now(b, 1))
        pool.tensor_tensor(self.rstd[:], self.ve[:], self.k.mhalf[0:R, 0:T], ALU.pow).then_inc(self.rstd_ready.sem, 1)

    def pe(self, pe, b):
        PS, ident = self.k.PS, self.k.ident
        for t in range(T):
            pe.wait_ge(self.xn_ready.sem, self.xn_ready.now(b, t + 1))
            for c in range(KC):
                bank, at = (c, t * R) if t < T - 1 else (2, c * R)
                ins = pe.transpose(PS[0:C, bank, at:at + R], self.xn[:, t, c * C:(c + 1) * C], ident[0:R, 0:R])
                if t >= T - 2 and not (t == T - 1 and c == 0):
                    ins.then_inc(self.turned.sem, 1)

    def act(self, act, b):
        PS, W = self.k.PS, (T - 1) * R
        for c in range(KC):
            act.wait_ge(self.turned.sem, self.turned.now(b, c + 1))
            act.activation(self.xT[0:C, c, 0:W], PS[0:C, c, 0:W], ACT.Copy).then_inc(self.xT_ready.sem, 1)
        act.wait_ge(self.turned.sem, self.turned.now(b, 3))
        act.activation(self.xT[0:C, :, W:NP], PS[0:C, 2, 0:KC * R].rearrange("p (c n) -> p c n", c=KC), ACT.Copy) \
           .then_inc(self.xT_ready.sem, 1)


def kin(c):
    return C + 1 if c == KC - 1 else C



def performer(k, A):
    nc, X, PS, ident = k.nc, k.X, k.PS, k.ident
    outer = ExitStack()

    def keep(name, shape):
        return outer.enter_context(nc.sbuf_tensor(name, shape, F32))

    wqkv = keep("pf_wqkv", [C, KC, 3 * D])
    wf = keep("pf_wf", [C, KC, 2, KC, HM])
    wp = keep("pf_wp", [C + 1, KC, D])
    nstab = keep("pf_nstab", [128, 1])
    kmax = keep("pf_kmax", [128, B * T])
    mx = keep("pf_mx", [128, 2])

    with ExitStack() as ctx:
        feat = ctx.enter_context(nc.sbuf_tensor("pf_feat", [C, HM], F32))
        wT = ctx.enter_context(nc.sbuf_tensor("pf_wT", [C, 2, KC, D], F32))
        w_in, z, tr, cp, ml = (nc.alloc_semaphore("pf_" + n) for n in ("w_in", "z", "tr", "cp", "ml"))
        HC = H // KC
        NW = 16 * (3 + HC)
        with nc.Block() as block:
            @block.sync
            def _(sp):
                sp.dma_start(wqkv[:], chunked(A["L0_attn_W_qkv"])).then_inc(w_in, 16)
                sp.dma_start(wp[0:C], chunked(A["L0_attn_W_proj"])).then_inc(w_in, 16)
                sp.dma_start(wp[C:C + 1, KC - 1, :], row(A["L0_attn_b_proj"])).then_inc(w_in, 16)
                sp.wait_ge(z, 1)
                for h in range(HC):
                    sp.dma_start(feat[h * HD:(h + 1) * HD, h * M:(h + 1) * M], A["attn_proj_matT"]).then_inc(w_in, 16)
                sp.wait_ge(w_in, NW)

            @block.vector
            def _(dve):
                dve.memset(feat[:], 0.0).then_inc(z, 1)
                dve.memset(kmax[:], -3.0e38).then_inc(z, 1)
                for q in range(2):
                    dve.wait_ge(tr, q + 1)
                    dve.tensor_copy(wT[:, q, :, :], PS[0:C, q, 0:KC * D].rearrange("p (c n) -> p c n", c=KC)).then_inc(cp, 1)
                for q in range(2):
                    for c in range(KC):
                        dve.wait_ge(ml, q * KC + c + 1)
                        dve.tensor_scalar(wf[:, :, q, c, :], PS[0:C, 2 + 2 * c:4 + 2 * c, 0:HM], 0.5, None, ALU.mult) \
                           .then_inc(cp, 1)

            @block.tensor
            def _(pe):
                pe.wait_ge(w_in, NW)
                for q in range(2):
                    for c in range(KC):
                        for ci in range(KC):
                            ins = pe.transpose(PS[0:C, q, c * D + ci * C:c * D + (ci + 1) * C],
                                               wqkv[:, ci, q * D + c * C:q * D + (c + 1) * C], ident[0:C, 0:C])
                    ins.then_inc(tr, 1)
                for q in range(2):
                    pe.wait_ge(cp, q + 1)
                    if q:
                        pe.wait_ge(cp, 2 + KC)
                    for c in range(KC):
                        for ci in range(KC):
                            ins = pe.matmul(PS[0:C, 2 + 2 * c + ci, 0:HM], wT[:, q, c, ci * C:(ci + 1) * C], feat[:],
                                            start=True, stop=True)
                        ins.then_inc(ml, 1)

    with ExitStack() as ctx:
        nm = Norm(k, ctx, "pm_")
        begun = nc.alloc_semaphore("pm_begun")
        prod = Signal(nc, "pm_prod", T)
        reduced = Signal(nc, "pm_reduced", T, primed=True)
        with nc.Block() as block:
            @block.vector
            def _(dve):
                reduced.prime(dve)
                with dve.Fori(0, B) as b:
                    nm.dve(dve, b)
                    for t in range(T):
                        p = 3 + 2 * (t % 2)
                        dve.wait_ge(prod.sem, prod.now(b, t + 1))
                        dve.tensor_reduce(kmax[0:rows(t), bass.ds(b * T + t, 1)],
                                          PS[0:rows(t), p:p + 2, 0:HM], AX.XY, ALU.max).then_inc(reduced.sem, 1)

            @block.gpsimd
            def _(pool):
                with pool.Fori(0, B) as b:
                    nm.pool(pool, b)

            @block.scalar
            def _(act):
                with act.Fori(0, B) as b:
                    act.wait_ge(reduced.sem, reduced.before(b, T))
                    nm.act(act, b)

            @block.tensor
            def _(pe):
                nm.turned.prime(pe)
                with pe.Fori(0, B) as b:
                    pe.wait_ge(reduced.sem, reduced.before(b, T))
                    nm.pe(pe, b)
                    pe.wait_ge(nm.xT_ready.sem, nm.xT_ready.now(b, 3))
                    for t in range(T):
                        p = 3 + 2 * (t % 2)
                        pe.wait_ge(reduced.sem, reduced.now(b, t - 1) if t >= 2 else reduced.before(b, T - 1 + t))
                        for c in range(KC):
                            for ci in range(KC):
                                ins = pe.matmul(PS[0:rows(t), p + c, 0:HM], nm.xT[0:C, ci, t * R:t * R + rows(t)],
                                                wf[:, ci, 1, c, :], start=ci == 0, stop=ci == KC - 1)
                        ins.then_inc(prod.sem, 1)

    with nc.Block() as block:
        r, g = nc.alloc_semaphore("pf_r"), nc.alloc_semaphore("pf_g")

        @block.vector
        def _(dve):
            dve.tensor_reduce(mx[:, 0:1], kmax[:], AX.X, ALU.max).then_inc(r, 1)
            dve.wait_ge(g, 1)
            dve.tensor_scalar(nstab[:], mx[:, 1:2], -1.0, None, ALU.mult).then_inc(r, 1)

        @block.gpsimd
        def _(pool):
            pool.wait_ge(r, 1)
            pool.partition_all_reduce(mx[:, 1:2], mx[:, 0:1], 128, bass.bass_isa.ReduceOp.max).then_inc(g, 1)

    RATIO, EPS, HC = M ** -0.5, 1e-4, H // KC
    with ExitStack() as ctx:
        def sb(name, shape):
            return ctx.enter_context(nc.sbuf_tensor("pf_" + name, shape, F32))

        nm = Norm(k, ctx, "pf_")
        sq = sb("sq", [R, 2, D])
        diag = sb("diag", [R, 2, H])
        mq = sb("mq", [R, H])
        e = sb("e", [R, 2, KC, HM])
        f = sb("f", [R, 2, KC, HM])
        v1 = sb("v1", [R, 2, KC, C + 1])
        kvS = sb("kvS", [C + 1, KC, HM])
        kv = sb("kv", [2 * M, KC, HC // 2, 2, HD + 1])
        own = sb("own", [2 * M, 2])
        fT = sb("fT", [2 * M, H // 2, R])
        z = sb("z", [R, H])
        o = sb("o", [R, D])
        oT = sb("oT", [C + 1, KC, R])

        ready = nc.alloc_semaphore("pf_ready")
        dvk = Signal(nc, "pf_dvk", T)
        dvq = Signal(nc, "pf_dvq", 3 * T)
        kprod = Signal(nc, "pf_kprod", T)
        ksq = Signal(nc, "pf_ksq", T)
        kexp_in = Signal(nc, "pf_kexp_in", T, primed=True)
        kexp = Signal(nc, "pf_kexp", T)
        kf = Signal(nc, "pf_kf", T)
        kvacc = Signal(nc, "pf_kvacc", T)
        kvcopy = Signal(nc, "pf_kvcopy", 1)
        kvturn = Signal(nc, "pf_kvturn", 1)
        kvmade = Signal(nc, "pf_kvmade", 1)
        qprod = Signal(nc, "pf_qprod", T)
        qsq = Signal(nc, "pf_qsq", T)
        qexp_in = Signal(nc, "pf_qexp_in", T)
        qexp = Signal(nc, "pf_qexp", T)
        qf = Signal(nc, "pf_qf", T)
        qturn = Signal(nc, "pf_qturn", T)
        qTc = Signal(nc, "pf_qTc", T)
        num = Signal(nc, "pf_num", T)
        o_ready = Signal(nc, "pf_o", T)
        oturn = Signal(nc, "pf_oturn", T)
        oTc = Signal(nc, "pf_oTc", T)
        yprod = Signal(nc, "pf_y", T)
        added = Signal(nc, "pf_added", T, primed=True)

        def by_head(a):
            return a.rearrange("p c (h m) -> p c h m", m=M)

        with nc.Block() as block:
            @block.gpsimd
            def _(pool):
                pool.memset(own[:], 1.0).then_inc(ready, 1)
                pool.wait_ge(ready, 1)
                pool.memset(v1[:, :, :, C:C + 1], 1.0).then_inc(ready, 1)
                pool.wait_ge(ready, 2)
                pool.memset(oT[C:C + 1, :, :], 1.0).then_inc(ready, 1)
                pool.wait_ge(ready, 3)
                pool.affine_select(out=own[:, 0:1], in_=own[:, 0:1], compare_op=ALU.is_gt, fill=0.0, base=M,
                                   pattern=[[0, 1]], channel_multiplier=-1).then_inc(ready, 1)
                pool.affine_select(out=own[:, 1:2], in_=own[:, 1:2], compare_op=ALU.is_ge, fill=0.0, base=-M,
                                   pattern=[[0, 1]], channel_multiplier=1).then_inc(ready, 1)
                with pool.Fori(0, B) as b:
                    nm.pool(pool, b)
                    for t in range(T):
                        p = t % 2
                        pool.wait_ge(kexp.sem, kexp.now(b, t + 1))
                        if t >= 2:
                            pool.wait_ge(kvacc.sem, kvacc.now(b, t - 1))
                        stand(k, pool)
                        pool.tensor_scalar(f[:, p], e[:, p], EPS, RATIO, ALU.add, ALU.mult).then_inc(kf.sem, 1)
                    for t in range(T):
                        p = t % 2
                        pool.wait_ge(qexp.sem, qexp.now(b, t + 1))
                        if t >= 2:
                            pool.wait_ge(qturn.sem, qturn.now(b, t - 1))
                        else:
                            pool.wait_ge(kvacc.sem, kvacc.now(b, T))
                        stand(k, pool)
                        pool.tensor_scalar(f[:, p], e[:, p], EPS, RATIO, ALU.add, ALU.mult).then_inc(qf.sem, 1)

            @block.vector
            def _(dve):
                kexp_in.prime(dve)
                added.prime(dve)
                dve.wait_ge(ready, 5)
                with dve.Fori(0, B) as b:
                    nm.dve(dve, b)
                    step = Chain(dve, dvk, b)
                    for t in range(T):
                        p = t % 2
                        dve.wait_ge(ksq.sem, ksq.now(b, t + 1))
                        step(dve.tensor_reduce(diag[:, p, :], sq[:, p, :].rearrange("p (h d) -> p h d", d=HD), AX.X, ALU.add))
                        if t >= 2:
                            dve.wait_ge(kf.sem, kf.now(b, t - 1))
                        dve.tensor_tensor(by_head(e[:, p]), by_head(PS[0:R, 3 * p:3 * p + 2, 0:HM]),
                                          diag[:, p, :].rearrange("p (c h) -> p c h", c=KC).unsqueeze(3)
                                          .broadcast_to([R, KC, HC, M]), ALU.subtract).then_inc(kexp_in.sem, 1)
                    step.end()
                    dve.wait_ge(kvturn.sem, kvturn.now(b, 1))
                    for j in range(HC // 2):
                        dve.tensor_tensor(kv[:, :, j, :, 0:HD],
                                          PS[0:2 * M, 3:5, j * (C + 1) + 2 * j * HD:j * (C + 1) + 2 * (j + 1) * HD]
                                          .rearrange("p c (a d) -> p c a d", d=HD),
                                          own[:].unsqueeze(1).unsqueeze(3).broadcast_to([2 * M, KC, 2, HD]), ALU.mult)
                    for j in range(HC // 2):
                        at = j * (C + 1) + C
                        ins = dve.tensor_tensor(kv[:, :, j, :, HD:HD + 1],
                                                PS[0:2 * M, 3:5, at:at + 1].unsqueeze(2).broadcast_to([2 * M, KC, 2, 1]),
                                                own[:].unsqueeze(1).unsqueeze(3).broadcast_to([2 * M, KC, 2, 1]), ALU.mult)
                    ins.then_inc(kvmade.sem, 1)
                    step = Chain(dve, dvq, b)
                    for t in range(T):
                        p = t % 2
                        dve.wait_ge(qprod.sem, qprod.now(b, t + 1))
                        dve.tensor_reduce(mq[:], by_head(PS[0:R, 0:2, 0:HM]), AX.X, ALU.max)
                        dve.wait_ge(qsq.sem, qsq.now(b, t + 1))
                        step(dve.tensor_reduce(diag[:, p, :], sq[:, p, :].rearrange("p (h d) -> p h d", d=HD), AX.X, ALU.add))
                        step(dve.tensor_tensor(diag[:, p, :], diag[:, p, :], mq[:], ALU.add))
                        if t >= 2:
                            dve.wait_ge(qf.sem, qf.now(b, t - 1))
                        else:
                            dve.wait_ge(kf.sem, kf.now(b, T))
                        dve.tensor_tensor(by_head(e[:, p]), by_head(PS[0:R, 0:2, 0:HM]),
                                          diag[:, p, :].rearrange("p (c h) -> p c h", c=KC).unsqueeze(3)
                                          .broadcast_to([R, KC, HC, M]), ALU.subtract).then_inc(qexp_in.sem, 1)
                        dve.wait_ge(num.sem, num.now(b, t + 1))
                        on = PS[0:R, 5, 0:H * (HD + 1)].rearrange("p (h d) -> p h d", d=HD + 1)
                        step(dve.reciprocal(z[:], on[:, :, HD]))
                        dve.tensor_tensor(o[:].rearrange("p (h d) -> p h d", d=HD), on[:, :, 0:HD],
                                          z[:].unsqueeze(2).broadcast_to([R, H, HD]), ALU.mult).then_inc(o_ready.sem, 1)
                        dve.wait_ge(yprod.sem, yprod.now(b, t + 1))
                        dve.tensor_tensor(X[:, b * T + t, :], PS[0:R, 7, 0:D], X[:, b * T + t, :], ALU.add) \
                           .then_inc(added.sem, 1)
                    step.end()

            @block.scalar
            def _(act):
                HALF = 0.125 ** 0.5
                with act.Fori(0, B) as b:
                    act.wait_ge(added.sem, added.before(b, T))
                    nm.act(act, b)
                    for t in range(T):
                        p = t % 2
                        act.wait_ge(kprod.sem, kprod.now(b, t + 1))
                        if t >= 2:
                            act.wait_ge(kexp_in.sem, kexp_in.now(b, t - 1))
                            act.wait_ge(kvacc.sem, kvacc.now(b, t - 1))
                        act.activation(v1[:, p, :, 0:C], PS[0:R, 3 * p + 2, D:2 * D].rearrange("p (c d) -> p c d", c=KC), ACT.Copy)
                        act.activation(sq[:, p, :], PS[0:R, 3 * p + 2, 0:D], ACT.Square, scale=HALF).then_inc(ksq.sem, 1)
                        act.wait_ge(kexp_in.sem, kexp_in.now(b, t + 1))
                        act.activation(e[:, p], e[:, p], ACT.Exp, bias=nstab[0:R, :]).then_inc(kexp.sem, 1)
                    act.wait_ge(kvacc.sem, kvacc.now(b, T))
                    act.activation(kvS[:], PS[0:C + 1, 6:8, 0:HM], ACT.Copy).then_inc(kvcopy.sem, 1)
                    for t in range(T):
                        p = t % 2
                        act.wait_ge(qprod.sem, qprod.now(b, t + 1))
                        if t >= 2:
                            act.wait_ge(qexp_in.sem, qexp_in.now(b, t - 1))
                        act.activation(sq[:, p, :], PS[0:R, 2, 0:D], ACT.Square, scale=HALF).then_inc(qsq.sem, 1)
                        act.wait_ge(qexp_in.sem, qexp_in.now(b, t + 1))
                        act.activation(e[:, p], e[:, p], ACT.Exp).then_inc(qexp.sem, 1)
                        act.wait_ge(qturn.sem, qturn.now(b, t + 1))
                        act.activation(fT[:].rearrange("p (c j) n -> p c j n", c=KC),
                                       PS[0:2 * M, 3:5, 0:HC // 2 * R].rearrange("p c (j n) -> p c j n", n=R), ACT.Copy) \
                           .then_inc(qTc.sem, 1)
                        act.wait_ge(oturn.sem, oturn.now(b, t + 1))
                        act.activation(oT[0:C], PS[0:C, 6, 0:KC * R].rearrange("p (c n) -> p c n", c=KC), ACT.Copy) \
                           .then_inc(oTc.sem, 1)

            @block.tensor
            def _(pe):
                nm.turned.prime(pe)
                pe.wait_ge(ready, 5)
                xT = nm.xT
                with pe.Fori(0, B) as b:
                    pe.wait_ge(added.sem, added.before(b, T))
                    nm.pe(pe, b)
                    pe.wait_ge(nm.xT_ready.sem, nm.xT_ready.now(b, 3))

                    def k_products(t):
                        p = 3 * (t % 2)
                        if t >= 2:
                            pe.wait_ge(kexp_in.sem, kexp_in.now(b, t - 1))
                        a = slice(t * R, t * R + R)
                        for ci in range(KC):
                            pe.matmul(PS[0:R, p + 2, 0:2 * D], xT[0:C, ci, a], wqkv[:, ci, D:3 * D],
                                      start=ci == 0, stop=ci == KC - 1)
                        for c in range(KC):
                            for ci in range(KC):
                                ins = pe.matmul(PS[0:R, p + c, 0:HM], xT[0:C, ci, a], wf[:, ci, 1, c, :],
                                                start=ci == 0, stop=ci == KC - 1)
                        ins.then_inc(kprod.sem, 1)

                    k_products(0)
                    for t in range(T):
                        if t + 1 < T:
                            k_products(t + 1)
                        pe.wait_ge(kf.sem, kf.now(b, t + 1))
                        for c in range(KC):
                            ins = pe.matmul(PS[0:C + 1, 6 + c, 0:HM], v1[0:rows(t), t % 2, c, :], f[0:rows(t), t % 2, c, :],
                                            start=t == 0, stop=t == T - 1)
                        ins.then_inc(kvacc.sem, 1)
                    pe.wait_ge(kvcopy.sem, kvcopy.now(b, 1))
                    for c in range(KC):
                        for j in range(HC // 2):
                            ins = pe.transpose(PS[0:2 * M, 3 + c, j * (C + 1):(j + 1) * (C + 1)],
                                               kvS[:, c, j * 2 * M:(j + 1) * 2 * M], ident[0:C + 1, 0:C + 1])
                    ins.then_inc(kvturn.sem, 1)
                    pe.wait_ge(kvmade.sem, kvmade.now(b, 1))
                    for t in range(T):
                        a = slice(t * R, t * R + R)
                        if t:
                            pe.wait_ge(qexp_in.sem, qexp_in.now(b, t))
                        for ci in range(KC):
                            pe.matmul(PS[0:R, 2, 0:D], xT[0:C, ci, a], wqkv[:, ci, 0:D], start=ci == 0, stop=ci == KC - 1)
                        for c in range(KC):
                            for ci in range(KC):
                                ins = pe.matmul(PS[0:R, c, 0:HM], xT[0:C, ci, a], wf[:, ci, 0, c, :],
                                                start=ci == 0, stop=ci == KC - 1)
                        ins.then_inc(qprod.sem, 1)
                        pe.wait_ge(qf.sem, qf.now(b, t + 1))
                        for c in range(KC):
                            for j in range(HC // 2):
                                ins = pe.transpose(PS[0:2 * M, 3 + c, j * R:(j + 1) * R],
                                                   f[:, t % 2, c, j * 2 * M:(j + 1) * 2 * M], ident[0:R, 0:R])
                        ins.then_inc(qturn.sem, 1)
                        pe.wait_ge(qTc.sem, qTc.now(b, t + 1))
                        for j in range(H // 2):
                            ins = pe.matmul(PS[0:R, 5, j * 2 * (HD + 1):(j + 1) * 2 * (HD + 1)], fT[:, j, :],
                                            kv[:, j // (HC // 2), j % (HC // 2), :, :], start=True, stop=True)
                        ins.then_inc(num.sem, 1)
                        pe.wait_ge(o_ready.sem, o_ready.now(b, t + 1))
                        for c in range(KC):
                            ins = pe.transpose(PS[0:C, 6, c * R:(c + 1) * R], o[:, c * C:(c + 1) * C], ident[0:R, 0:R])
                        ins.then_inc(oturn.sem, 1)
                        pe.wait_ge(oTc.sem, oTc.now(b, t + 1))
                        for c in range(KC):
                            ins = pe.matmul(PS[0:R, 7, 0:D], oT[0:kin(c), c, :], wp[0:kin(c), c, :],
                                            start=c == 0, stop=c == KC - 1)
                        ins.then_inc(yprod.sem, 1)
    outer.close()


def gated_attention(k, A):
    nc, X, PS, ident = k.nc, k.X, k.PS, k.ident
    SCALE = HD0 ** -0.5
    NU = T * E0
    HALF = NP // 2
    with ExitStack() as ctx:
        def sb(name, shape):
            return ctx.enter_context(nc.sbuf_tensor("ga_" + name, shape, F32))

        wqk = sb("wqk", [C + 1, KC, 2 * D])
        wv = sb("wv", [C + 1, KC, D])
        wg1 = sb("wg1", [C + 1, KC, HID])
        wg2 = sb("wg2", [HID + 1, E0])
        wp = sb("wp", [C + 1, KC, D])
        cw = sb("cw", [HD0, 3])
        cb = sb("cb", [HD0, 1])
        w_in = nc.alloc_semaphore("ga_w_in")
        NW = 16 * (4 * 2 + 2 * E0 + 2 + 2 + 2 + 2)
        GROUPS = [(0, 128, 0), (D, 128, 128), (128, 64, 256), (D + 128, 64, 320)]

        def load(sp):
            for src, n, dst in GROUPS:
                sp.dma_start(wqk[0:C, :, dst:dst + n], chunked(A["L0_ffn_Wqk"])[:, :, src:src + n]).then_inc(w_in, 16)
                sp.dma_start(wqk[C:C + 1, KC - 1, dst:dst + n], row(A["L0_ffn_bqk"])[:, src:src + n]).then_inc(w_in, 16)
            for e in range(E0):
                sp.dma_start(wv[0:C, :, e * HD0:(e + 1) * HD0], chunked(A["L0_ffn_Wv"][e])).then_inc(w_in, 16)
                sp.dma_start(wv[C:C + 1, KC - 1, e * HD0:(e + 1) * HD0], row(A["L0_ffn_bv"][e])).then_inc(w_in, 16)
            sp.dma_start(wg1[0:C], chunked(A["L0_ffn_Wg1"])).then_inc(w_in, 16)
            sp.dma_start(wg1[C:C + 1, KC - 1, :], row(A["L0_ffn_bg1"])).then_inc(w_in, 16)
            sp.dma_start(wg2[0:HID], A["L0_ffn_Wg2"]).then_inc(w_in, 16)
            sp.dma_start(wg2[HID:HID + 1], row(A["L0_ffn_bg2"])).then_inc(w_in, 16)
            sp.dma_start(wp[0:C], chunked(A["L0_ffn_Wp"])).then_inc(w_in, 16)
            sp.dma_start(wp[C:C + 1, KC - 1, :], row(A["L0_ffn_bp"])).then_inc(w_in, 16)
            sp.dma_start(cw[:], A["L0_ffn_conv_w"].rearrange("d a w -> d (a w)")).then_inc(w_in, 16)
            sp.dma_start(cb[:], A["L0_ffn_conv_b"].rearrange("(d a) -> d a", a=1)).then_inc(w_in, 16)
            sp.wait_ge(w_in, NW)

        nm = Norm(k, ctx, "ga_")
        g1 = sb("g1", [HID + 1, NP])
        gm = sb("gm", [R, T])
        gs = sb("gs", [R, T])
        g = sb("g", [R, T, E0])
        e3 = sb("e3", [R, T, E0])
        kept = sb("kept", [R, T, E0])
        m01 = sb("m01", [R, T])
        w = sb("w", [R, T, E0])
        q01 = sb("q01", [128, NP + 2])
        qc = sb("qc", [HD0, NP])
        k01 = sb("k01", [128, NP])
        q2 = sb("q2", [HD0, NP])
        k2 = sb("k2", [HD0, NP])
        v = sb("v", [R, T, D])
        nmx = sb("nmx", [R, NU])
        rs = sb("rs", [R, NU])
        rw = sb("rw", [R, NU])
        P = sb("P", [R, 2, N])
        PT = sb("PT", [R, 2, T, R])
        comb = sb("comb", [R, 2, D])
        cT = sb("cT", [C + 1, KC, R])

        ready = nc.alloc_semaphore("ga_ready")
        dvg = Signal(nc, "ga_dvg", 15)
        dvc = Signal(nc, "ga_dvc", 2)
        dvu = Signal(nc, "ga_dvu", 2 * NU)
        hidden = Signal(nc, "ga_hidden", 1)
        relued = Signal(nc, "ga_relued", 1)
        logits = Signal(nc, "ga_logits", 1)
        gexp_in = Signal(nc, "ga_gexp_in", 2)
        gexp = Signal(nc, "ga_gexp", 2)
        qkprod = Signal(nc, "ga_qkprod", 4)
        qkcopy = Signal(nc, "ga_qkcopy", 5)
        conv = Signal(nc, "ga_conv", 1)
        vprod = Signal(nc, "ga_vprod", 2)
        vcopy = Signal(nc, "ga_vcopy", 2)
        score = Signal(nc, "ga_score", NU)
        bias = Signal(nc, "ga_bias", NU)
        prob = Signal(nc, "ga_prob", NU)
        weight = Signal(nc, "ga_weight", NU)
        turned = Signal(nc, "ga_pturned", NU)
        ptcopy = Signal(nc, "ga_ptcopy", NU)
        pv = Signal(nc, "ga_pv", NU)
        combined = Signal(nc, "ga_combined", NU)
        cturn = Signal(nc, "ga_cturn", T)
        ccopy = Signal(nc, "ga_ccopy", T)
        yprod = Signal(nc, "ga_y", T)
        added = Signal(nc, "ga_added", T, primed=True)

        def keys(u):
            return min((u // E0 + 1) * R, N)

        def scores(u):
            b0 = 2 * (u % 2)
            return PS[0:R, b0:b0 + 2, :].rearrange("p a n -> p (a n)")[:, 0:keys(u)]

        def last_of_tile(u):
            return 0 <= u < NU and u % E0 == E0 - 1

        with nc.Block() as block:
            @block.sync
            def _(sp):
                load(sp)

            @block.gpsimd
            def _(pool):
                pool.memset(g1[HID:HID + 1, :], 1.0).then_inc(ready, 1)
                pool.wait_ge(ready, 1)
                pool.memset(q01[:], 0.0).then_inc(ready, 1)
                pool.memset(qc[:], 0.0).then_inc(ready, 1)
                pool.wait_ge(ready, 3)
                pool.memset(cT[C:C + 1, :, :], 1.0).then_inc(ready, 1)
                pool.wait_ge(ready, 4)
                pool.memset(nm.xT[C:C + 1, :, :], 1.0).then_inc(ready, 1)
                with pool.Fori(0, B) as b:
                    nm.pool(pool, b)

            @block.vector
            def _(dve):
                added.prime(dve)
                dve.wait_ge(ready, 5)
                dve.wait_ge(w_in, NW)
                with dve.Fori(0, B) as b:
                    nm.dve(dve, b)
                    step = Chain(dve, dvc, b)
                    dve.wait_ge(qkprod.sem, qkprod.now(b, 1))
                    dve.tensor_copy(q01[:, 1:1 + HALF], PS[:, 6, 0:HALF]).then_inc(qkcopy.sem, 1)
                    dve.tensor_copy(q01[:, 1 + HALF:1 + N], PS[:, 7, 0:N - HALF]).then_inc(qkcopy.sem, 1)
                    dve.wait_ge(qkprod.sem, qkprod.now(b, 2))
                    dve.tensor_copy(k01[:].rearrange("p (a n) -> p a n", a=2), PS[:, 3:5, 0:HALF]).then_inc(qkcopy.sem, 1)
                    dve.wait_ge(qkcopy.sem, qkcopy.now(b, 2))
                    step(dve.tensor_scalar(qc[:, 0:N], q01[0:HD0, 1:N + 1], cw[:, 1:2], cb[:, 0:1], ALU.mult, ALU.add))
                    step(dve.scalar_tensor_tensor(qc[:, 0:N], q01[0:HD0, 0:N], cw[:, 0:1], qc[:, 0:N], ALU.mult, ALU.add))
                    dve.scalar_tensor_tensor(qc[:, 0:N], q01[0:HD0, 2:N + 2], cw[:, 2:3], qc[:, 0:N],
                                             ALU.mult, ALU.add).then_inc(conv.sem, 1)
                    step.end()
                    dve.wait_ge(qkprod.sem, qkprod.now(b, 3))
                    dve.tensor_copy(q2[:].rearrange("p (a n) -> p a n", a=2), PS[0:HD0, 6:8, 0:HALF]).then_inc(qkcopy.sem, 1)
                    dve.wait_ge(qkprod.sem, qkprod.now(b, 4))
                    dve.tensor_copy(k2[:].rearrange("p (a n) -> p a n", a=2), PS[0:HD0, 3:5, 0:HALF]).then_inc(qkcopy.sem, 1)
                    step = Chain(dve, dvg, b)

                    def wide(a):
                        return a[:].unsqueeze(2).broadcast_to([R, T, E0])

                    dve.wait_ge(logits.sem, logits.now(b, 1))
                    lg = PS[0:R, 5, 0:T * E0].rearrange("p (t e) -> p t e", e=E0)
                    step(dve.tensor_reduce(gm[:], lg, AX.X, ALU.max))
                    dve.tensor_tensor(e3[:], lg, wide(gm), ALU.subtract).then_inc(gexp_in.sem, 1)
                    dve.wait_ge(gexp.sem, gexp.now(b, 1))
                    step(dve.tensor_reduce(gs[:], e3[:], AX.X, ALU.add))
                    step(dve.reciprocal(gs[:], gs[:]))
                    step(dve.tensor_tensor(g[:], e3[:], wide(gs), ALU.mult))
                    dve.tensor_tensor(m01[:], g[:, :, 0], g[:, :, 1], ALU.min)
                    dve.tensor_tensor(kept[:, :, 1], g[:, :, 1], g[:, :, 0], ALU.is_gt)
                    step(dve.tensor_reduce(gm[:], g[:], AX.X, ALU.max))
                    step(dve.tensor_tensor(kept[:, :, 2], g[:, :, 2], m01[:], ALU.is_gt))
                    dve.tensor_tensor(e3[:], g[:], wide(gm), ALU.subtract).then_inc(gexp_in.sem, 1)
                    step(dve.tensor_scalar(m01[:], kept[:, :, 2], -1.0, 1.0, ALU.mult, ALU.add))
                    step(dve.tensor_tensor(kept[:, :, 1], kept[:, :, 1], m01[:], ALU.max))
                    step(dve.tensor_tensor(m01[:], kept[:, :, 1], kept[:, :, 2], ALU.add))
                    step(dve.tensor_scalar(kept[:, :, 0], m01[:], -1.0, 2.0, ALU.mult, ALU.add))
                    dve.wait_ge(gexp.sem, gexp.now(b, 2))
                    step(dve.tensor_tensor(e3[:], e3[:], kept[:], ALU.mult))
                    step(dve.tensor_reduce(gs[:], e3[:], AX.X, ALU.add))
                    step(dve.reciprocal(gs[:], gs[:]))
                    step(dve.tensor_tensor(w[:], e3[:], wide(gs), ALU.mult))
                    step(dve.tensor_scalar(nmx[:, 0:1], w[:, 0, 0:1], 0.0, None, ALU.mult))
                    step.end()
                    step = Chain(dve, dvu, b)
                    for i in range(NU + 5):
                        if i < NU:
                            dve.wait_ge(score.sem, score.now(b, i + 1))
                            step(dve.tensor_reduce(nmx[:, i:i + 1], scores(i), AX.X, ALU.max, negate=True))
                            dve.tensor_scalar(nmx[:, i:i + 1], nmx[:, i:i + 1], SCALE, None, ALU.mult).then_inc(bias.sem, 1)
                        u = i - 1
                        if 0 <= u < NU:
                            dve.wait_ge(prob.sem, prob.now(b, u + 1))
                            step(dve.reciprocal(rw[:, u:u + 1], rs[:, u:u + 1]))
                            dve.tensor_tensor(rw[:, u:u + 1], rw[:, u:u + 1], w[:, u // E0, u % E0:u % E0 + 1], ALU.mult) \
                               .then_inc(weight.sem, 1)
                        u = i - 2
                        if 0 <= u < NU:
                            dve.wait_ge(pv.sem, pv.now(b, u + 1))
                            dve.wait_ge(weight.sem, weight.now(b, u + 1))
                            e = u % E0
                            dve.tensor_scalar(comb[:, u // E0 % 2, e * HD0:(e + 1) * HD0], PS[0:R, 6, 0:HD0],
                                              rw[:, u:u + 1], None, ALU.mult).then_inc(combined.sem, 1)
                        if last_of_tile(i - 4):
                            t = (i - 4) // E0
                            dve.wait_ge(yprod.sem, yprod.now(b, t + 1))
                            dve.tensor_tensor(X[:, b * T + t, :], PS[0:R, 7, 256:256 + D], X[:, b * T + t, :], ALU.add) \
                               .then_inc(added.sem, 1)
                    step.end()

            @block.scalar
            def _(act):
                with act.Fori(0, B) as b:
                    act.wait_ge(added.sem, added.before(b, T))
                    nm.act(act, b)
                    act.wait_ge(hidden.sem, hidden.now(b, 1))
                    act.activation(g1[0:HID, :].rearrange("p (a n) -> p a n", a=2), PS[0:HID, 3:5, 0:HALF], ACT.Relu) \
                       .then_inc(relued.sem, 1)
                    act.wait_ge(vprod.sem, vprod.now(b, 1))
                    act.activation(v[:, 0:4, :].rearrange("p (a t) d -> p a (t d)", a=2), PS[0:R, 0:2, 0:2 * D], ACT.Copy) \
                       .then_inc(vcopy.sem, 1)
                    act.wait_ge(vprod.sem, vprod.now(b, 2))
                    act.activation(v[:, 4, :], PS[0:R, 2, 0:D], ACT.Copy).then_inc(vcopy.sem, 1)
                    for i in range(2):
                        act.wait_ge(gexp_in.sem, gexp_in.now(b, i + 1))
                        act.activation(e3[:], e3[:], ACT.Exp).then_inc(gexp.sem, 1)
                    for i in range(NU + 4):
                        if i < NU:
                            act.wait_ge(bias.sem, bias.now(b, i + 1))
                            if i >= 2:
                                act.wait_ge(turned.sem, turned.now(b, i - 1))
                            act.activation(P[:, i % 2, 0:keys(i)], scores(i), ACT.Exp, bias=nmx[:, i:i + 1], scale=SCALE,
                                           accum_out=rs[:, i:i + 1]).then_inc(prob.sem, 1)
                        u = i - 1
                        if 0 <= u < NU:
                            act.wait_ge(turned.sem, turned.now(b, u + 1))
                            if u >= 2:
                                act.wait_ge(pv.sem, pv.now(b, u - 1))
                            n = min(u // E0 + 1, 4)
                            ins = act.activation(PT[:, u % 2, 0:n, :], PS[0:R, 4, 0:n * R].rearrange("p (t n) -> p t n", n=R),
                                                 ACT.Copy)
                            if u // E0 == T - 1:
                                ins = act.activation(PT[0:LAST, u % 2, T - 1, :], PS[0:LAST, 5, 0:R], ACT.Copy)
                            ins.then_inc(ptcopy.sem, 1)
                        if last_of_tile(i - 3):
                            t = (i - 3) // E0
                            act.wait_ge(cturn.sem, cturn.now(b, t + 1))
                            act.activation(cT[0:C], PS[0:C, 7, 0:KC * R].rearrange("p (c n) -> p c n", c=KC), ACT.Copy) \
                               .then_inc(ccopy.sem, 1)

            @block.tensor
            def _(pe):
                nm.turned.prime(pe)
                pe.wait_ge(ready, 5)
                pe.wait_ge(w_in, NW)
                xT = nm.xT
                with pe.Fori(0, B) as b:
                    pe.wait_ge(added.sem, added.before(b, T))
                    nm.pe(pe, b)
                    pe.wait_ge(nm.xT_ready.sem, nm.xT_ready.now(b, 3))

                    def halves(bank, rows_out, weights):
                        for a in range(2):
                            for c in range(KC):
                                ins = pe.matmul(PS[0:rows_out, bank + a, 0:HALF], weights(c),
                                                xT[0:kin(c), c, a * HALF:(a + 1) * HALF], start=c == 0, stop=c == KC - 1)
                        return ins

                    halves(3, HID, lambda c: wg1[0:kin(c), c, :]).then_inc(hidden.sem, 1)
                    halves(6, 128, lambda c: wqk[0:kin(c), c, 0:128]).then_inc(qkprod.sem, 1)
                    pe.wait_ge(relued.sem, relued.now(b, 1))
                    halves(3, 128, lambda c: wqk[0:kin(c), c, 128:256]).then_inc(qkprod.sem, 1)
                    for t in range(T):
                        ins = pe.matmul(PS[0:R, 5, t * E0:(t + 1) * E0], g1[:, t * R:(t + 1) * R], wg2[:], start=True, stop=True)
                    ins.then_inc(logits.sem, 1)
                    for t in range(T):
                        for c in range(KC):
                            ins = pe.matmul(PS[0:R, t // 2, t % 2 * D:(t % 2 + 1) * D], xT[0:kin(c), c, t * R:(t + 1) * R],
                                            wv[0:kin(c), c, :], start=c == 0, stop=c == KC - 1)
                        if t >= 3:
                            ins.then_inc(vprod.sem, 1)
                    pe.wait_ge(qkcopy.sem, qkcopy.now(b, 2))
                    halves(6, HD0, lambda c: wqk[0:kin(c), c, 256:320]).then_inc(qkprod.sem, 1)
                    pe.wait_ge(qkcopy.sem, qkcopy.now(b, 3))
                    halves(3, HD0, lambda c: wqk[0:kin(c), c, 320:384]).then_inc(qkprod.sem, 1)
                    pe.wait_ge(vcopy.sem, vcopy.now(b, 2))
                    pe.wait_ge(conv.sem, conv.now(b, 1))
                    pe.wait_ge(qkcopy.sem, qkcopy.now(b, 5))
                    for i in range(NU + 5):
                        if i < NU:
                            t, e, bank = i // E0, i % E0, 2 * (i % 2)
                            if i >= 2:
                                pe.wait_ge(prob.sem, prob.now(b, i - 1))
                            q = (qc[:, t * R:(t + 1) * R], q01[HD0:128, 1 + t * R:1 + (t + 1) * R], q2[:, t * R:(t + 1) * R])[e]
                            kk = (k01[0:HD0], k01[HD0:128], k2[:])[e]
                            nk, d0 = keys(i), t * R
                            pe.matmul(PS[0:R, bank, 0:min(nk, 512)], q, kk[:, 0:min(nk, 512)], start=True, stop=False)
                            if nk > 512:
                                pe.matmul(PS[0:R, bank + 1, 0:nk - 512], q, kk[:, 512:nk], start=True, stop=False)
                            m = min(nk, 512) - d0
                            ins = pe.matmul(PS[0:R, bank, d0:d0 + m], ident[0:R, 0:R], k.causal[:, 0:m], start=False, stop=True)
                            if nk > 512:
                                ins = pe.matmul(PS[0:R, bank + 1, 0:nk - 512], ident[0:R, 0:R], k.causal[:, m:m + nk - 512],
                                                start=False, stop=True)
                            ins.then_inc(score.sem, 1)
                        u = i - 2
                        if 0 <= u < NU:
                            t, e = u // E0, u % E0
                            pe.wait_ge(ptcopy.sem, ptcopy.now(b, u + 1))
                            if u >= 1:
                                pe.wait_ge(combined.sem, combined.now(b, u))
                            for kt in range(t + 1):
                                ins = pe.matmul(PS[0:R, 6, 0:HD0], PT[0:rows(kt), u % 2, kt, :],
                                                v[0:rows(kt), kt, e * HD0:(e + 1) * HD0], start=kt == 0, stop=kt == t)
                            ins.then_inc(pv.sem, 1)
                        u = i - 1
                        if 0 <= u < NU:
                            pe.wait_ge(prob.sem, prob.now(b, u + 1))
                            if u >= 1:
                                pe.wait_ge(ptcopy.sem, ptcopy.now(b, u))
                            for kt in range(u // E0 + 1):
                                n = rows(kt)
                                ins = pe.transpose(PS[0:n, 4 + kt // 4, kt % 4 * R:(kt % 4 + 1) * R],
                                                   P[:, u % 2, kt * R:kt * R + n], ident[0:R, 0:R])
                            ins.then_inc(turned.sem, 1)
                        if last_of_tile(i - 3):
                            t = (i - 3) // E0
                            pe.wait_ge(combined.sem, combined.now(b, i - 2))
                            if t >= 1:
                                pe.wait_ge(added.sem, added.now(b, t))
                            for c in range(KC):
                                ins = pe.transpose(PS[0:C, 7, c * R:(c + 1) * R], comb[:, t % 2, c * C:(c + 1) * C], ident[0:R, 0:R])
                            ins.then_inc(cturn.sem, 1)
                        if last_of_tile(i - 4):
                            t = (i - 4) // E0
                            pe.wait_ge(ccopy.sem, ccopy.now(b, t + 1))
                            for c in range(KC):
                                ins = pe.matmul(PS[0:R, 7, 256:256 + D], cT[0:kin(c), c, :], wp[0:kin(c), c, :],
                                                start=c == 0, stop=c == KC - 1)
                            ins.then_inc(yprod.sem, 1)


def talking_heads(k, A):
    nc, X, PS, ident = k.nc, k.X, k.PS, k.ident
    HALF, HK = NP // 2, N // 2
    HC = H // KC
    GQ = QT * QG
    outer = ExitStack()

    def keep(name, shape):
        return outer.enter_context(nc.sbuf_tensor("th_" + name, shape, F32))

    wT = [keep(n, [C + 1, KC, D]) for n in ("wq", "wk", "wv", "wo")]
    wq, wk, wv, wo = wT
    th1 = keep("th1", [C, KC, H])
    mix = keep("mix", [HQ + 1, H, QT])
    qg = keep("qg", [C + 1, 2, KC, H, QT])
    own = keep("own", [C, HC])

    with ExitStack() as ctx:
        b1 = ctx.enter_context(nc.sbuf_tensor("th_b1", [C + 1, H], F32))
        b2 = ctx.enter_context(nc.sbuf_tensor("th_b2", [1, 2, H * QT], F32))
        th2 = ctx.enter_context(nc.sbuf_tensor("th_th2", [HQ, H], F32))
        d3 = ctx.enter_context(nc.sbuf_tensor("th_d3", [HQ, H, QT], F32))
        d2 = ctx.enter_context(nc.sbuf_tensor("th_d2", [HQ, QT], F32))
        w_in, z, tr, cp = (nc.alloc_semaphore("th_" + n) for n in ("w_in", "z", "b2_in", "cp"))
        NW = 16 * (8 + KC * HC + H + 2)
        with nc.Block() as block:
            @block.sync
            def _(sp):
                for i, n in enumerate(("q", "k", "v", "o")):
                    sp.dma_start(wT[i][0:C], chunked(A[f"attn1_w{n}T"])).then_inc(w_in, 16)
                    sp.dma_start(wT[i][C:C + 1, KC - 1, :], row(A["L1_attn_b" + n])).then_inc(w_in, 16)
                for h in range(H):
                    hc, hh = h // HC, h % HC
                    sp.dma_start(th1[hh * HD:(hh + 1) * HD, hc, :], A["attn1_th1_wT"][h:h + 1].broadcast_to([HD, H])) \
                      .then_inc(w_in, 16)
                    sp.dma_start(th2[h * QT:(h + 1) * QT, :], A["attn1_th2_wT"][h:h + 1].broadcast_to([QT, H])).then_inc(w_in, 16)
                sp.dma_start(b1[C:C + 1, :], row(A["L1_attn_th1_b"])).then_inc(w_in, 16)
                sp.dma_start(b2[:, 1, 0:H], row(A["L1_attn_th2_b"])).then_inc(w_in, 16)
                sp.wait_ge(w_in, NW)
                sp.wait_ge(cp, 1)
                sp.dma_start(mix[HQ:HQ + 1, :, :].rearrange("p h n -> p (h n)"), b2[:, 0, :]).then_inc(tr, 16)
                sp.wait_ge(tr, 16)

            @block.gpsimd
            def _(pool):
                pool.memset(d3[:], 0.0).then_inc(z, 1)
                pool.memset(own[:], 1.0).then_inc(z, 1)
                pool.wait_ge(z, 2)
                pool.affine_select(out=d3[:], in_=d3[:], compare_op=ALU.not_equal, fill=1.0, base=0,
                                   pattern=[[-QT, H], [-1, QT]], channel_multiplier=1).then_inc(z, 1)
                pool.affine_select(out=own[:], in_=own[:], compare_op=ALU.is_ge, fill=0.0, base=0,
                                   pattern=[[-HD, HC]], channel_multiplier=1).then_inc(z, 1)
                pool.wait_ge(z, 4)
                pool.affine_select(out=own[:], in_=own[:], compare_op=ALU.is_gt, fill=0.0, base=HD,
                                   pattern=[[HD, HC]], channel_multiplier=-1).then_inc(z, 1)

            @block.vector
            def _(dve):
                dve.wait_ge(w_in, NW)
                dve.tensor_copy(b2[:, 0, :].rearrange("p (h n) -> p h n", n=QT),
                                b2[:, 1, 0:H].unsqueeze(2).broadcast_to([1, H, QT])).then_inc(cp, 1)
                for i in range(2):
                    dve.tensor_copy(qg[C:C + 1, i, KC - 1], b1[C:C + 1, :].unsqueeze(2).broadcast_to([1, H, QT]))
                dve.wait_ge(z, 5)
                dve.tensor_reduce(d2[:], d3[:].rearrange("p h n -> p n h"), AX.X, ALU.add).then_inc(cp, 1)
                dve.tensor_scalar(th1[:], th1[:], HD ** -0.5, None, ALU.mult).then_inc(cp, 1)
                dve.wait_ge(cp, 3)
                dve.tensor_tensor(mix[0:HQ], th2[:].unsqueeze(2).broadcast_to([HQ, H, QT]),
                                  d2[:].unsqueeze(1).broadcast_to([HQ, H, QT]), ALU.mult).then_inc(cp, 1)

    with ExitStack() as ctx:
        def sb(name, shape):
            return ctx.enter_context(nc.sbuf_tensor("th_" + name, shape, F32))

        nm = Norm(k, ctx, "th_")
        qT = sb("qT", [C, KC, NQ])
        kT = sb("kT", [C + 1, KC, NP])
        v = sb("v", [R, T, D])
        nmx = sb("nmx", [HQ, 2])
        rs = sb("rs", [128, 2])
        mixn = sb("mixn", [HQ + 1, 2, H, QT])
        P = sb("P", [HQ + 1, 2, N])
        P2 = sb("P2", [R, T, H, GQ])
        om = sb("om", [C, KC, HC, GQ])
        oT = sb("oT", [C + 1, KC, NQ])

        ready = nc.alloc_semaphore("th_ready")
        qprod = Signal(nc, "th_qprod", 2 * KC)
        qcopy = Signal(nc, "th_qcopy", 2 * KC)
        vprod = Signal(nc, "th_vprod", 2)
        vcopy = Signal(nc, "th_vcopy", 2)
        dvu = Signal(nc, "th_dvu", QG)
        qg_ready = Signal(nc, "th_qg", QG)
        score = Signal(nc, "th_score", QG, primed=True)
        bias = Signal(nc, "th_bias", QG)
        prob = Signal(nc, "th_prob", QG, primed=True)
        scaled = Signal(nc, "th_scaled", QG)
        mixed = Signal(nc, "th_mixed", QG, primed=True)
        p2copy = Signal(nc, "th_p2copy", QG, primed=True)
        pv = Signal(nc, "th_pv", KC, primed=True)
        masked = Signal(nc, "th_masked", KC, primed=True)
        summed = Signal(nc, "th_summed", KC)
        yprod = Signal(nc, "th_y", T)
        added = Signal(nc, "th_added", T, primed=True)

        with nc.Block() as block:
            @block.gpsimd
            def _(pool):
                for i, (a, x) in enumerate(((nm.xT[C:C + 1, :, :], 1.0), (kT[C:C + 1, :, :], 1.0), (oT[C:C + 1, :, :], 1.0),
                                            (P[C:HQ + 1, :, :], 1.0), (rs[:], 1.0), (qT[:, :, NP:NQ], 0.0))):
                    pool.memset(a, x).then_inc(ready, 1)
                    pool.wait_ge(ready, i + 1)
                with pool.Fori(0, B) as b:
                    nm.pool(pool, b)
                    pool.wait_ge(qcopy.sem, qcopy.now(b, 2 * KC))
                    stand(k, pool)
                    with pool.Fori(0, NG) as g:
                        tg = b * NG + g
                        for i in range(QG):
                            pool.wait_ge(score.sem, score.now(tg, i - 1) if i >= 2 else score.before(tg, QG - 1 + i))
                            for c in range(KC):
                                stand(k, pool)
                                ins = pool.tensor_tensor(qg[0:C, i % 2, c], qT[:, c, bass.ds(g * GQ + i * QT, QT)].unsqueeze(1)
                                                         .broadcast_to([C, H, QT]),
                                                         th1[:, c, :].unsqueeze(2).broadcast_to([C, H, QT]), ALU.mult)
                            ins.then_inc(qg_ready.sem, 1)

            @block.vector
            def _(dve):
                added.prime(dve)
                masked.prime(dve)
                dve.wait_ge(ready, 6)
                with dve.Fori(0, B) as b:
                    nm.dve(dve, b)
                    for i in range(2 * KC):
                        dst = (qT if i < KC else kT)[0:C, i % KC, 0:NP]
                        bank = 4 + 2 * (i % 2)
                        dve.wait_ge(qprod.sem, qprod.now(b, i + 1))
                        dve.tensor_copy(dst.rearrange("p (a n) -> p a n", a=2), PS[0:C, bank:bank + 2, 0:HALF]) \
                           .then_inc(qcopy.sem, 1)
                    with dve.Fori(0, NG) as g:
                        tg = b * NG + g
                        step = Chain(dve, dvu, tg)
                        for i in range(QG + 1):
                            if i < QG:
                                dve.wait_ge(score.sem, score.now(tg, i + 1))
                                dve.tensor_reduce(nmx[:, i % 2:i % 2 + 1], PS[0:HQ, 2 * (i % 2):2 * (i % 2) + 2, 0:HK], AX.XY,
                                                  ALU.max, negate=True).then_inc(bias.sem, 1)
                            u = i - 1
                            if 0 <= u:
                                p = u % 2
                                dve.wait_ge(prob.sem, prob.now(tg, u + 1))
                                dve.wait_ge(mixed.sem, mixed.now(tg, u - 1) if u >= 2 else mixed.before(tg, QG - 1 + u))
                                step(dve.reciprocal(rs[0:HQ, p:p + 1], rs[0:HQ, p:p + 1]))
                                dve.tensor_scalar(mixn[:, p], mix[:], rs[0:HQ + 1, p:p + 1], None, ALU.mult).then_inc(scaled.sem, 1)
                        step.end()
                        for c in range(KC):
                            dve.wait_ge(pv.sem, pv.now(tg, c + 1))
                            dve.tensor_tensor(om[:, c], PS[0:C, 6 + c, 0:HC * GQ].rearrange("p (h n) -> p h n", n=GQ),
                                              own[:].unsqueeze(2).broadcast_to([C, HC, GQ]), ALU.mult).then_inc(masked.sem, 1)
                            dve.wait_ge(masked.sem, masked.now(tg, c + 1))
                            stand(k, dve)
                            dve.tensor_reduce(oT[0:C, c, bass.ds(g * GQ, GQ)], om[:, c].rearrange("p h n -> p n h"), AX.X,
                                              ALU.add).then_inc(summed.sem, 1)
                    for t in range(T):
                        dve.wait_ge(yprod.sem, yprod.now(b, t + 1))
                        dve.tensor_tensor(X[:, b * T + t, :], PS[0:R, t, 0:D], X[:, b * T + t, :], ALU.add) \
                           .then_inc(added.sem, 1)

            @block.scalar
            def _(act):
                prob.prime(act)
                p2copy.prime(act)
                with act.Fori(0, B) as b:
                    act.wait_ge(added.sem, added.before(b, T))
                    nm.act(act, b)
                    act.wait_ge(vprod.sem, vprod.now(b, 1))
                    act.activation(v[:, 0:4, :].rearrange("p (a t) d -> p a (t d)", a=2), PS[0:R, 0:2, 0:2 * D], ACT.Copy) \
                       .then_inc(vcopy.sem, 1)
                    act.wait_ge(vprod.sem, vprod.now(b, 2))
                    act.activation(v[:, 4, :], PS[0:R, 2, 0:D], ACT.Copy).then_inc(vcopy.sem, 1)
                    with act.Fori(0, NG) as g:
                        tg = b * NG + g
                        for i in range(QG + 1):
                            if i < QG:
                                act.wait_ge(bias.sem, bias.now(tg, i + 1))
                                act.wait_ge(mixed.sem, mixed.now(tg, i - 1) if i >= 2 else mixed.before(tg, QG - 1 + i))
                                act.activation(P[0:HQ, i % 2, :].rearrange("p (a n) -> p a n", a=2),
                                               PS[0:HQ, 2 * (i % 2):2 * (i % 2) + 2, 0:HK], ACT.Exp,
                                               bias=nmx[:, i % 2:i % 2 + 1], accum_out=rs[0:HQ, i % 2:i % 2 + 1]) \
                                   .then_inc(prob.sem, 1)
                            u = i - 1
                            if 0 <= u:
                                act.wait_ge(mixed.sem, mixed.now(tg, u + 1))
                                if u == 0:
                                    act.wait_ge(pv.sem, pv.before(tg, KC))
                                act.activation(P2[:, 0:4, :, u * QT:(u + 1) * QT],
                                               PS[0:R, 4, 0:4 * HQ].rearrange("p (t h n) -> p t h n", t=4, h=H), ACT.Copy)
                                act.activation(P2[0:LAST, 4, :, u * QT:(u + 1) * QT],
                                               PS[0:LAST, 5, 0:HQ].rearrange("p (h n) -> p h n", h=H), ACT.Copy) \
                                   .then_inc(p2copy.sem, 1)

            @block.tensor
            def _(pe):
                nm.turned.prime(pe)
                score.prime(pe)
                mixed.prime(pe)
                pv.prime(pe)
                pe.wait_ge(ready, 6)
                xT = nm.xT
                with pe.Fori(0, B) as b:
                    pe.wait_ge(added.sem, added.before(b, T))
                    nm.pe(pe, b)
                    pe.wait_ge(nm.xT_ready.sem, nm.xT_ready.now(b, 3))
                    for i in range(2 * KC):
                        w, co, bank = (wq if i < KC else wk), i % KC, 4 + 2 * (i % 2)
                        if i >= 2:
                            pe.wait_ge(qcopy.sem, qcopy.now(b, i - 1))
                        for a in range(2):
                            for c in range(KC):
                                ins = pe.matmul(PS[0:C, bank + a, 0:HALF], w[0:kin(c), c, co * C:(co + 1) * C],
                                                xT[0:kin(c), c, a * HALF:(a + 1) * HALF], start=c == 0, stop=c == KC - 1)
                        ins.then_inc(qprod.sem, 1)
                    for t in range(T):
                        for c in range(KC):
                            ins = pe.matmul(PS[0:R, t // 2, t % 2 * D:(t % 2 + 1) * D], xT[0:kin(c), c, t * R:(t + 1) * R],
                                            wv[0:kin(c), c, :], start=c == 0, stop=c == KC - 1)
                        if t >= 3:
                            ins.then_inc(vprod.sem, 1)
                    pe.wait_ge(qcopy.sem, qcopy.now(b, 2 * KC))
                    pe.wait_ge(vcopy.sem, vcopy.now(b, 2))
                    stand(k, pe)
                    with pe.Fori(0, NG) as g:
                        tg = b * NG + g
                        for i in range(QG + 1):
                            if i < QG:
                                bank = 2 * (i % 2)
                                pe.wait_ge(qg_ready.sem, qg_ready.now(tg, i + 1))
                                pe.wait_ge(prob.sem, prob.now(tg, i - 1) if i >= 2 else prob.before(tg, QG - 1 + i))
                                for c in range(KC):
                                    for a in range(2):
                                        ins = pe.matmul(PS[0:HQ, bank + a, 0:HK], qg[0:kin(c), i % 2, c],
                                                        kT[0:kin(c), c, a * HK:(a + 1) * HK], start=c == 0, stop=c == KC - 1)
                                ins.then_inc(score.sem, 1)
                            u = i - 1
                            if 0 <= u:
                                pe.wait_ge(scaled.sem, scaled.now(tg, u + 1))
                                pe.wait_ge(p2copy.sem, p2copy.now(tg, u) if u else p2copy.before(tg, QG))
                                for t in range(T):
                                    ins = pe.matmul(PS[0:rows(t), 4 + t // 4, t % 4 * HQ:(t % 4 + 1) * HQ],
                                                    P[:, u % 2, t * R:t * R + rows(t)], mixn[:, u % 2], start=True, stop=True)
                                ins.then_inc(mixed.sem, 1)
                        pe.wait_ge(p2copy.sem, p2copy.now(tg, QG))
                        for c in range(KC):
                            pe.wait_ge(masked.sem, masked.before(tg, c + 1))
                            for t in range(T):
                                ins = pe.matmul(PS[0:C, 6 + c, 0:HC * GQ], v[0:rows(t), t, c * C:(c + 1) * C],
                                                P2[0:rows(t), t, c * HC:(c + 1) * HC, :], start=t == 0, stop=t == T - 1)
                            ins.then_inc(pv.sem, 1)
                    pe.wait_ge(summed.sem, summed.now(b * NG + (NG - 1), KC))
                    for t in range(T):
                        for c in range(KC):
                            ins = pe.matmul(PS[0:R, t, 0:D], oT[0:kin(c), c, t * R:(t + 1) * R], wo[0:kin(c), c, :],
                                            start=c == 0, stop=c == KC - 1)
                        ins.then_inc(yprod.sem, 1)
    outer.close()



def experts(k, A):
    nc, X, PS = k.nc, k.X, k.PS
    HALF = NP // 2
    with ExitStack() as outer:
        def keep(name, shape):
            return outer.enter_context(nc.sbuf_tensor("ex_" + name, shape, F32))

        xall = keep("xall", [C + 1, B, KC, NP])
        share = keep("share", [R, E1, B * T])
        with ExitStack() as ctx:
            def sb(name, shape):
                return ctx.enter_context(nc.sbuf_tensor("ex_" + name, shape, F32))

            ws = sb("ws", [C + 1, KC, E1])
            rank = sb("rank", [R, E1])
            nm = Norm(k, ctx, "ex_")
            e = sb("e", [R, T, E1])
            mx = sb("mx", [R, T])
            sm = sb("sm", [R, T])
            pm = sb("pm", [R, T])
            w_in, ready = nc.alloc_semaphore("ex_w_in"), nc.alloc_semaphore("ex_ready")
            dv = Signal(nc, "ex_dv", 11)
            logits = Signal(nc, "ex_logits", 1)
            exp_in = Signal(nc, "ex_exp_in", 1)
            exped = Signal(nc, "ex_exped", 1)
            kept = Signal(nc, "ex_kept", 1, primed=True)
            routed = Signal(nc, "ex_routed", 1, primed=True)
            with nc.Block() as block:
                @block.sync
                def _(sp):
                    sp.dma_start(ws[0:C], chunked(A["L1_ffn_Ws"])).then_inc(w_in, 16)
                    sp.dma_start(ws[C:C + 1, KC - 1, :], row(A["L1_ffn_bs"])).then_inc(w_in, 16)
                    sp.wait_ge(w_in, 32)

                @block.gpsimd
                def _(pool):
                    kept.prime(pool)
                    pool.memset(nm.xT[C:C + 1, :, :], 1.0).then_inc(ready, 1)
                    pool.wait_ge(ready, 1)
                    pool.iota(rank[:], pattern=[[-1, E1]], base=E1, channel_multiplier=0,
                              allow_small_or_imprecise_dtypes=True).then_inc(ready, 1)
                    pool.wait_ge(ready, 2)
                    with pool.Fori(0, B) as b:
                        nm.pool(pool, b)
                        pool.wait_ge(nm.xT_ready.sem, nm.xT_ready.now(b, 3))
                        stand(k, pool)
                        pool.tensor_copy(xall[:, b], nm.xT[:]).then_inc(kept.sem, 1)

                @block.vector
                def _(dve):
                    routed.prime(dve)
                    dve.wait_ge(ready, 2)
                    with dve.Fori(0, B) as b:
                        nm.dve(dve, b)
                        step = Chain(dve, dv, b)

                        def wide(a):
                            return a[:].unsqueeze(2).broadcast_to([R, T, E1])

                        dve.wait_ge(logits.sem, logits.now(b, 1))
                        lg = PS[0:R, 3, 0:T * E1].rearrange("p (t e) -> p t e", e=E1)
                        step(dve.tensor_reduce(mx[:], lg, AX.X, ALU.max))
                        dve.tensor_tensor(e[:], lg, wide(mx), ALU.subtract).then_inc(exp_in.sem, 1)
                        dve.wait_ge(exped.sem, exped.now(b, 1))
                        step(dve.tensor_reduce(sm[:], e[:], AX.X, ALU.add))
                        step(dve.reciprocal(sm[:], sm[:]))
                        step(dve.tensor_tensor(e[:], e[:], wide(sm), ALU.mult))
                        step(dve.tensor_reduce(pm[:], e[:], AX.X, ALU.max))
                        step(dve.tensor_tensor(e[:], e[:], wide(pm), ALU.is_equal))
                        step(dve.tensor_tensor(e[:], e[:], rank[:].unsqueeze(1).broadcast_to([R, T, E1]), ALU.mult))
                        step(dve.tensor_reduce(mx[:], e[:], AX.X, ALU.max))
                        step(dve.tensor_tensor(e[:], e[:], wide(mx), ALU.is_equal))
                        step(dve.tensor_tensor(e[:], e[:], wide(pm), ALU.mult))
                        dve.tensor_copy(share[:, :, bass.ds(b * T, T)], e[:].rearrange("p t e -> p e t"))
                        step(dve.tensor_scalar(pm[:], pm[:], -1.0, 1.0, ALU.mult, ALU.add))
                        stand(k, dve)
                        dve.tensor_tensor(share[:, 0, bass.ds(b * T, T)], e[:, :, 0], pm[:], ALU.add).then_inc(routed.sem, 1)
                        step.end()

                @block.scalar
                def _(act):
                    with act.Fori(0, B) as b:
                        act.wait_ge(routed.sem, routed.before(b, 1))
                        act.wait_ge(kept.sem, kept.before(b, 1))
                        nm.act(act, b)
                        act.wait_ge(exp_in.sem, exp_in.now(b, 1))
                        act.activation(e[:], e[:], ACT.Exp).then_inc(exped.sem, 1)

                @block.tensor
                def _(pe):
                    nm.turned.prime(pe)
                    pe.wait_ge(w_in, 32)
                    pe.wait_ge(ready, 2)
                    with pe.Fori(0, B) as b:
                        pe.wait_ge(routed.sem, routed.before(b, 1))
                        nm.pe(pe, b)
                        pe.wait_ge(nm.xT_ready.sem, nm.xT_ready.now(b, 3))
                        for t in range(T):
                            for c in range(KC):
                                ins = pe.matmul(PS[0:R, 3, t * E1:(t + 1) * E1], nm.xT[0:kin(c), c, t * R:(t + 1) * R],
                                                ws[0:kin(c), c, :], start=c == 0, stop=c == KC - 1)
                        ins.then_inc(logits.sem, 1)

        def sb(name, shape):
            return outer.enter_context(nc.sbuf_tensor("ex_" + name, shape, F32))

        w1 = sb("w1", [C + 1, KC, FF])
        w2 = sb("w2", [128, FC, D])
        b2 = sb("b2", [1, D])
        ones = sb("ones", [1, R])
        h = sb("h", [128, FC, NP])
        w1_in = Signal(nc, "ex_w1_in", 32)
        w2_in = Signal(nc, "ex_w2_in", 32)
        hprod = Signal(nc, "ex_hprod", FC, primed=True)
        gelu = Signal(nc, "ex_gelu", FC, primed=True)
        yprod = Signal(nc, "ex_yprod", T, primed=True)
        added = Signal(nc, "ex_added", T, primed=True)
        ready = nc.alloc_semaphore("ex_ready2")
        with nc.Block() as block:
            @block.sync
            def _(sp):
                with sp.Fori(0, E1) as x:
                    sp.wait_ge(hprod.sem, x * (B * FC) + FC)
                    sp.dma_start(w1[0:C], A["L1_ffn_W1"][x].rearrange("(c p) n -> p c n", c=KC)).then_inc(w1_in.sem, 16)
                    sp.dma_start(w1[C:C + 1, KC - 1, :], A["L1_ffn_b1"][bass.ds(x, 1), :]).then_inc(w1_in.sem, 16)
                    sp.wait_ge(yprod.sem, x * (B * T) + T)
                    sp.dma_start(w2[:], A["L1_ffn_W2"][x].rearrange("(c p) n -> p c n", c=FC)).then_inc(w2_in.sem, 16)
                    sp.dma_start(b2[:], A["L1_ffn_b2"][bass.ds(x, 1), :]).then_inc(w2_in.sem, 16)

            @block.gpsimd
            def _(pool):
                pool.memset(ones[:], 1.0).then_inc(ready, 1)

            @block.vector
            def _(dve):
                added.prime(dve)
                with dve.Fori(0, E1) as x:
                    with dve.Fori(0, B) as b:
                        xb = x * B + b
                        for t in range(T):
                            dve.wait_ge(yprod.sem, yprod.now(xb, t + 1))
                            stand(k, dve)
                            xt = X[:, b * T + t, :]
                            dve.scalar_tensor_tensor(xt, PS[0:R, 4 + t % 4, 0:D], share[:, x, bass.ds(b * T + t, 1)], xt,
                                                     ALU.mult, ALU.add).then_inc(added.sem, 1)

            @block.scalar
            def _(act):
                gelu.prime(act)
                with act.Fori(0, E1) as x:
                    with act.Fori(0, B) as b:
                        xb = x * B + b
                        for f in range(FC):
                            act.wait_ge(hprod.sem, hprod.now(xb, f + 1))
                            if f == 0:
                                act.wait_ge(yprod.sem, yprod.before(xb, T))
                            bank = 2 * (f % 2)
                            act.activation(h[:, f, :].rearrange("p (a n) -> p a n", a=2), PS[:, bank:bank + 2, 0:HALF],
                                           ACT.Gelu).then_inc(gelu.sem, 1)

            @block.tensor
            def _(pe):
                hprod.prime(pe)
                yprod.prime(pe)
                pe.wait_ge(ready, 1)
                with pe.Fori(0, E1) as x:
                    pe.wait_ge(w1_in.sem, w1_in.now(x, 32))
                    pe.wait_ge(w2_in.sem, w2_in.now(x, 32))
                    stand(k, pe)
                    with pe.Fori(0, B) as b:
                        xb = x * B + b
                        for f in range(FC):
                            bank = 2 * (f % 2)
                            pe.wait_ge(gelu.sem, gelu.now(xb, f - 1) if f >= 2 else gelu.before(xb, FC - 1 + f))
                            stand(k, pe)
                            for c in range(KC):
                                for a in range(2):
                                    ins = pe.matmul(PS[:, bank + a, 0:HALF], w1[0:kin(c), c, f * 128:(f + 1) * 128],
                                                    xall[0:kin(c), b, c, a * HALF:(a + 1) * HALF], start=c == 0, stop=c == KC - 1)
                            ins.then_inc(hprod.sem, 1)
                        for t in range(T):
                            if t % 4 == 0:
                                pe.wait_ge(added.sem, added.now(xb, 1) if t else added.before(xb, T))
                            for f in range(FC):
                                if t == 0:
                                    pe.wait_ge(gelu.sem, gelu.now(xb, f + 1))
                                pe.matmul(PS[0:R, 4 + t % 4, 0:D], h[:, f, t * R:(t + 1) * R], w2[:, f, :], start=f == 0, stop=False)
                            pe.matmul(PS[0:R, 4 + t % 4, 0:D], ones[:], b2[:], start=False, stop=True).then_inc(yprod.sem, 1)


def store(k, out):
    with k.nc.Block() as block:
        stored = k.nc.alloc_semaphore("stored")

        @block.sync
        def _(sp):
            dst = out.rearrange("b n d -> n b d")
            for t in range(T):
                sp.dma_start(dst[t * R:t * R + rows(t)], k.X[0:rows(t), t::T, :]).then_inc(stored, 16)
            sp.wait_ge(stored, 16 * T)


def build(nc, A, out, stages=99):
    k = Core()
    k.nc = nc
    setup(k, A)
    patch_tokens(k, A)
    if stages >= 1:
        performer(k, A)
    if stages >= 2:
        gated_attention(k, A)
    if stages >= 3:
        talking_heads(k, A)
    if stages >= 4:
        experts(k, A)
    store(k, out)


_AS_IS = ["txt", "L0_tok_conv_w", "L0_tok_conv_b", "L0_tok_proj_b", "L0_tok_pos_emb", "L0_attn_W_qkv",
          "L0_attn_W_proj", "L0_attn_b_proj", "L0_ffn_Wqk", "L0_ffn_bqk", "L0_ffn_Wv", "L0_ffn_bv", "L0_ffn_conv_w",
          "L0_ffn_conv_b", "L0_ffn_Wg1", "L0_ffn_bg1", "L0_ffn_Wg2", "L0_ffn_bg2", "L0_ffn_Wp", "L0_ffn_bp",
          "L1_attn_bq", "L1_attn_bk", "L1_attn_bv", "L1_attn_bo", "L1_attn_th1_b", "L1_attn_th2_b", "L1_ffn_Ws",
          "L1_ffn_bs", "L1_ffn_W1", "L1_ffn_b1", "L1_ffn_W2", "L1_ffn_b2"]


def _patches(a):
    lead = a.shape[:-3]
    n = len(lead)
    a = a.reshape(*lead, CH, SIDE, PATCH, SIDE, PATCH)
    return a.transpose(*range(n), n + 1, n + 3, n, n + 2, n + 4).reshape(*lead, NPATCH, PIX)


def layout(inputs):
    laid = {name: inputs[name] for name in _AS_IS}
    laid["x_patches"] = _patches(inputs["x"])
    laid["tok_ln_w_patches"] = _patches(inputs["L0_tok_ln_w"])
    laid["tok_ln_b_patches"] = _patches(inputs["L0_tok_ln_b"])
    laid["tok_proj_wT"] = inputs["L0_tok_proj_w"].T
    laid["attn_proj_matT"] = inputs["L0_attn_proj_mat"].T
    for n in ("wq", "wk", "wv", "wo", "th1_w", "th2_w"):
        laid[f"attn1_{n}T"] = inputs["L1_attn_" + n].T
    return laid


def kernel(**inputs):
    import numpy as _np
    import concourse.bacc as _bacc
    from concourse import mybir as _mybir
    from concourse.bass_utils import run_bass_kernel_spmd as _run

    nc = _bacc.Bacc("TRN2", target_bir_lowering=False, num_devices=1)
    arrays, args = {}, {}
    for name, a in layout({n: _np.asarray(a) for n, a in inputs.items()}).items():
        a = _np.ascontiguousarray(a)
        arrays[f"in_{name}"] = a
        args[name] = nc.dram_tensor(f"in_{name}", a.shape, _mybir.dt.from_np(a.dtype), kind="ExternalInput").ap()
    out = nc.dram_tensor("out_h", (B, N, D), F32, kind="ExternalOutput").ap()
    build(nc, args, out)
    r = _run(nc, [arrays], core_ids=[0])
    return r.results[0]["out_h"]
```

```python
from contextlib import ExitStack

import concourse.bass as bass
from concourse import mybir
from concourse.alu_op_type import AluOpType as ALU

ACT = mybir.ActivationFunctionType
AX = mybir.AxisListType
F32, I32, U32 = mybir.dt.float32, mybir.dt.int32, mybir.dt.uint32

B = 16
IMG, PATCH, CH = 96, 16, 3
SIDE = IMG // PATCH
NPATCH = SIDE * SIDE
PIX = CH * PATCH * PATCH
NTXT = 512
N = NPATCH + NTXT
R = 110
T = 5
NP = R * T
LAST = N - R * (T - 1)
D = 192
C = 96
KC = D // C
H = 12
HD = D // H
M = 44
HM = H * M // KC
E0 = 3
HD0 = D // E0
HID = 32
E1 = 9
FF = 768
FC = FF // 128
SL = 128
SLOT_TILES = (B * N + E1 * (SL - 1)) // SL
NEG = -1.0e30

QT = 10
QG = 8
NG = 7
NQ = QT * QG * NG
HQ = H * QT


def rows(t):
    return LAST if t == T - 1 else R


class Signal:

    def __init__(self, nc, name, per, primed=False):
        self.sem, self.per, self.first = nc.alloc_semaphore(name), per, int(primed)

    def prime(self, eng):
        eng.sem_inc(self.sem, self.per)

    def now(self, turn, k):
        return turn * self.per + (self.first * self.per + k)

    def before(self, turn, k):
        assert self.first and k >= 1
        return turn * self.per + k


class Chain:

    def __init__(self, eng, marks, turn):
        self.eng, self.marks, self.turn, self.n = eng, marks, turn, 0

    def __call__(self, ins):
        self.n += 1
        ins.then_inc(self.marks.sem, 1)
        self.eng.wait_ge(self.marks.sem, self.marks.now(self.turn, self.n))

    def end(self):
        assert self.n == self.marks.per, (self.n, self.marks.per)


def stand(k, eng):
    eng.sem_inc(k.passed, 1)


class Core:
    pass


def chunked(w):
    return w.rearrange("(c p) n -> p c n", c=KC)


def row(v):
    return v.rearrange("(a n) -> a n", a=1)



def setup(k, A):
    nc = k.nc
    k.X = nc.alloc_sbuf_tensor("X", [R, B * T, D], F32)
    k.ident = nc.alloc_sbuf_tensor("ident", [128, 128], F32)
    k.causal = nc.alloc_sbuf_tensor("causal", [R, R], F32)
    k.mhalf = nc.alloc_sbuf_tensor("mhalf", [128, 16], F32)
    k.passed = nc.alloc_semaphore("passed")
    k.PS = nc.alloc_psum_tensor("PS", [128, 8, 512], F32)
    zeroed = nc.alloc_semaphore("zeroed")
    k.text_in = nc.alloc_semaphore("text_in")
    filled = nc.alloc_semaphore("filled")
    with nc.Block() as block:
        @block.gpsimd
        def _(pool):
            pool.memset(k.ident[:], 0.0).then_inc(filled, 1)
            pool.memset(k.causal[:], 0.0).then_inc(filled, 1)
            pool.memset(k.mhalf[:], -0.5)
            pool.wait_ge(filled, 2)
            pool.affine_select(out=k.ident[:], in_=k.ident[:], compare_op=ALU.not_equal, fill=1.0,
                               base=0, pattern=[[-1, 128]], channel_multiplier=1)
            pool.affine_select(out=k.causal[:], in_=k.causal[:], compare_op=ALU.is_ge, fill=NEG,
                               base=0, pattern=[[-1, R]], channel_multiplier=1)

        @block.vector
        def _(dve):
            dve.memset(k.X[C:R, T - 1::T, :], 0.0).then_inc(zeroed, 1)

        @block.sync
        def _(sp):
            txt = A["txt"].rearrange("b n d -> n b d")
            sp.dma_start(k.X[NPATCH:R, 0::T, :], txt[0:R - NPATCH]).then_inc(k.text_in, 16)
            for t in range(1, T):
                if t == T - 1:
                    sp.wait_ge(zeroed, 1)
                n0 = t * R - NPATCH
                sp.dma_start(k.X[0:rows(t), t::T, :], txt[n0:n0 + rows(t)]).then_inc(k.text_in, 16)
            sp.wait_ge(k.text_in, 16 * T)



def patch_tokens(k, A):
    nc, X, PS = k.nc, k.X, k.PS
    KP = PIX // 128
    with ExitStack() as ctx:
        def sb(name, shape):
            return ctx.enter_context(nc.sbuf_tensor(name, shape, F32))

        projT = sb("tk_projT", [128, KP, D])
        weff = sb("tk_weff", [128, KP, D])
        cw = sb("tk_cw", [128, CH * CH])
        cb = sb("tk_cb", [128, CH])
        cbw = sb("tk_cbw", [128, KP, NPATCH])
        posb = sb("tk_posb", [NPATCH, D])
        pb = sb("tk_pb", [NPATCH, D])
        lnw = sb("tk_lnw", [NPATCH, PIX])
        lnb = sb("tk_lnb", [NPATCH, PIX])
        mean_of = sb("tk_mean_of", [NPATCH, NPATCH])
        img = sb("tk_img", [NPATCH, B, PIX])
        xn = sb("tk_xn", [NPATCH, PIX])
        xT = sb("tk_xT", [128, KP, NPATCH])
        st = sb("tk_st", [NPATCH, 2, 6])
        mv = sb("tk_mv", [NPATCH, 2])
        avg = sb("tk_avg", [NPATCH, 2])
        var = sb("tk_var", [NPATCH, 2])
        rstd = sb("tk_rstd", [NPATCH, 1])

        w_in = nc.alloc_semaphore("tk_w_in")
        img_in = nc.alloc_semaphore("tk_img_in")
        biased = nc.alloc_semaphore("tk_biased")
        copied = nc.alloc_semaphore("tk_copied")
        made = nc.alloc_semaphore("tk_made")

        NW = 16 * 7

        with nc.Block() as block:
            @block.sync
            def _(sp):
                sp.dma_start(projT[:], A["tok_proj_wT"].rearrange("(q p) n -> p q n", p=128)).then_inc(w_in, 16)
                sp.dma_start(cw[:], row(A["L0_tok_conv_w"].rearrange("o c y x -> (o c y x)"))
                             .broadcast_to([128, CH * CH])).then_inc(w_in, 16)
                sp.dma_start(cb[:], row(A["L0_tok_conv_b"]).broadcast_to([128, CH])).then_inc(w_in, 16)
                sp.dma_start(pb[:], row(A["L0_tok_proj_b"]).broadcast_to([NPATCH, D])).then_inc(w_in, 16)
                sp.dma_start(posb[:], A["L0_tok_pos_emb"][0]).then_inc(w_in, 16)
                sp.dma_start(lnw[:], A["tok_ln_w_patches"]).then_inc(w_in, 16)
                sp.dma_start(lnb[:], A["tok_ln_b_patches"]).then_inc(w_in, 16)
                sp.wait_ge(w_in, NW)

            @block.scalar
            def _(act):
                act.dma_start(img[:], A["x_patches"].rearrange("b p n -> p b n")).then_inc(img_in, 16)
                act.wait_ge(img_in, 16)

            @block.gpsimd
            def _(pool):
                pool.memset(mean_of[:], 1.0 / NPATCH)

            @block.tensor
            def _(pe):
                pe.wait_ge(made, 1)
                for q in range(KP):
                    ins = pe.matmul(PS[0:NPATCH, 6, 0:D], cbw[:, q, :], projT[:, q, :],
                                    start=q == 0, stop=q == KP - 1)
                ins.then_inc(biased, 1)

            @block.vector
            def _(dve):
                dve.memset(cbw[:], 0.0).then_inc(copied, 1)
                dve.wait_ge(w_in, NW)
                dve.wait_ge(copied, 1)
                for q in range(KP):
                    ins = dve.tensor_scalar(cbw[:, q, :], cbw[:, q, :], cb[:, q // 2:q // 2 + 1], None, ALU.add)
                ins.then_inc(made, 1)
                n = 1
                for c in range(CH):
                    w = weff[:, 2 * c:2 * c + 2, :]
                    for o in range(CH):
                        s = cw[:, o * CH + c:o * CH + c + 1]
                        p = projT[:, 2 * o:2 * o + 2, :]
                        if o == 0:
                            dve.tensor_scalar(w, p, s, None, ALU.mult).then_inc(copied, 1)
                        else:
                            dve.scalar_tensor_tensor(w, p, s, w, ALU.mult, ALU.add).then_inc(copied, 1)
                        n += 1
                        dve.wait_ge(copied, n)
                dve.tensor_tensor(posb[:], posb[:], pb[:], ALU.add).then_inc(copied, 1)
                dve.wait_ge(copied, n + 1)
                dve.wait_ge(biased, 1)
                dve.tensor_tensor(posb[:], PS[0:NPATCH, 6, 0:D], posb[:], ALU.add).then_inc(copied, 1)

        dv = Signal(nc, "tk_dve", 12)
        stats = Signal(nc, "tk_stats", 1)
        averaged = Signal(nc, "tk_averaged", 1)
        varr = Signal(nc, "tk_varr", 1)
        powed = Signal(nc, "tk_powed", 1)
        normed = Signal(nc, "tk_normed", 1)
        tr = Signal(nc, "tk_tr", 1)
        trc = Signal(nc, "tk_trc", 1)
        prod = Signal(nc, "tk_prod", 1)
        added = Signal(nc, "tk_added", 1, primed=True)
        with nc.Block() as block:
            @block.vector
            def _(dve):
                added.prime(dve)
                with dve.Fori(0, B) as b:
                    step = Chain(dve, dv, b)
                    im = img[:, b, :]
                    dve.bn_stats(st[:, 0, :], im[:, 0:PIX // 2])
                    step(dve.bn_stats(st[:, 1, :], im[:, PIX // 2:PIX]))
                    stand(k, dve)
                    step(dve.bn_aggr(mv[:], st[:]))
                    step(dve.scalar_tensor_tensor(mv[:, 1:2], mv[:, 0:1], mv[:, 0:1], mv[:, 1:2], ALU.mult, ALU.add))
                    dve.sem_inc(stats.sem, 1)
                    dve.wait_ge(averaged.sem, averaged.now(b, 1))
                    step(dve.tensor_copy(avg[:], PS[0:NPATCH, 7, 0:2]))
                    step(dve.tensor_tensor(var[:, 0:1], avg[:, 0:1], avg[:, 0:1], ALU.mult))
                    step(dve.tensor_tensor(var[:, 1:2], avg[:, 1:2], var[:, 0:1], ALU.subtract))
                    step(dve.tensor_scalar(var[:, 1:2], var[:, 1:2], 1e-5, None, ALU.add))
                    dve.sem_inc(varr.sem, 1)
                    dve.wait_ge(powed.sem, powed.now(b, 1))
                    step(dve.tensor_scalar(xn[:], im, avg[:, 0:1], rstd[:, 0:1], ALU.subtract, ALU.mult))
                    step(dve.tensor_tensor(xn[:], xn[:], lnw[:], ALU.mult))
                    step(dve.tensor_tensor(xn[:], xn[:], lnb[:], ALU.add))
                    dve.sem_inc(normed.sem, 1)
                    dve.wait_ge(tr.sem, tr.now(b, 1))
                    step(dve.tensor_copy(xT[:], PS[:, 0, 0:KP * NPATCH].rearrange("p (q n) -> p q n", n=NPATCH)))
                    dve.sem_inc(trc.sem, 1)
                    dve.wait_ge(prod.sem, prod.now(b, 1))
                    step(dve.tensor_tensor(X[0:NPATCH, b * T, :], PS[0:NPATCH, 1, 0:D], posb[:], ALU.add))
                    dve.sem_inc(added.sem, 1)
                    step.end()

            @block.gpsimd
            def _(pool):
                with pool.Fori(0, B) as b:
                    pool.wait_ge(varr.sem, varr.now(b, 1))
                    pool.tensor_tensor(rstd[:], var[:, 1:2], k.mhalf[0:NPATCH, 0:1], ALU.pow).then_inc(powed.sem, 1)

            @block.tensor
            def _(pe):
                with pe.Fori(0, B) as b:
                    pe.wait_ge(stats.sem, stats.now(b, 1))
                    stand(k, pe)
                    pe.matmul(PS[0:NPATCH, 7, 0:2], mean_of[:], mv[:], start=True, stop=True).then_inc(averaged.sem, 1)
                    pe.wait_ge(normed.sem, normed.now(b, 1))
                    stand(k, pe)
                    for q in range(KP):
                        ins = pe.transpose(PS[:, 0, q * NPATCH:(q + 1) * NPATCH], xn[:, q * 128:(q + 1) * 128],
                                           k.ident[0:NPATCH, 0:NPATCH])
                    ins.then_inc(tr.sem, 1)
                    pe.wait_ge(trc.sem, trc.now(b, 1))
                    pe.wait_ge(added.sem, added.before(b, 1))
                    for q in range(KP):
                        ins = pe.matmul(PS[0:NPATCH, 1, 0:D], xT[:, q, :], weff[:, q, :],
                                        start=q == 0, stop=q == KP - 1)
                    ins.then_inc(prod.sem, 1)


class Norm:

    def __init__(self, k, ctx, name):
        nc = k.nc
        self.k = k
        def sb(n, shape):
            return ctx.enter_context(nc.sbuf_tensor(name + n, shape, F32))
        self.st = sb("st", [R, T, 6])
        self.mv = sb("mv", [R, T, 2])
        self.ve = sb("ve", [R, T])
        self.rstd = sb("rstd", [R, T])
        self.xn = sb("xn", [R, T, D])
        self.xT = sb("xT", [C + 1, KC, NP])
        self.dv = Signal(nc, name + "nd", 3)
        self.var_ready = Signal(nc, name + "var", 1)
        self.rstd_ready = Signal(nc, name + "rstd", 1)
        self.xn_ready = Signal(nc, name + "xn", T)
        self.turned = Signal(nc, name + "turned", 3, primed=True)
        self.xT_ready = Signal(nc, name + "xT", 3)

    def dve(self, dve, b):
        k = self.k
        step = Chain(dve, self.dv, b)
        for t in range(T):
            ins = dve.bn_stats(self.st[:, t, :], k.X[:, b * T + t, :])
        step(ins)
        stand(k, dve)
        for t in range(T):
            ins = dve.bn_aggr(self.mv[:, t, :], self.st[:, t, :])
        step(ins)
        step(dve.tensor_scalar(self.ve[:], self.mv[:, :, 1], 1e-5, None, ALU.add))
        step.end()
        dve.sem_inc(self.var_ready.sem, 1)
        dve.wait_ge(self.rstd_ready.sem, self.rstd_ready.now(b, 1))
        dve.wait_ge(self.turned.sem, self.turned.before(b, 3))
        for t in range(T):
            dve.tensor_scalar(self.xn[:, t, :], k.X[:, b * T + t, :], self.mv[:, t, 0:1], self.rstd[:, t:t + 1],
                              ALU.subtract, ALU.mult).then_inc(self.xn_ready.sem, 1)

    def pool(self, pool, b):
        pool.wait_ge(self.var_ready.sem, self.var_ready.now(b, 1))
        pool.tensor_tensor(self.rstd[:], self.ve[:], self.k.mhalf[0:R, 0:T], ALU.pow).then_inc(self.rstd_ready.sem, 1)

    def pe(self, pe, b):
        PS, ident = self.k.PS, self.k.ident
        for t in range(T):
            pe.wait_ge(self.xn_ready.sem, self.xn_ready.now(b, t + 1))
            for c in range(KC):
                bank, at = (c, t * R) if t < T - 1 else (2, c * R)
                ins = pe.transpose(PS[0:C, bank, at:at + R], self.xn[:, t, c * C:(c + 1) * C], ident[0:R, 0:R])
                if t >= T - 2 and not (t == T - 1 and c == 0):
                    ins.then_inc(self.turned.sem, 1)

    def act(self, act, b):
        PS, W = self.k.PS, (T - 1) * R
        for c in range(KC):
            act.wait_ge(self.turned.sem, self.turned.now(b, c + 1))
            act.activation(self.xT[0:C, c, 0:W], PS[0:C, c, 0:W], ACT.Copy).then_inc(self.xT_ready.sem, 1)
        act.wait_ge(self.turned.sem, self.turned.now(b, 3))
        act.activation(self.xT[0:C, :, W:NP], PS[0:C, 2, 0:KC * R].rearrange("p (c n) -> p c n", c=KC), ACT.Copy) \
           .then_inc(self.xT_ready.sem, 1)


def kin(c):
    return C + 1 if c == KC - 1 else C



def performer(k, A):
    nc, X, PS, ident = k.nc, k.X, k.PS, k.ident
    outer = ExitStack()

    def keep(name, shape):
        return outer.enter_context(nc.sbuf_tensor(name, shape, F32))

    wqkv = keep("pf_wqkv", [C, KC, 3 * D])
    wf = keep("pf_wf", [C, KC, 2, KC, HM])
    wp = keep("pf_wp", [C + 1, KC, D])
    nstab = keep("pf_nstab", [128, 1])
    kmax = keep("pf_kmax", [128, B * T])
    mx = keep("pf_mx", [128, 2])

    with ExitStack() as ctx:
        feat = ctx.enter_context(nc.sbuf_tensor("pf_feat", [C, HM], F32))
        wT = ctx.enter_context(nc.sbuf_tensor("pf_wT", [C, 2, KC, D], F32))
        w_in, z, tr, cp, ml = (nc.alloc_semaphore("pf_" + n) for n in ("w_in", "z", "tr", "cp", "ml"))
        HC = H // KC
        NW = 16 * (3 + HC)
        with nc.Block() as block:
            @block.sync
            def _(sp):
                sp.dma_start(wqkv[:], chunked(A["L0_attn_W_qkv"])).then_inc(w_in, 16)
                sp.dma_start(wp[0:C], chunked(A["L0_attn_W_proj"])).then_inc(w_in, 16)
                sp.dma_start(wp[C:C + 1, KC - 1, :], row(A["L0_attn_b_proj"])).then_inc(w_in, 16)
                sp.wait_ge(z, 1)
                for h in range(HC):
                    sp.dma_start(feat[h * HD:(h + 1) * HD, h * M:(h + 1) * M], A["attn_proj_matT"]).then_inc(w_in, 16)
                sp.wait_ge(w_in, NW)

            @block.vector
            def _(dve):
                dve.memset(feat[:], 0.0).then_inc(z, 1)
                dve.memset(kmax[:], -3.0e38).then_inc(z, 1)
                for q in range(2):
                    dve.wait_ge(tr, q + 1)
                    dve.tensor_copy(wT[:, q, :, :], PS[0:C, q, 0:KC * D].rearrange("p (c n) -> p c n", c=KC)).then_inc(cp, 1)
                for q in range(2):
                    for c in range(KC):
                        dve.wait_ge(ml, q * KC + c + 1)
                        dve.tensor_scalar(wf[:, :, q, c, :], PS[0:C, 2 + 2 * c:4 + 2 * c, 0:HM], 0.5, None, ALU.mult) \
                           .then_inc(cp, 1)

            @block.tensor
            def _(pe):
                pe.wait_ge(w_in, NW)
                for q in range(2):
                    for c in range(KC):
                        for ci in range(KC):
                            ins = pe.transpose(PS[0:C, q, c * D + ci * C:c * D + (ci + 1) * C],
                                               wqkv[:, ci, q * D + c * C:q * D + (c + 1) * C], ident[0:C, 0:C])
                    ins.then_inc(tr, 1)
                for q in range(2):
                    pe.wait_ge(cp, q + 1)
                    if q:
                        pe.wait_ge(cp, 2 + KC)
                    for c in range(KC):
                        for ci in range(KC):
                            ins = pe.matmul(PS[0:C, 2 + 2 * c + ci, 0:HM], wT[:, q, c, ci * C:(ci + 1) * C], feat[:],
                                            start=True, stop=True)
                        ins.then_inc(ml, 1)

    with ExitStack() as ctx:
        nm = Norm(k, ctx, "pm_")
        begun = nc.alloc_semaphore("pm_begun")
        prod = Signal(nc, "pm_prod", T)
        reduced = Signal(nc, "pm_reduced", T, primed=True)
        with nc.Block() as block:
            @block.vector
            def _(dve):
                reduced.prime(dve)
                with dve.Fori(0, B) as b:
                    nm.dve(dve, b)
                    for t in range(T):
                        p = 3 + 2 * (t % 2)
                        dve.wait_ge(prod.sem, prod.now(b, t + 1))
                        dve.tensor_reduce(kmax[0:rows(t), bass.ds(b * T + t, 1)],
                                          PS[0:rows(t), p:p + 2, 0:HM], AX.XY, ALU.max).then_inc(reduced.sem, 1)

            @block.gpsimd
            def _(pool):
                with pool.Fori(0, B) as b:
                    nm.pool(pool, b)

            @block.scalar
            def _(act):
                with act.Fori(0, B) as b:
                    act.wait_ge(reduced.sem, reduced.before(b, T))
                    nm.act(act, b)

            @block.tensor
            def _(pe):
                nm.turned.prime(pe)
                with pe.Fori(0, B) as b:
                    pe.wait_ge(reduced.sem, reduced.before(b, T))
                    nm.pe(pe, b)
                    pe.wait_ge(nm.xT_ready.sem, nm.xT_ready.now(b, 3))
                    for t in range(T):
                        p = 3 + 2 * (t % 2)
                        pe.wait_ge(reduced.sem, reduced.now(b, t - 1) if t >= 2 else reduced.before(b, T - 1 + t))
                        for c in range(KC):
                            for ci in range(KC):
                                ins = pe.matmul(PS[0:rows(t), p + c, 0:HM], nm.xT[0:C, ci, t * R:t * R + rows(t)],
                                                wf[:, ci, 1, c, :], start=ci == 0, stop=ci == KC - 1)
                        ins.then_inc(prod.sem, 1)

    with nc.Block() as block:
        r, g = nc.alloc_semaphore("pf_r"), nc.alloc_semaphore("pf_g")

        @block.vector
        def _(dve):
            dve.tensor_reduce(mx[:, 0:1], kmax[:], AX.X, ALU.max).then_inc(r, 1)
            dve.wait_ge(g, 1)
            dve.tensor_scalar(nstab[:], mx[:, 1:2], -1.0, None, ALU.mult).then_inc(r, 1)

        @block.gpsimd
        def _(pool):
            pool.wait_ge(r, 1)
            pool.partition_all_reduce(mx[:, 1:2], mx[:, 0:1], 128, bass.bass_isa.ReduceOp.max).then_inc(g, 1)

    RATIO, EPS, HC = M ** -0.5, 1e-4, H // KC
    with ExitStack() as ctx:
        def sb(name, shape):
            return ctx.enter_context(nc.sbuf_tensor("pf_" + name, shape, F32))

        nm = Norm(k, ctx, "pf_")
        sq = sb("sq", [R, 2, D])
        diag = sb("diag", [R, 2, H])
        mq = sb("mq", [R, H])
        e = sb("e", [R, 2, KC, HM])
        f = sb("f", [R, 2, KC, HM])
        v1 = sb("v1", [R, 2, KC, C + 1])
        kvS = sb("kvS", [C + 1, KC, HM])
        kv = sb("kv", [2 * M, KC, HC // 2, 2, HD + 1])
        own = sb("own", [2 * M, 2])
        fT = sb("fT", [2 * M, H // 2, R])
        z = sb("z", [R, H])
        o = sb("o", [R, D])
        oT = sb("oT", [C + 1, KC, R])

        ready = nc.alloc_semaphore("pf_ready")
        dvk = Signal(nc, "pf_dvk", T)
        dvq = Signal(nc, "pf_dvq", 3 * T)
        kprod = Signal(nc, "pf_kprod", T)
        ksq = Signal(nc, "pf_ksq", T)
        kexp_in = Signal(nc, "pf_kexp_in", T, primed=True)
        kexp = Signal(nc, "pf_kexp", T)
        kf = Signal(nc, "pf_kf", T)
        kvacc = Signal(nc, "pf_kvacc", T)
        kvcopy = Signal(nc, "pf_kvcopy", 1)
        kvturn = Signal(nc, "pf_kvturn", 1)
        kvmade = Signal(nc, "pf_kvmade", 1)
        qprod = Signal(nc, "pf_qprod", T)
        qsq = Signal(nc, "pf_qsq", T)
        qexp_in = Signal(nc, "pf_qexp_in", T)
        qexp = Signal(nc, "pf_qexp", T)
        qf = Signal(nc, "pf_qf", T)
        qturn = Signal(nc, "pf_qturn", T)
        qTc = Signal(nc, "pf_qTc", T)
        num = Signal(nc, "pf_num", T)
        o_ready = Signal(nc, "pf_o", T)
        oturn = Signal(nc, "pf_oturn", T)
        oTc = Signal(nc, "pf_oTc", T)
        yprod = Signal(nc, "pf_y", T)
        added = Signal(nc, "pf_added", T, primed=True)

        def by_head(a):
            return a.rearrange("p c (h m) -> p c h m", m=M)

        with nc.Block() as block:
            @block.gpsimd
            def _(pool):
                pool.memset(own[:], 1.0).then_inc(ready, 1)
                pool.wait_ge(ready, 1)
                pool.memset(v1[:, :, :, C:C + 1], 1.0).then_inc(ready, 1)
                pool.wait_ge(ready, 2)
                pool.memset(oT[C:C + 1, :, :], 1.0).then_inc(ready, 1)
                pool.wait_ge(ready, 3)
                pool.affine_select(out=own[:, 0:1], in_=own[:, 0:1], compare_op=ALU.is_gt, fill=0.0, base=M,
                                   pattern=[[0, 1]], channel_multiplier=-1).then_inc(ready, 1)
                pool.affine_select(out=own[:, 1:2], in_=own[:, 1:2], compare_op=ALU.is_ge, fill=0.0, base=-M,
                                   pattern=[[0, 1]], channel_multiplier=1).then_inc(ready, 1)
                with pool.Fori(0, B) as b:
                    nm.pool(pool, b)
                    for t in range(T):
                        p = t % 2
                        pool.wait_ge(kexp.sem, kexp.now(b, t + 1))
                        if t >= 2:
                            pool.wait_ge(kvacc.sem, kvacc.now(b, t - 1))
                        stand(k, pool)
                        pool.tensor_scalar(f[:, p], e[:, p], EPS, RATIO, ALU.add, ALU.mult).then_inc(kf.sem, 1)
                    for t in range(T):
                        p = t % 2
                        pool.wait_ge(qexp.sem, qexp.now(b, t + 1))
                        if t >= 2:
                            pool.wait_ge(qturn.sem, qturn.now(b, t - 1))
                        else:
                            pool.wait_ge(kvacc.sem, kvacc.now(b, T))
                        stand(k, pool)
                        pool.tensor_scalar(f[:, p], e[:, p], EPS, RATIO, ALU.add, ALU.mult).then_inc(qf.sem, 1)

            @block.vector
            def _(dve):
                kexp_in.prime(dve)
                added.prime(dve)
                dve.wait_ge(ready, 5)
                with dve.Fori(0, B) as b:
                    nm.dve(dve, b)
                    step = Chain(dve, dvk, b)
                    for t in range(T):
                        p = t % 2
                        dve.wait_ge(ksq.sem, ksq.now(b, t + 1))
                        step(dve.tensor_reduce(diag[:, p, :], sq[:, p, :].rearrange("p (h d) -> p h d", d=HD), AX.X, ALU.add))
                        if t >= 2:
                            dve.wait_ge(kf.sem, kf.now(b, t - 1))
                        dve.tensor_tensor(by_head(e[:, p]), by_head(PS[0:R, 3 * p:3 * p + 2, 0:HM]),
                                          diag[:, p, :].rearrange("p (c h) -> p c h", c=KC).unsqueeze(3)
                                          .broadcast_to([R, KC, HC, M]), ALU.subtract).then_inc(kexp_in.sem, 1)
                    step.end()
                    dve.wait_ge(kvturn.sem, kvturn.now(b, 1))
                    for j in range(HC // 2):
                        dve.tensor_tensor(kv[:, :, j, :, 0:HD],
                                          PS[0:2 * M, 3:5, j * (C + 1) + 2 * j * HD:j * (C + 1) + 2 * (j + 1) * HD]
                                          .rearrange("p c (a d) -> p c a d", d=HD),
                                          own[:].unsqueeze(1).unsqueeze(3).broadcast_to([2 * M, KC, 2, HD]), ALU.mult)
                    for j in range(HC // 2):
                        at = j * (C + 1) + C
                        ins = dve.tensor_tensor(kv[:, :, j, :, HD:HD + 1],
                                                PS[0:2 * M, 3:5, at:at + 1].unsqueeze(2).broadcast_to([2 * M, KC, 2, 1]),
                                                own[:].unsqueeze(1).unsqueeze(3).broadcast_to([2 * M, KC, 2, 1]), ALU.mult)
                    ins.then_inc(kvmade.sem, 1)
                    step = Chain(dve, dvq, b)
                    for t in range(T):
                        p = t % 2
                        dve.wait_ge(qprod.sem, qprod.now(b, t + 1))
                        dve.tensor_reduce(mq[:], by_head(PS[0:R, 0:2, 0:HM]), AX.X, ALU.max)
                        dve.wait_ge(qsq.sem, qsq.now(b, t + 1))
                        step(dve.tensor_reduce(diag[:, p, :], sq[:, p, :].rearrange("p (h d) -> p h d", d=HD), AX.X, ALU.add))
                        step(dve.tensor_tensor(diag[:, p, :], diag[:, p, :], mq[:], ALU.add))
                        if t >= 2:
                            dve.wait_ge(qf.sem, qf.now(b, t - 1))
                        else:
                            dve.wait_ge(kf.sem, kf.now(b, T))
                        dve.tensor_tensor(by_head(e[:, p]), by_head(PS[0:R, 0:2, 0:HM]),
                                          diag[:, p, :].rearrange("p (c h) -> p c h", c=KC).unsqueeze(3)
                                          .broadcast_to([R, KC, HC, M]), ALU.subtract).then_inc(qexp_in.sem, 1)
                        dve.wait_ge(num.sem, num.now(b, t + 1))
                        on = PS[0:R, 5, 0:H * (HD + 1)].rearrange("p (h d) -> p h d", d=HD + 1)
                        step(dve.reciprocal(z[:], on[:, :, HD]))
                        dve.tensor_tensor(o[:].rearrange("p (h d) -> p h d", d=HD), on[:, :, 0:HD],
                                          z[:].unsqueeze(2).broadcast_to([R, H, HD]), ALU.mult).then_inc(o_ready.sem, 1)
                        dve.wait_ge(yprod.sem, yprod.now(b, t + 1))
                        dve.tensor_tensor(X[:, b * T + t, :], PS[0:R, 7, 0:D], X[:, b * T + t, :], ALU.add) \
                           .then_inc(added.sem, 1)
                    step.end()

            @block.scalar
            def _(act):
                HALF = 0.125 ** 0.5
                with act.Fori(0, B) as b:
                    act.wait_ge(added.sem, added.before(b, T))
                    nm.act(act, b)
                    for t in range(T):
                        p = t % 2
                        act.wait_ge(kprod.sem, kprod.now(b, t + 1))
                        if t >= 2:
                            act.wait_ge(kexp_in.sem, kexp_in.now(b, t - 1))
                            act.wait_ge(kvacc.sem, kvacc.now(b, t - 1))
                        act.activation(v1[:, p, :, 0:C], PS[0:R, 3 * p + 2, D:2 * D].rearrange("p (c d) -> p c d", c=KC), ACT.Copy)
                        act.activation(sq[:, p, :], PS[0:R, 3 * p + 2, 0:D], ACT.Square, scale=HALF).then_inc(ksq.sem, 1)
                        act.wait_ge(kexp_in.sem, kexp_in.now(b, t + 1))
                        act.activation(e[:, p], e[:, p], ACT.Exp, bias=nstab[0:R, :]).then_inc(kexp.sem, 1)
                    act.wait_ge(kvacc.sem, kvacc.now(b, T))
                    act.activation(kvS[:], PS[0:C + 1, 6:8, 0:HM], ACT.Copy).then_inc(kvcopy.sem, 1)
                    for t in range(T):
                        p = t % 2
                        act.wait_ge(qprod.sem, qprod.now(b, t + 1))
                        if t >= 2:
                            act.wait_ge(qexp_in.sem, qexp_in.now(b, t - 1))
                        act.activation(sq[:, p, :], PS[0:R, 2, 0:D], ACT.Square, scale=HALF).then_inc(qsq.sem, 1)
                        act.wait_ge(qexp_in.sem, qexp_in.now(b, t + 1))
                        act.activation(e[:, p], e[:, p], ACT.Exp).then_inc(qexp.sem, 1)
                        act.wait_ge(qturn.sem, qturn.now(b, t + 1))
                        act.activation(fT[:].rearrange("p (c j) n -> p c j n", c=KC),
                                       PS[0:2 * M, 3:5, 0:HC // 2 * R].rearrange("p c (j n) -> p c j n", n=R), ACT.Copy) \
                           .then_inc(qTc.sem, 1)
                        act.wait_ge(oturn.sem, oturn.now(b, t + 1))
                        act.activation(oT[0:C], PS[0:C, 6, 0:KC * R].rearrange("p (c n) -> p c n", c=KC), ACT.Copy) \
                           .then_inc(oTc.sem, 1)

            @block.tensor
            def _(pe):
                nm.turned.prime(pe)
                pe.wait_ge(ready, 5)
                xT = nm.xT
                with pe.Fori(0, B) as b:
                    pe.wait_ge(added.sem, added.before(b, T))
                    nm.pe(pe, b)
                    pe.wait_ge(nm.xT_ready.sem, nm.xT_ready.now(b, 3))

                    def k_products(t):
                        p = 3 * (t % 2)
                        if t >= 2:
                            pe.wait_ge(kexp_in.sem, kexp_in.now(b, t - 1))
                        a = slice(t * R, t * R + R)
                        for ci in range(KC):
                            pe.matmul(PS[0:R, p + 2, 0:2 * D], xT[0:C, ci, a], wqkv[:, ci, D:3 * D],
                                      start=ci == 0, stop=ci == KC - 1)
                        for c in range(KC):
                            for ci in range(KC):
                                ins = pe.matmul(PS[0:R, p + c, 0:HM], xT[0:C, ci, a], wf[:, ci, 1, c, :],
                                                start=ci == 0, stop=ci == KC - 1)
                        ins.then_inc(kprod.sem, 1)

                    k_products(0)
                    for t in range(T):
                        if t + 1 < T:
                            k_products(t + 1)
                        pe.wait_ge(kf.sem, kf.now(b, t + 1))
                        for c in range(KC):
                            ins = pe.matmul(PS[0:C + 1, 6 + c, 0:HM], v1[0:rows(t), t % 2, c, :], f[0:rows(t), t % 2, c, :],
                                            start=t == 0, stop=t == T - 1)
                        ins.then_inc(kvacc.sem, 1)
                    pe.wait_ge(kvcopy.sem, kvcopy.now(b, 1))
                    for c in range(KC):
                        for j in range(HC // 2):
                            ins = pe.transpose(PS[0:2 * M, 3 + c, j * (C + 1):(j + 1) * (C + 1)],
                                               kvS[:, c, j * 2 * M:(j + 1) * 2 * M], ident[0:C + 1, 0:C + 1])
                    ins.then_inc(kvturn.sem, 1)
                    pe.wait_ge(kvmade.sem, kvmade.now(b, 1))
                    for t in range(T):
                        a = slice(t * R, t * R + R)
                        if t:
                            pe.wait_ge(qexp_in.sem, qexp_in.now(b, t))
                        for ci in range(KC):
                            pe.matmul(PS[0:R, 2, 0:D], xT[0:C, ci, a], wqkv[:, ci, 0:D], start=ci == 0, stop=ci == KC - 1)
                        for c in range(KC):
                            for ci in range(KC):
                                ins = pe.matmul(PS[0:R, c, 0:HM], xT[0:C, ci, a], wf[:, ci, 0, c, :],
                                                start=ci == 0, stop=ci == KC - 1)
                        ins.then_inc(qprod.sem, 1)
                        pe.wait_ge(qf.sem, qf.now(b, t + 1))
                        for c in range(KC):
                            for j in range(HC // 2):
                                ins = pe.transpose(PS[0:2 * M, 3 + c, j * R:(j + 1) * R],
                                                   f[:, t % 2, c, j * 2 * M:(j + 1) * 2 * M], ident[0:R, 0:R])
                        ins.then_inc(qturn.sem, 1)
                        pe.wait_ge(qTc.sem, qTc.now(b, t + 1))
                        for j in range(H // 2):
                            ins = pe.matmul(PS[0:R, 5, j * 2 * (HD + 1):(j + 1) * 2 * (HD + 1)], fT[:, j, :],
                                            kv[:, j // (HC // 2), j % (HC // 2), :, :], start=True, stop=True)
                        ins.then_inc(num.sem, 1)
                        pe.wait_ge(o_ready.sem, o_ready.now(b, t + 1))
                        for c in range(KC):
                            ins = pe.transpose(PS[0:C, 6, c * R:(c + 1) * R], o[:, c * C:(c + 1) * C], ident[0:R, 0:R])
                        ins.then_inc(oturn.sem, 1)
                        pe.wait_ge(oTc.sem, oTc.now(b, t + 1))
                        for c in range(KC):
                            ins = pe.matmul(PS[0:R, 7, 0:D], oT[0:kin(c), c, :], wp[0:kin(c), c, :],
                                            start=c == 0, stop=c == KC - 1)
                        ins.then_inc(yprod.sem, 1)
    outer.close()


def gated_attention(k, A):
    nc, X, PS, ident = k.nc, k.X, k.PS, k.ident
    SCALE = HD0 ** -0.5
    NU = T * E0
    HALF = NP // 2
    with ExitStack() as ctx:
        def sb(name, shape):
            return ctx.enter_context(nc.sbuf_tensor("ga_" + name, shape, F32))

        wqk = sb("wqk", [C + 1, KC, 2 * D])
        wv = sb("wv", [C + 1, KC, D])
        wg1 = sb("wg1", [C + 1, KC, HID])
        wg2 = sb("wg2", [HID + 1, E0])
        wp = sb("wp", [C + 1, KC, D])
        cw = sb("cw", [HD0, 3])
        cb = sb("cb", [HD0, 1])
        w_in = nc.alloc_semaphore("ga_w_in")
        NW = 16 * (4 * 2 + 2 * E0 + 2 + 2 + 2 + 2)
        GROUPS = [(0, 128, 0), (D, 128, 128), (128, 64, 256), (D + 128, 64, 320)]

        def load(sp):
            for src, n, dst in GROUPS:
                sp.dma_start(wqk[0:C, :, dst:dst + n], chunked(A["L0_ffn_Wqk"])[:, :, src:src + n]).then_inc(w_in, 16)
                sp.dma_start(wqk[C:C + 1, KC - 1, dst:dst + n], row(A["L0_ffn_bqk"])[:, src:src + n]).then_inc(w_in, 16)
            for e in range(E0):
                sp.dma_start(wv[0:C, :, e * HD0:(e + 1) * HD0], chunked(A["L0_ffn_Wv"][e])).then_inc(w_in, 16)
                sp.dma_start(wv[C:C + 1, KC - 1, e * HD0:(e + 1) * HD0], row(A["L0_ffn_bv"][e])).then_inc(w_in, 16)
            sp.dma_start(wg1[0:C], chunked(A["L0_ffn_Wg1"])).then_inc(w_in, 16)
            sp.dma_start(wg1[C:C + 1, KC - 1, :], row(A["L0_ffn_bg1"])).then_inc(w_in, 16)
            sp.dma_start(wg2[0:HID], A["L0_ffn_Wg2"]).then_inc(w_in, 16)
            sp.dma_start(wg2[HID:HID + 1], row(A["L0_ffn_bg2"])).then_inc(w_in, 16)
            sp.dma_start(wp[0:C], chunked(A["L0_ffn_Wp"])).then_inc(w_in, 16)
            sp.dma_start(wp[C:C + 1, KC - 1, :], row(A["L0_ffn_bp"])).then_inc(w_in, 16)
            sp.dma_start(cw[:], A["L0_ffn_conv_w"].rearrange("d a w -> d (a w)")).then_inc(w_in, 16)
            sp.dma_start(cb[:], A["L0_ffn_conv_b"].rearrange("(d a) -> d a", a=1)).then_inc(w_in, 16)
            sp.wait_ge(w_in, NW)

        nm = Norm(k, ctx, "ga_")
        g1 = sb("g1", [HID + 1, NP])
        gm = sb("gm", [R, T])
        gs = sb("gs", [R, T])
        g = sb("g", [R, T, E0])
        e3 = sb("e3", [R, T, E0])
        kept = sb("kept", [R, T, E0])
        m01 = sb("m01", [R, T])
        w = sb("w", [R, T, E0])
        q01 = sb("q01", [128, NP + 2])
        qc = sb("qc", [HD0, NP])
        k01 = sb("k01", [128, NP])
        q2 = sb("q2", [HD0, NP])
        k2 = sb("k2", [HD0, NP])
        v = sb("v", [R, T, D])
        nmx = sb("nmx", [R, NU])
        rs = sb("rs", [R, NU])
        rw = sb("rw", [R, NU])
        P = sb("P", [R, 2, N])
        PT = sb("PT", [R, 2, T, R])
        comb = sb("comb", [R, 2, D])
        cT = sb("cT", [C + 1, KC, R])

        ready = nc.alloc_semaphore("ga_ready")
        dvg = Signal(nc, "ga_dvg", 15)
        dvc = Signal(nc, "ga_dvc", 2)
        dvu = Signal(nc, "ga_dvu", 2 * NU)
        hidden = Signal(nc, "ga_hidden", 1)
        relued = Signal(nc, "ga_relued", 1)
        logits = Signal(nc, "ga_logits", 1)
        gexp_in = Signal(nc, "ga_gexp_in", 2)
        gexp = Signal(nc, "ga_gexp", 2)
        qkprod = Signal(nc, "ga_qkprod", 4)
        qkcopy = Signal(nc, "ga_qkcopy", 5)
        conv = Signal(nc, "ga_conv", 1)
        vprod = Signal(nc, "ga_vprod", 2)
        vcopy = Signal(nc, "ga_vcopy", 2)
        score = Signal(nc, "ga_score", NU)
        bias = Signal(nc, "ga_bias", NU)
        prob = Signal(nc, "ga_prob", NU)
        weight = Signal(nc, "ga_weight", NU)
        turned = Signal(nc, "ga_pturned", NU)
        ptcopy = Signal(nc, "ga_ptcopy", NU)
        pv = Signal(nc, "ga_pv", NU)
        combined = Signal(nc, "ga_combined", NU)
        cturn = Signal(nc, "ga_cturn", T)
        ccopy = Signal(nc, "ga_ccopy", T)
        yprod = Signal(nc, "ga_y", T)
        added = Signal(nc, "ga_added", T, primed=True)

        def keys(u):
            return min((u // E0 + 1) * R, N)

        def scores(u):
            b0 = 2 * (u % 2)
            return PS[0:R, b0:b0 + 2, :].rearrange("p a n -> p (a n)")[:, 0:keys(u)]

        def last_of_tile(u):
            return 0 <= u < NU and u % E0 == E0 - 1

        with nc.Block() as block:
            @block.sync
            def _(sp):
                load(sp)

            @block.gpsimd
            def _(pool):
                pool.memset(g1[HID:HID + 1, :], 1.0).then_inc(ready, 1)
                pool.wait_ge(ready, 1)
                pool.memset(q01[:], 0.0).then_inc(ready, 1)
                pool.memset(qc[:], 0.0).then_inc(ready, 1)
                pool.wait_ge(ready, 3)
                pool.memset(cT[C:C + 1, :, :], 1.0).then_inc(ready, 1)
                pool.wait_ge(ready, 4)
                pool.memset(nm.xT[C:C + 1, :, :], 1.0).then_inc(ready, 1)
                with pool.Fori(0, B) as b:
                    nm.pool(pool, b)

            @block.vector
            def _(dve):
                added.prime(dve)
                dve.wait_ge(ready, 5)
                dve.wait_ge(w_in, NW)
                with dve.Fori(0, B) as b:
                    nm.dve(dve, b)
                    step = Chain(dve, dvc, b)
                    dve.wait_ge(qkprod.sem, qkprod.now(b, 1))
                    dve.tensor_copy(q01[:, 1:1 + HALF], PS[:, 6, 0:HALF]).then_inc(qkcopy.sem, 1)
                    dve.tensor_copy(q01[:, 1 + HALF:1 + N], PS[:, 7, 0:N - HALF]).then_inc(qkcopy.sem, 1)
                    dve.wait_ge(qkprod.sem, qkprod.now(b, 2))
                    dve.tensor_copy(k01[:].rearrange("p (a n) -> p a n", a=2), PS[:, 3:5, 0:HALF]).then_inc(qkcopy.sem, 1)
                    dve.wait_ge(qkcopy.sem, qkcopy.now(b, 2))
                    step(dve.tensor_scalar(qc[:, 0:N], q01[0:HD0, 1:N + 1], cw[:, 1:2], cb[:, 0:1], ALU.mult, ALU.add))
                    step(dve.scalar_tensor_tensor(qc[:, 0:N], q01[0:HD0, 0:N], cw[:, 0:1], qc[:, 0:N], ALU.mult, ALU.add))
                    dve.scalar_tensor_tensor(qc[:, 0:N], q01[0:HD0, 2:N + 2], cw[:, 2:3], qc[:, 0:N],
                                             ALU.mult, ALU.add).then_inc(conv.sem, 1)
                    step.end()
                    dve.wait_ge(qkprod.sem, qkprod.now(b, 3))
                    dve.tensor_copy(q2[:].rearrange("p (a n) -> p a n", a=2), PS[0:HD0, 6:8, 0:HALF]).then_inc(qkcopy.sem, 1)
                    dve.wait_ge(qkprod.sem, qkprod.now(b, 4))
                    dve.tensor_copy(k2[:].rearrange("p (a n) -> p a n", a=2), PS[0:HD0, 3:5, 0:HALF]).then_inc(qkcopy.sem, 1)
                    step = Chain(dve, dvg, b)

                    def wide(a):
                        return a[:].unsqueeze(2).broadcast_to([R, T, E0])

                    dve.wait_ge(logits.sem, logits.now(b, 1))
                    lg = PS[0:R, 5, 0:T * E0].rearrange("p (t e) -> p t e", e=E0)
                    step(dve.tensor_reduce(gm[:], lg, AX.X, ALU.max))
                    dve.tensor_tensor(e3[:], lg, wide(gm), ALU.subtract).then_inc(gexp_in.sem, 1)
                    dve.wait_ge(gexp.sem, gexp.now(b, 1))
                    step(dve.tensor_reduce(gs[:], e3[:], AX.X, ALU.add))
                    step(dve.reciprocal(gs[:], gs[:]))
                    step(dve.tensor_tensor(g[:], e3[:], wide(gs), ALU.mult))
                    dve.tensor_tensor(m01[:], g[:, :, 0], g[:, :, 1], ALU.min)
                    dve.tensor_tensor(kept[:, :, 1], g[:, :, 1], g[:, :, 0], ALU.is_gt)
                    step(dve.tensor_reduce(gm[:], g[:], AX.X, ALU.max))
                    step(dve.tensor_tensor(kept[:, :, 2], g[:, :, 2], m01[:], ALU.is_gt))
                    dve.tensor_tensor(e3[:], g[:], wide(gm), ALU.subtract).then_inc(gexp_in.sem, 1)
                    step(dve.tensor_scalar(m01[:], kept[:, :, 2], -1.0, 1.0, ALU.mult, ALU.add))
                    step(dve.tensor_tensor(kept[:, :, 1], kept[:, :, 1], m01[:], ALU.max))
                    step(dve.tensor_tensor(m01[:], kept[:, :, 1], kept[:, :, 2], ALU.add))
                    step(dve.tensor_scalar(kept[:, :, 0], m01[:], -1.0, 2.0, ALU.mult, ALU.add))
                    dve.wait_ge(gexp.sem, gexp.now(b, 2))
                    step(dve.tensor_tensor(e3[:], e3[:], kept[:], ALU.mult))
                    step(dve.tensor_reduce(gs[:], e3[:], AX.X, ALU.add))
                    step(dve.reciprocal(gs[:], gs[:]))
                    step(dve.tensor_tensor(w[:], e3[:], wide(gs), ALU.mult))
                    step(dve.tensor_scalar(nmx[:, 0:1], w[:, 0, 0:1], 0.0, None, ALU.mult))
                    step.end()
                    step = Chain(dve, dvu, b)
                    for i in range(NU + 5):
                        if i < NU:
                            dve.wait_ge(score.sem, score.now(b, i + 1))
                            step(dve.tensor_reduce(nmx[:, i:i + 1], scores(i), AX.X, ALU.max, negate=True))
                            dve.tensor_scalar(nmx[:, i:i + 1], nmx[:, i:i + 1], SCALE, None, ALU.mult).then_inc(bias.sem, 1)
                        u = i - 1
                        if 0 <= u < NU:
                            dve.wait_ge(prob.sem, prob.now(b, u + 1))
                            step(dve.reciprocal(rw[:, u:u + 1], rs[:, u:u + 1]))
                            dve.tensor_tensor(rw[:, u:u + 1], rw[:, u:u + 1], w[:, u // E0, u % E0:u % E0 + 1], ALU.mult) \
                               .then_inc(weight.sem, 1)
                        u = i - 2
                        if 0 <= u < NU:
                            dve.wait_ge(pv.sem, pv.now(b, u + 1))
                            dve.wait_ge(weight.sem, weight.now(b, u + 1))
                            e = u % E0
                            dve.tensor_scalar(comb[:, u // E0 % 2, e * HD0:(e + 1) * HD0], PS[0:R, 6, 0:HD0],
                                              rw[:, u:u + 1], None, ALU.mult).then_inc(combined.sem, 1)
                        if last_of_tile(i - 4):
                            t = (i - 4) // E0
                            dve.wait_ge(yprod.sem, yprod.now(b, t + 1))
                            dve.tensor_tensor(X[:, b * T + t, :], PS[0:R, 7, 256:256 + D], X[:, b * T + t, :], ALU.add) \
                               .then_inc(added.sem, 1)
                    step.end()

            @block.scalar
            def _(act):
                with act.Fori(0, B) as b:
                    act.wait_ge(added.sem, added.before(b, T))
                    nm.act(act, b)
                    act.wait_ge(hidden.sem, hidden.now(b, 1))
                    act.activation(g1[0:HID, :].rearrange("p (a n) -> p a n", a=2), PS[0:HID, 3:5, 0:HALF], ACT.Relu) \
                       .then_inc(relued.sem, 1)
                    act.wait_ge(vprod.sem, vprod.now(b, 1))
                    act.activation(v[:, 0:4, :].rearrange("p (a t) d -> p a (t d)", a=2), PS[0:R, 0:2, 0:2 * D], ACT.Copy) \
                       .then_inc(vcopy.sem, 1)
                    act.wait_ge(vprod.sem, vprod.now(b, 2))
                    act.activation(v[:, 4, :], PS[0:R, 2, 0:D], ACT.Copy).then_inc(vcopy.sem, 1)
                    for i in range(2):
                        act.wait_ge(gexp_in.sem, gexp_in.now(b, i + 1))
                        act.activation(e3[:], e3[:], ACT.Exp).then_inc(gexp.sem, 1)
                    for i in range(NU + 4):
                        if i < NU:
                            act.wait_ge(bias.sem, bias.now(b, i + 1))
                            if i >= 2:
                                act.wait_ge(turned.sem, turned.now(b, i - 1))
                            act.activation(P[:, i % 2, 0:keys(i)], scores(i), ACT.Exp, bias=nmx[:, i:i + 1], scale=SCALE,
                                           accum_out=rs[:, i:i + 1]).then_inc(prob.sem, 1)
                        u = i - 1
                        if 0 <= u < NU:
                            act.wait_ge(turned.sem, turned.now(b, u + 1))
                            if u >= 2:
                                act.wait_ge(pv.sem, pv.now(b, u - 1))
                            n = min(u // E0 + 1, 4)
                            ins = act.activation(PT[:, u % 2, 0:n, :], PS[0:R, 4, 0:n * R].rearrange("p (t n) -> p t n", n=R),
                                                 ACT.Copy)
                            if u // E0 == T - 1:
                                ins = act.activation(PT[0:LAST, u % 2, T - 1, :], PS[0:LAST, 5, 0:R], ACT.Copy)
                            ins.then_inc(ptcopy.sem, 1)
                        if last_of_tile(i - 3):
                            t = (i - 3) // E0
                            act.wait_ge(cturn.sem, cturn.now(b, t + 1))
                            act.activation(cT[0:C], PS[0:C, 7, 0:KC * R].rearrange("p (c n) -> p c n", c=KC), ACT.Copy) \
                               .then_inc(ccopy.sem, 1)

            @block.tensor
            def _(pe):
                nm.turned.prime(pe)
                pe.wait_ge(ready, 5)
                pe.wait_ge(w_in, NW)
                xT = nm.xT
                with pe.Fori(0, B) as b:
                    pe.wait_ge(added.sem, added.before(b, T))
                    nm.pe(pe, b)
                    pe.wait_ge(nm.xT_ready.sem, nm.xT_ready.now(b, 3))

                    def halves(bank, rows_out, weights):
                        for a in range(2):
                            for c in range(KC):
                                ins = pe.matmul(PS[0:rows_out, bank + a, 0:HALF], weights(c),
                                                xT[0:kin(c), c, a * HALF:(a + 1) * HALF], start=c == 0, stop=c == KC - 1)
                        return ins

                    halves(3, HID, lambda c: wg1[0:kin(c), c, :]).then_inc(hidden.sem, 1)
                    halves(6, 128, lambda c: wqk[0:kin(c), c, 0:128]).then_inc(qkprod.sem, 1)
                    pe.wait_ge(relued.sem, relued.now(b, 1))
                    halves(3, 128, lambda c: wqk[0:kin(c), c, 128:256]).then_inc(qkprod.sem, 1)
                    for t in range(T):
                        ins = pe.matmul(PS[0:R, 5, t * E0:(t + 1) * E0], g1[:, t * R:(t + 1) * R], wg2[:], start=True, stop=True)
                    ins.then_inc(logits.sem, 1)
                    for t in range(T):
                        for c in range(KC):
                            ins = pe.matmul(PS[0:R, t // 2, t % 2 * D:(t % 2 + 1) * D], xT[0:kin(c), c, t * R:(t + 1) * R],
                                            wv[0:kin(c), c, :], start=c == 0, stop=c == KC - 1)
                        if t >= 3:
                            ins.then_inc(vprod.sem, 1)
                    pe.wait_ge(qkcopy.sem, qkcopy.now(b, 2))
                    halves(6, HD0, lambda c: wqk[0:kin(c), c, 256:320]).then_inc(qkprod.sem, 1)
                    pe.wait_ge(qkcopy.sem, qkcopy.now(b, 3))
                    halves(3, HD0, lambda c: wqk[0:kin(c), c, 320:384]).then_inc(qkprod.sem, 1)
                    pe.wait_ge(vcopy.sem, vcopy.now(b, 2))
                    pe.wait_ge(conv.sem, conv.now(b, 1))
                    pe.wait_ge(qkcopy.sem, qkcopy.now(b, 5))
                    for i in range(NU + 5):
                        if i < NU:
                            t, e, bank = i // E0, i % E0, 2 * (i % 2)
                            if i >= 2:
                                pe.wait_ge(prob.sem, prob.now(b, i - 1))
                            q = (qc[:, t * R:(t + 1) * R], q01[HD0:128, 1 + t * R:1 + (t + 1) * R], q2[:, t * R:(t + 1) * R])[e]
                            kk = (k01[0:HD0], k01[HD0:128], k2[:])[e]
                            nk, d0 = keys(i), t * R
                            pe.matmul(PS[0:R, bank, 0:min(nk, 512)], q, kk[:, 0:min(nk, 512)], start=True, stop=False)
                            if nk > 512:
                                pe.matmul(PS[0:R, bank + 1, 0:nk - 512], q, kk[:, 512:nk], start=True, stop=False)
                            m = min(nk, 512) - d0
                            ins = pe.matmul(PS[0:R, bank, d0:d0 + m], ident[0:R, 0:R], k.causal[:, 0:m], start=False, stop=True)
                            if nk > 512:
                                ins = pe.matmul(PS[0:R, bank + 1, 0:nk - 512], ident[0:R, 0:R], k.causal[:, m:m + nk - 512],
                                                start=False, stop=True)
                            ins.then_inc(score.sem, 1)
                        u = i - 2
                        if 0 <= u < NU:
                            t, e = u // E0, u % E0
                            pe.wait_ge(ptcopy.sem, ptcopy.now(b, u + 1))
                            if u >= 1:
                                pe.wait_ge(combined.sem, combined.now(b, u))
                            for kt in range(t + 1):
                                ins = pe.matmul(PS[0:R, 6, 0:HD0], PT[0:rows(kt), u % 2, kt, :],
                                                v[0:rows(kt), kt, e * HD0:(e + 1) * HD0], start=kt == 0, stop=kt == t)
                            ins.then_inc(pv.sem, 1)
                        u = i - 1
                        if 0 <= u < NU:
                            pe.wait_ge(prob.sem, prob.now(b, u + 1))
                            if u >= 1:
                                pe.wait_ge(ptcopy.sem, ptcopy.now(b, u))
                            for kt in range(u // E0 + 1):
                                n = rows(kt)
                                ins = pe.transpose(PS[0:n, 4 + kt // 4, kt % 4 * R:(kt % 4 + 1) * R],
                                                   P[:, u % 2, kt * R:kt * R + n], ident[0:R, 0:R])
                            ins.then_inc(turned.sem, 1)
                        if last_of_tile(i - 3):
                            t = (i - 3) // E0
                            pe.wait_ge(combined.sem, combined.now(b, i - 2))
                            if t >= 1:
                                pe.wait_ge(added.sem, added.now(b, t))
                            for c in range(KC):
                                ins = pe.transpose(PS[0:C, 7, c * R:(c + 1) * R], comb[:, t % 2, c * C:(c + 1) * C], ident[0:R, 0:R])
                            ins.then_inc(cturn.sem, 1)
                        if last_of_tile(i - 4):
                            t = (i - 4) // E0
                            pe.wait_ge(ccopy.sem, ccopy.now(b, t + 1))
                            for c in range(KC):
                                ins = pe.matmul(PS[0:R, 7, 256:256 + D], cT[0:kin(c), c, :], wp[0:kin(c), c, :],
                                                start=c == 0, stop=c == KC - 1)
                            ins.then_inc(yprod.sem, 1)


def talking_heads(k, A):
    nc, X, PS, ident = k.nc, k.X, k.PS, k.ident
    HALF, HK = NP // 2, N // 2
    HC = H // KC
    GQ = QT * QG
    outer = ExitStack()

    def keep(name, shape):
        return outer.enter_context(nc.sbuf_tensor("th_" + name, shape, F32))

    wT = [keep(n, [C + 1, KC, D]) for n in ("wq", "wk", "wv", "wo")]
    wq, wk, wv, wo = wT
    th1 = keep("th1", [C, KC, H])
    mix = keep("mix", [HQ + 1, H, QT])
    qg = keep("qg", [C + 1, 2, KC, H, QT])
    own = keep("own", [C, HC])

    with ExitStack() as ctx:
        b1 = ctx.enter_context(nc.sbuf_tensor("th_b1", [C + 1, H], F32))
        b2 = ctx.enter_context(nc.sbuf_tensor("th_b2", [1, 2, H * QT], F32))
        th2 = ctx.enter_context(nc.sbuf_tensor("th_th2", [HQ, H], F32))
        d3 = ctx.enter_context(nc.sbuf_tensor("th_d3", [HQ, H, QT], F32))
        d2 = ctx.enter_context(nc.sbuf_tensor("th_d2", [HQ, QT], F32))
        w_in, z, tr, cp = (nc.alloc_semaphore("th_" + n) for n in ("w_in", "z", "b2_in", "cp"))
        NW = 16 * (8 + KC * HC + H + 2)
        with nc.Block() as block:
            @block.sync
            def _(sp):
                for i, n in enumerate(("q", "k", "v", "o")):
                    sp.dma_start(wT[i][0:C], chunked(A[f"attn1_w{n}T"])).then_inc(w_in, 16)
                    sp.dma_start(wT[i][C:C + 1, KC - 1, :], row(A["L1_attn_b" + n])).then_inc(w_in, 16)
                for h in range(H):
                    hc, hh = h // HC, h % HC
                    sp.dma_start(th1[hh * HD:(hh + 1) * HD, hc, :], A["attn1_th1_wT"][h:h + 1].broadcast_to([HD, H])) \
                      .then_inc(w_in, 16)
                    sp.dma_start(th2[h * QT:(h + 1) * QT, :], A["attn1_th2_wT"][h:h + 1].broadcast_to([QT, H])).then_inc(w_in, 16)
                sp.dma_start(b1[C:C + 1, :], row(A["L1_attn_th1_b"])).then_inc(w_in, 16)
                sp.dma_start(b2[:, 1, 0:H], row(A["L1_attn_th2_b"])).then_inc(w_in, 16)
                sp.wait_ge(w_in, NW)
                sp.wait_ge(cp, 1)
                sp.dma_start(mix[HQ:HQ + 1, :, :].rearrange("p h n -> p (h n)"), b2[:, 0, :]).then_inc(tr, 16)
                sp.wait_ge(tr, 16)

            @block.gpsimd
            def _(pool):
                pool.memset(d3[:], 0.0).then_inc(z, 1)
                pool.memset(own[:], 1.0).then_inc(z, 1)
                pool.wait_ge(z, 2)
                pool.affine_select(out=d3[:], in_=d3[:], compare_op=ALU.not_equal, fill=1.0, base=0,
                                   pattern=[[-QT, H], [-1, QT]], channel_multiplier=1).then_inc(z, 1)
                pool.affine_select(out=own[:], in_=own[:], compare_op=ALU.is_ge, fill=0.0, base=0,
                                   pattern=[[-HD, HC]], channel_multiplier=1).then_inc(z, 1)
                pool.wait_ge(z, 4)
                pool.affine_select(out=own[:], in_=own[:], compare_op=ALU.is_gt, fill=0.0, base=HD,
                                   pattern=[[HD, HC]], channel_multiplier=-1).then_inc(z, 1)

            @block.vector
            def _(dve):
                dve.wait_ge(w_in, NW)
                dve.tensor_copy(b2[:, 0, :].rearrange("p (h n) -> p h n", n=QT),
                                b2[:, 1, 0:H].unsqueeze(2).broadcast_to([1, H, QT])).then_inc(cp, 1)
                for i in range(2):
                    dve.tensor_copy(qg[C:C + 1, i, KC - 1], b1[C:C + 1, :].unsqueeze(2).broadcast_to([1, H, QT]))
                dve.wait_ge(z, 5)
                dve.tensor_reduce(d2[:], d3[:].rearrange("p h n -> p n h"), AX.X, ALU.add).then_inc(cp, 1)
                dve.tensor_scalar(th1[:], th1[:], HD ** -0.5, None, ALU.mult).then_inc(cp, 1)
                dve.wait_ge(cp, 3)
                dve.tensor_tensor(mix[0:HQ], th2[:].unsqueeze(2).broadcast_to([HQ, H, QT]),
                                  d2[:].unsqueeze(1).broadcast_to([HQ, H, QT]), ALU.mult).then_inc(cp, 1)

    with ExitStack() as ctx:
        def sb(name, shape):
            return ctx.enter_context(nc.sbuf_tensor("th_" + name, shape, F32))

        nm = Norm(k, ctx, "th_")
        qT = sb("qT", [C, KC, NQ])
        kT = sb("kT", [C + 1, KC, NP])
        v = sb("v", [R, T, D])
        nmx = sb("nmx", [HQ, 2])
        rs = sb("rs", [128, 2])
        mixn = sb("mixn", [HQ + 1, 2, H, QT])
        P = sb("P", [HQ + 1, 2, N])
        P2 = sb("P2", [R, T, H, GQ])
        om = sb("om", [C, KC, HC, GQ])
        oT = sb("oT", [C + 1, KC, NQ])

        ready = nc.alloc_semaphore("th_ready")
        qprod = Signal(nc, "th_qprod", 2 * KC)
        qcopy = Signal(nc, "th_qcopy", 2 * KC)
        vprod = Signal(nc, "th_vprod", 2)
        vcopy = Signal(nc, "th_vcopy", 2)
        dvu = Signal(nc, "th_dvu", QG)
        qg_ready = Signal(nc, "th_qg", QG)
        score = Signal(nc, "th_score", QG, primed=True)
        bias = Signal(nc, "th_bias", QG)
        prob = Signal(nc, "th_prob", QG, primed=True)
        scaled = Signal(nc, "th_scaled", QG)
        mixed = Signal(nc, "th_mixed", QG, primed=True)
        p2copy = Signal(nc, "th_p2copy", QG, primed=True)
        pv = Signal(nc, "th_pv", KC, primed=True)
        masked = Signal(nc, "th_masked", KC, primed=True)
        summed = Signal(nc, "th_summed", KC)
        yprod = Signal(nc, "th_y", T)
        added = Signal(nc, "th_added", T, primed=True)

        with nc.Block() as block:
            def scale_queries(pool, tg, g, i):
                pool.wait_ge(score.sem, score.now(tg, i - 1))
                for c in range(KC):
                    stand(k, pool)
                    ins = pool.tensor_tensor(qg[0:C, i % 2, c], qT[:, c, bass.ds(g * GQ + i * QT, QT)].unsqueeze(1)
                                             .broadcast_to([C, H, QT]),
                                             th1[:, c, :].unsqueeze(2).broadcast_to([C, H, QT]), ALU.mult)
                ins.then_inc(qg_ready.sem, 1)

            @block.gpsimd
            def _(pool):
                for i, (a, x) in enumerate(((nm.xT[C:C + 1, :, :], 1.0), (kT[C:C + 1, :, :], 1.0), (oT[C:C + 1, :, :], 1.0),
                                            (P[C:HQ + 1, :, :], 1.0), (rs[:], 1.0), (qT[:, :, NP:NQ], 0.0))):
                    pool.memset(a, x).then_inc(ready, 1)
                    pool.wait_ge(ready, i + 1)
                with pool.Fori(0, B) as b:
                    nm.pool(pool, b)
                    pool.wait_ge(qcopy.sem, qcopy.now(b, 2 * KC))
                    for i in range(2):
                        scale_queries(pool, b * NG, 0, i)
                    with pool.Fori(0, NG - 1) as g:
                        for i in range(2, QG + 2):
                            scale_queries(pool, b * NG + g, g, i)
                    for i in range(2, QG):
                        scale_queries(pool, b * NG + (NG - 1), NG - 1, i)

            def largest(dve, tg, i):
                dve.wait_ge(score.sem, score.now(tg, i + 1))
                dve.tensor_reduce(nmx[:, i % 2:i % 2 + 1], PS[0:HQ, 2 * (i % 2):2 * (i % 2) + 2, 0:HK], AX.XY,
                                  ALU.max, negate=True).then_inc(bias.sem, 1)

            def scale_mix(dve, tg, i):
                p = i % 2
                dve.wait_ge(prob.sem, prob.now(tg, i + 1))
                dve.wait_ge(mixed.sem, mixed.now(tg, i - 1))
                dve.reciprocal(rs[0:HQ, p:p + 1], rs[0:HQ, p:p + 1]).then_inc(dvu.sem, 1)
                dve.wait_ge(dvu.sem, dvu.now(tg, i + 1))
                dve.tensor_scalar(mixn[:, p], mix[:], rs[0:HQ + 1, p:p + 1], None, ALU.mult).then_inc(scaled.sem, 1)

            def own_heads(dve, tg, g):
                for c in range(KC):
                    dve.wait_ge(pv.sem, pv.now(tg, c + 1))
                    dve.tensor_tensor(om[:, c], PS[0:C, 6 + c, 0:HC * GQ].rearrange("p (h n) -> p h n", n=GQ),
                                      own[:].unsqueeze(2).broadcast_to([C, HC, GQ]), ALU.mult).then_inc(masked.sem, 1)
                    dve.wait_ge(masked.sem, masked.now(tg, c + 1))
                    stand(k, dve)
                    dve.tensor_reduce(oT[0:C, c, bass.ds(g * GQ, GQ)], om[:, c].rearrange("p h n -> p n h"), AX.X,
                                      ALU.add).then_inc(summed.sem, 1)

            @block.vector
            def _(dve):
                added.prime(dve)
                masked.prime(dve)
                dve.wait_ge(ready, 6)
                with dve.Fori(0, B) as b:
                    nm.dve(dve, b)
                    for i in range(2 * KC):
                        dst = (qT if i < KC else kT)[0:C, i % KC, 0:NP]
                        bank = 4 + 2 * (i % 2)
                        dve.wait_ge(qprod.sem, qprod.now(b, i + 1))
                        dve.tensor_copy(dst.rearrange("p (a n) -> p a n", a=2), PS[0:C, bank:bank + 2, 0:HALF]) \
                           .then_inc(qcopy.sem, 1)
                    largest(dve, b * NG, 0)
                    largest(dve, b * NG, 1)
                    scale_mix(dve, b * NG, 0)
                    with dve.Fori(0, NG - 1) as g:
                        for i in range(QG):
                            scale_mix(dve, b * NG + g, i + 1)
                            largest(dve, b * NG + g, i + 2)
                        own_heads(dve, b * NG + g, g)
                    for i in range(QG - 1):
                        scale_mix(dve, b * NG + (NG - 1), i + 1)
                        if i + 2 < QG:
                            largest(dve, b * NG + (NG - 1), i + 2)
                    own_heads(dve, b * NG + (NG - 1), NG - 1)
                    for t in range(T):
                        dve.wait_ge(yprod.sem, yprod.now(b, t + 1))
                        dve.tensor_tensor(X[:, b * T + t, :], PS[0:R, t, 0:D], X[:, b * T + t, :], ALU.add) \
                           .then_inc(added.sem, 1)

            def exponentials(act, tg, i):
                act.wait_ge(bias.sem, bias.now(tg, i + 1))
                act.wait_ge(mixed.sem, mixed.now(tg, i - 1))
                act.activation(P[0:HQ, i % 2, :].rearrange("p (a n) -> p a n", a=2),
                               PS[0:HQ, 2 * (i % 2):2 * (i % 2) + 2, 0:HK], ACT.Exp,
                               bias=nmx[:, i % 2:i % 2 + 1], accum_out=rs[0:HQ, i % 2:i % 2 + 1]).then_inc(prob.sem, 1)

            def keep_mixed(act, tg, i):
                act.wait_ge(mixed.sem, mixed.now(tg, i + 1))
                if i == 0:
                    act.wait_ge(pv.sem, pv.before(tg, KC))
                act.activation(P2[:, 0:4, :, i * QT:(i + 1) * QT],
                               PS[0:R, 4, 0:4 * HQ].rearrange("p (t h n) -> p t h n", t=4, h=H), ACT.Copy)
                act.activation(P2[0:LAST, 4, :, i * QT:(i + 1) * QT],
                               PS[0:LAST, 5, 0:HQ].rearrange("p (h n) -> p h n", h=H), ACT.Copy).then_inc(p2copy.sem, 1)

            @block.scalar
            def _(act):
                prob.prime(act)
                p2copy.prime(act)
                with act.Fori(0, B) as b:
                    act.wait_ge(added.sem, added.before(b, T))
                    nm.act(act, b)
                    act.wait_ge(vprod.sem, vprod.now(b, 1))
                    act.activation(v[:, 0:4, :].rearrange("p (a t) d -> p a (t d)", a=2), PS[0:R, 0:2, 0:2 * D], ACT.Copy) \
                       .then_inc(vcopy.sem, 1)
                    act.wait_ge(vprod.sem, vprod.now(b, 2))
                    act.activation(v[:, 4, :], PS[0:R, 2, 0:D], ACT.Copy).then_inc(vcopy.sem, 1)
                    exponentials(act, b * NG, 0)
                    exponentials(act, b * NG, 1)
                    with act.Fori(0, NG - 1) as g:
                        for i in range(QG):
                            keep_mixed(act, b * NG + g, i)
                            exponentials(act, b * NG + g, i + 2)
                    for i in range(QG):
                        keep_mixed(act, b * NG + (NG - 1), i)
                        if i + 2 < QG:
                            exponentials(act, b * NG + (NG - 1), i + 2)

            def scores(pe, tg, i):
                bank = 2 * (i % 2)
                pe.wait_ge(qg_ready.sem, qg_ready.now(tg, i + 1))
                pe.wait_ge(prob.sem, prob.now(tg, i - 1))
                for c in range(KC):
                    for a in range(2):
                        ins = pe.matmul(PS[0:HQ, bank + a, 0:HK], qg[0:kin(c), i % 2, c],
                                        kT[0:kin(c), c, a * HK:(a + 1) * HK], start=c == 0, stop=c == KC - 1)
                ins.then_inc(score.sem, 1)

            def mixing(pe, tg, i):
                pe.wait_ge(scaled.sem, scaled.now(tg, i + 1))
                pe.wait_ge(p2copy.sem, p2copy.now(tg, i))
                for t in range(T):
                    ins = pe.matmul(PS[0:rows(t), 4 + t // 4, t % 4 * HQ:(t % 4 + 1) * HQ],
                                    P[:, i % 2, t * R:t * R + rows(t)], mixn[:, i % 2], start=True, stop=True)
                ins.then_inc(mixed.sem, 1)

            def values(pe, tg):
                pe.wait_ge(p2copy.sem, p2copy.now(tg, QG))
                for c in range(KC):
                    pe.wait_ge(masked.sem, masked.before(tg, c + 1))
                    for t in range(T):
                        ins = pe.matmul(PS[0:C, 6 + c, 0:HC * GQ], v[0:rows(t), t, c * C:(c + 1) * C],
                                        P2[0:rows(t), t, c * HC:(c + 1) * HC, :], start=t == 0, stop=t == T - 1)
                    ins.then_inc(pv.sem, 1)

            @block.tensor
            def _(pe):
                nm.turned.prime(pe)
                score.prime(pe)
                mixed.prime(pe)
                pv.prime(pe)
                pe.wait_ge(ready, 6)
                xT = nm.xT
                with pe.Fori(0, B) as b:
                    pe.wait_ge(added.sem, added.before(b, T))
                    nm.pe(pe, b)
                    pe.wait_ge(nm.xT_ready.sem, nm.xT_ready.now(b, 3))
                    for i in range(2 * KC):
                        w, co, bank = (wq if i < KC else wk), i % KC, 4 + 2 * (i % 2)
                        if i >= 2:
                            pe.wait_ge(qcopy.sem, qcopy.now(b, i - 1))
                        for a in range(2):
                            for c in range(KC):
                                ins = pe.matmul(PS[0:C, bank + a, 0:HALF], w[0:kin(c), c, co * C:(co + 1) * C],
                                                xT[0:kin(c), c, a * HALF:(a + 1) * HALF], start=c == 0, stop=c == KC - 1)
                        ins.then_inc(qprod.sem, 1)
                    for t in range(T):
                        for c in range(KC):
                            ins = pe.matmul(PS[0:R, t // 2, t % 2 * D:(t % 2 + 1) * D], xT[0:kin(c), c, t * R:(t + 1) * R],
                                            wv[0:kin(c), c, :], start=c == 0, stop=c == KC - 1)
                        if t >= 3:
                            ins.then_inc(vprod.sem, 1)
                    pe.wait_ge(qcopy.sem, qcopy.now(b, 2 * KC))
                    pe.wait_ge(vcopy.sem, vcopy.now(b, 2))
                    scores(pe, b * NG, 0)
                    scores(pe, b * NG, 1)
                    with pe.Fori(0, NG - 1) as g:
                        for i in range(QG):
                            mixing(pe, b * NG + g, i)
                            scores(pe, b * NG + g, i + 2)
                        values(pe, b * NG + g)
                    for i in range(QG):
                        mixing(pe, b * NG + (NG - 1), i)
                        if i + 2 < QG:
                            scores(pe, b * NG + (NG - 1), i + 2)
                    values(pe, b * NG + (NG - 1))
                    pe.wait_ge(summed.sem, summed.now(b * NG + (NG - 1), KC))
                    for t in range(T):
                        for c in range(KC):
                            ins = pe.matmul(PS[0:R, t, 0:D], oT[0:kin(c), c, t * R:(t + 1) * R], wo[0:kin(c), c, :],
                                            start=c == 0, stop=c == KC - 1)
                        ins.then_inc(yprod.sem, 1)
    outer.close()



def experts(k, A):
    nc, X, PS = k.nc, k.X, k.PS
    HALF = NP // 2
    NT = B * T
    tokens = nc.dram_tensor("ex_tokens", (NT * R, D), F32, kind="Internal").ap()
    listed = nc.dram_tensor("ex_listed", (SLOT_TILES * SL, 1), F32, kind="Internal").ap()
    outputs = nc.dram_tensor("ex_outputs", (SLOT_TILES * SL, D), F32, kind="Internal").ap()
    with ExitStack() as outer:
        def keep(name, shape, dt=F32):
            return outer.enter_context(nc.sbuf_tensor("ex_" + name, shape, dt))

        prob = keep("prob", [R, NT])
        rest = keep("rest", [R, NT])
        slot = keep("slot", [R, NT], U32)
        expert_of = keep("expert_of", [1, SLOT_TILES], I32)
        token_of = keep("token_of", [SL, SLOT_TILES], U32)
        ones = keep("ones", [1, SL])
        with ExitStack() as middle:
            xall = middle.enter_context(nc.sbuf_tensor("ex_xall", [C + 1, B, KC, NP], F32))
            with ExitStack() as ctx:
                chosen = ctx.enter_context(nc.sbuf_tensor("ex_chosen", [R, NT, E1], F32))
                route(k, A, xall, chosen, prob, rest, tokens)
                sort_tokens(k, chosen, slot, expert_of, listed)
            expert_of_all(k, A, xall, rest, slot, token_of, ones, listed)
        chosen_experts(k, A, token_of, expert_of, ones, tokens, outputs)
        add_chosen(k, prob, slot, outputs)


def route(k, A, xall, chosen, prob, rest, tokens):
    nc, PS = k.nc, k.PS
    with ExitStack() as ctx:
        def sb(name, shape):
            return ctx.enter_context(nc.sbuf_tensor("ex_" + name, shape, F32))

        ws = sb("ws", [C + 1, KC, E1])
        rank = sb("rank", [R, E1])
        true = sb("true", [R, T, E1])
        nm = Norm(k, ctx, "ex_")
        e = sb("e", [R, T, E1])
        mx = sb("mx", [R, T])
        sm = sb("sm", [R, T])
        pm = sb("pm", [R, T])
        w_in, ready = nc.alloc_semaphore("ex_w_in"), nc.alloc_semaphore("ex_ready")
        dv = Signal(nc, "ex_dv", 10)
        saved = Signal(nc, "ex_saved", 16, primed=True)
        logits = Signal(nc, "ex_logits", 1)
        exp_in = Signal(nc, "ex_exp_in", 1)
        exped = Signal(nc, "ex_exped", 1)
        kept = Signal(nc, "ex_kept", 1, primed=True)
        routed = Signal(nc, "ex_routed", 1, primed=True)
        with nc.Block() as block:
            @block.sync
            def _(sp):
                sp.dma_start(ws[0:C], chunked(A["L1_ffn_Ws"])).then_inc(w_in, 16)
                sp.dma_start(ws[C:C + 1, KC - 1, :], row(A["L1_ffn_bs"])).then_inc(w_in, 16)
                sp.wait_ge(w_in, 32)
                saved.prime(sp)
                with sp.Fori(0, B) as b:
                    sp.wait_ge(nm.xn_ready.sem, nm.xn_ready.now(b, T))
                    sp.dma_start(tokens[bass.ds(b * NP, NP), :].rearrange("(t r) d -> r t d", r=R),
                                 nm.xn[:]).then_inc(saved.sem, 16)
                sp.wait_ge(saved.sem, saved.now(B - 1, 16))

            @block.gpsimd
            def _(pool):
                kept.prime(pool)
                pool.memset(nm.xT[C:C + 1, :, :], 1.0).then_inc(ready, 1)
                pool.wait_ge(ready, 1)
                pool.iota(rank[:], pattern=[[-1, E1]], base=E1, channel_multiplier=0,
                          allow_small_or_imprecise_dtypes=True).then_inc(ready, 1)
                pool.wait_ge(ready, 2)
                pool.memset(true[:], 1.0).then_inc(ready, 1)
                pool.wait_ge(ready, 3)
                pool.affine_select(out=true[:, T - 1, :], in_=true[:, T - 1, :], compare_op=ALU.is_ge, fill=0.0,
                                   base=LAST - 1, pattern=[[0, E1]], channel_multiplier=-1).then_inc(ready, 1)
                with pool.Fori(0, B) as b:
                    nm.pool(pool, b)
                    pool.wait_ge(nm.xT_ready.sem, nm.xT_ready.now(b, 3))
                    stand(k, pool)
                    pool.tensor_copy(xall[:, b], nm.xT[:]).then_inc(kept.sem, 1)

            @block.vector
            def _(dve):
                routed.prime(dve)
                dve.wait_ge(ready, 4)
                with dve.Fori(0, B) as b:
                    dve.wait_ge(saved.sem, saved.before(b, 16))
                    nm.dve(dve, b)
                    step = Chain(dve, dv, b)

                    def wide(a):
                        return a[:].unsqueeze(2).broadcast_to([R, T, E1])

                    dve.wait_ge(logits.sem, logits.now(b, 1))
                    lg = PS[0:R, 3, 0:T * E1].rearrange("p (t e) -> p t e", e=E1)
                    step(dve.tensor_reduce(mx[:], lg, AX.X, ALU.max))
                    dve.tensor_tensor(e[:], lg, wide(mx), ALU.subtract).then_inc(exp_in.sem, 1)
                    dve.wait_ge(exped.sem, exped.now(b, 1))
                    step(dve.tensor_reduce(sm[:], e[:], AX.X, ALU.add))
                    step(dve.reciprocal(sm[:], sm[:]))
                    step(dve.tensor_tensor(e[:], e[:], wide(sm), ALU.mult))
                    step(dve.tensor_reduce(pm[:], e[:], AX.X, ALU.max))
                    step(dve.tensor_tensor(e[:], e[:], wide(pm), ALU.is_equal))
                    step(dve.tensor_tensor(e[:], e[:], rank[:].unsqueeze(1).broadcast_to([R, T, E1]), ALU.mult))
                    step(dve.tensor_reduce(mx[:], e[:], AX.X, ALU.max))
                    step(dve.tensor_tensor(e[:], e[:], wide(mx), ALU.is_equal))
                    dve.tensor_tensor(chosen[:, bass.ds(b * T, T), :], e[:], true[:], ALU.mult)
                    dve.tensor_copy(prob[:, bass.ds(b * T, T)], pm[:])
                    step(dve.tensor_scalar(rest[:, bass.ds(b * T, T)], pm[:], -1.0, 1.0, ALU.mult, ALU.add))
                    dve.sem_inc(routed.sem, 1)
                    step.end()

            @block.scalar
            def _(act):
                with act.Fori(0, B) as b:
                    act.wait_ge(routed.sem, routed.before(b, 1))
                    act.wait_ge(kept.sem, kept.before(b, 1))
                    nm.act(act, b)
                    act.wait_ge(exp_in.sem, exp_in.now(b, 1))
                    act.activation(e[:], e[:], ACT.Exp).then_inc(exped.sem, 1)

            @block.tensor
            def _(pe):
                nm.turned.prime(pe)
                pe.wait_ge(w_in, 32)
                pe.wait_ge(ready, 2)
                with pe.Fori(0, B) as b:
                    pe.wait_ge(routed.sem, routed.before(b, 1))
                    nm.pe(pe, b)
                    pe.wait_ge(nm.xT_ready.sem, nm.xT_ready.now(b, 3))
                    for t in range(T):
                        for c in range(KC):
                            ins = pe.matmul(PS[0:R, 3, t * E1:(t + 1) * E1], nm.xT[0:kin(c), c, t * R:(t + 1) * R],
                                            ws[0:kin(c), c, :], start=c == 0, stop=c == KC - 1)
                    ins.then_inc(logits.sem, 1)



def sort_tokens(k, chosen, slot, expert_of, listed):
    nc, PS = k.nc, k.PS
    NT = B * T
    HT = NT // 2
    JT = -(-B * N // SL)
    with ExitStack() as ctx:
        def sb(name, shape, dt=F32):
            return ctx.enter_context(nc.sbuf_tensor("so_" + name, shape, dt))

        below = sb("below", [R, R])
        every = sb("every", [R, R])
        zero = sb("zero", [SLOT_TILES, SL])
        total = sb("total", [R, NT, E1])
        ahead = [sb("ahead0", [R, NT, E1]), sb("ahead1", [R, NT, E1])]
        fill = sb("fill", [R, JT])
        count = sb("count", [R, E1])
        full = sb("full", [R, E1, JT])
        tiles = sb("tiles", [R, E1])
        end = sb("end", [R, E1 + 1])
        first = sb("first", [R, E1])
        number = sb("number", [R, SLOT_TILES])
        past = sb("past", [R, SLOT_TILES, E1 - 1])
        which = sb("which", [R, SLOT_TILES])
        at = sb("at", [R, NT])
        made, ones_in = nc.alloc_semaphore("so_made"), nc.alloc_semaphore("so_pool")
        counted = nc.alloc_semaphore("so_counted")
        zeroed = nc.alloc_semaphore("so_zeroed")
        done = nc.alloc_semaphore("so_dve")
        with nc.Block() as block:
            @block.gpsimd
            def _(pool):
                pool.memset(below[:], 1.0).then_inc(ones_in, 1)
                pool.memset(every[:], 1.0).then_inc(ones_in, 1)
                pool.memset(zero[:], 0.0).then_inc(ones_in, 1)
                pool.wait_ge(ones_in, 3)
                pool.affine_select(out=below[:], in_=below[:], compare_op=ALU.is_ge, fill=0.0, base=-1,
                                   pattern=[[1, R]], channel_multiplier=-1).then_inc(made, 1)
                pool.wait_ge(made, 1)
                pool.iota(fill[:], pattern=[[SL, JT]], base=0, channel_multiplier=0,
                          allow_small_or_imprecise_dtypes=True).then_inc(made, 1)
                pool.wait_ge(made, 2)
                pool.iota(number[:], pattern=[[1, SLOT_TILES]], base=0, channel_multiplier=0,
                          allow_small_or_imprecise_dtypes=True).then_inc(made, 1)

            @block.sync
            def _(sp):
                sp.wait_ge(ones_in, 3)
                sp.dma_start(listed.rearrange("(t p) o -> t (p o)", p=SL), zero[:]).then_inc(zeroed, 16)
                sp.wait_ge(zeroed, 16)

            @block.tensor
            def _(pe):
                pe.wait_ge(made, 1)
                for a in range(2):
                    sel = chosen[:, a * HT:(a + 1) * HT, :].rearrange("p t e -> p (t e)")
                    pe.matmul(PS[0:R, a, 0:HT * E1], below[:], sel, start=True, stop=True)
                    pe.matmul(PS[0:R, 2 + a, 0:HT * E1], every[:], sel, start=True, stop=True).then_inc(counted, 1)

            @block.vector
            def _(dve):
                n = 0

                def step(ins):
                    nonlocal n
                    n += 1
                    ins.then_inc(done, 1)
                    dve.wait_ge(done, n)

                dve.wait_ge(counted, 2)
                dve.wait_ge(made, 3)
                rank = PS[0:R, 0:2, 0:HT * E1].rearrange("p a (t e) -> p a t e", e=E1)
                tot = PS[0:R, 2:4, 0:HT * E1].rearrange("p a (t e) -> p a t e", e=E1)
                step(dve.tensor_copy(total[:].rearrange("p (a t) e -> p a t e", a=2), tot))
                a, o = ahead
                step(dve.memset(a[:, 0:1, :], 0.0))
                step(dve.tensor_copy(a[:, 1:NT, :], total[:, 0:NT - 1, :]))
                s = 1
                while s < NT:
                    step(dve.tensor_copy(o[:, 0:s, :], a[:, 0:s, :]))
                    step(dve.tensor_tensor(o[:, s:NT, :], a[:, s:NT, :], a[:, 0:NT - s, :], ALU.add))
                    a, o = o, a
                    s *= 2
                step(dve.tensor_tensor(count[:], a[:, NT - 1, :], total[:, NT - 1, :], ALU.add))
                step(dve.tensor_tensor(full[:], count[:].unsqueeze(2).broadcast_to([R, E1, JT]),
                                       fill[:].unsqueeze(1).broadcast_to([R, E1, JT]), ALU.is_gt))
                step(dve.tensor_reduce(tiles[:], full[:], AX.X, ALU.add))
                step(dve.memset(end[:, 0:1], 0.0))
                for e in range(E1):
                    step(dve.tensor_tensor(end[:, e + 1:e + 2], end[:, e:e + 1], tiles[:, e:e + 1], ALU.add))
                step(dve.tensor_scalar(first[:], end[:, 0:E1], float(SL), None, ALU.mult))
                step(dve.tensor_tensor(a[:], a[:], first[:].unsqueeze(1).broadcast_to([R, NT, E1]), ALU.add))
                step(dve.tensor_tensor(a[:].rearrange("p (a t) e -> p a t e", a=2), rank,
                                       a[:].rearrange("p (a t) e -> p a t e", a=2), ALU.add))
                step(dve.tensor_tensor(a[:], a[:], chosen[:], ALU.mult))
                step(dve.tensor_reduce(at[:], a[:], AX.X, ALU.add))
                step(dve.tensor_copy(slot[:], at[:]))
                step(dve.tensor_tensor(past[:], number[:].unsqueeze(2).broadcast_to([R, SLOT_TILES, E1 - 1]),
                                       end[:, 1:E1].unsqueeze(1).broadcast_to([R, SLOT_TILES, E1 - 1]), ALU.is_ge))
                step(dve.tensor_reduce(which[:], past[:], AX.X, ALU.add))
                step(dve.tensor_copy(expert_of[:], which[0:1, :]))


def expert_of_all(k, A, xall, rest, slot, token_of, ones, listed):
    nc, X, PS = k.nc, k.X, k.PS
    HALF = NP // 2
    NT = B * T
    with ExitStack() as ctx:
        def sb(name, shape, dt=F32):
            return ctx.enter_context(nc.sbuf_tensor("ea_" + name, shape, dt))

        w1 = sb("w1", [C + 1, KC, FF])
        w2 = sb("w2", [128, FC, D])
        b2 = sb("b2", [1, D])
        h = sb("h", [128, FC, NP])
        number = sb("number", [R, NT])
        mine = sb("mine", [R, T])
        where = sb("where", [R, T], U32)
        lists = sb("lists", [SLOT_TILES, SL])
        w_in = nc.alloc_semaphore("ea_w_in")
        hprod = Signal(nc, "ea_hprod", FC)
        gelu = Signal(nc, "ea_gelu", FC, primed=True)
        yprod = Signal(nc, "ea_yprod", T, primed=True)
        added = Signal(nc, "ea_added", T, primed=True)
        picked = Signal(nc, "ea_picked", 1)
        written = Signal(nc, "ea_written", 16 * T)
        ready = nc.alloc_semaphore("ea_ready")
        listed_in = nc.alloc_semaphore("ea_listed_in")
        turned = nc.alloc_semaphore("ea_turned")
        with nc.Block() as block:
            @block.sync
            def _(sp):
                sp.dma_start(w1[0:C], chunked(A["L1_ffn_W1"][0])).then_inc(w_in, 16)
                sp.dma_start(w1[C:C + 1, KC - 1, :], A["L1_ffn_b1"][0:1, :]).then_inc(w_in, 16)
                sp.dma_start(w2[:], A["L1_ffn_W2"][0].rearrange("(c p) n -> p c n", c=FC)).then_inc(w_in, 16)
                sp.dma_start(b2[:], A["L1_ffn_b2"][0:1, :]).then_inc(w_in, 16)

            @block.gpsimd
            def _(pool):
                pool.memset(ones[:], 1.0).then_inc(ready, 1)
                pool.wait_ge(ready, 1)
                pool.iota(number[:], pattern=[[R, NT]], base=0, channel_multiplier=1,
                          allow_small_or_imprecise_dtypes=True).then_inc(ready, 1)
                pool.wait_ge(ready, 2)
                with pool.Fori(0, B) as b:
                    pool.tensor_copy(mine[:], number[:, bass.ds(b * T, T)])
                    pool.tensor_copy(where[:], slot[:, bass.ds(b * T, T)]).then_inc(picked.sem, 1)
                    pool.wait_ge(picked.sem, picked.now(b, 1))
                    stand(k, pool)
                    for t in range(T):
                        pool.indirect_dma_start(listed, bass.IndirectOffsetOnAxis(ap=where[0:rows(t), t:t + 1], axis=0),
                                                mine[0:rows(t), t:t + 1], None).then_inc(written.sem, 16)
                    pool.wait_ge(written.sem, written.now(b, 16 * T))
                    stand(k, pool)
                pool.dma_start(lists[:], listed.rearrange("(t p) o -> t (p o)", p=SL)).then_inc(listed_in, 16)

            @block.vector
            def _(dve):
                added.prime(dve)
                with dve.Fori(0, B) as b:
                    for t in range(T):
                        dve.wait_ge(yprod.sem, yprod.now(b, t + 1))
                        stand(k, dve)
                        xt = X[:, b * T + t, :]
                        dve.scalar_tensor_tensor(xt, PS[0:R, 4 + t % 4, 0:D], rest[:, bass.ds(b * T + t, 1)], xt,
                                                 ALU.mult, ALU.add).then_inc(added.sem, 1)
                dve.wait_ge(turned, 1)
                dve.tensor_copy(token_of[:], PS[:, 0, 0:SLOT_TILES])

            @block.scalar
            def _(act):
                gelu.prime(act)
                with act.Fori(0, B) as b:
                    for f in range(FC):
                        act.wait_ge(hprod.sem, hprod.now(b, f + 1))
                        if f == 0:
                            act.wait_ge(yprod.sem, yprod.before(b, T))
                        bank = 2 * (f % 2)
                        act.activation(h[:, f, :].rearrange("p (a n) -> p a n", a=2), PS[:, bank:bank + 2, 0:HALF],
                                       ACT.Gelu).then_inc(gelu.sem, 1)

            @block.tensor
            def _(pe):
                yprod.prime(pe)
                pe.wait_ge(ready, 1)
                pe.wait_ge(w_in, 64)
                with pe.Fori(0, B) as b:
                    for f in range(FC):
                        bank = 2 * (f % 2)
                        pe.wait_ge(gelu.sem, gelu.now(b, f - 1) if f >= 2 else gelu.before(b, FC - 1 + f))
                        stand(k, pe)
                        for c in range(KC):
                            for a in range(2):
                                ins = pe.matmul(PS[:, bank + a, 0:HALF], w1[0:kin(c), c, f * 128:(f + 1) * 128],
                                                xall[0:kin(c), b, c, a * HALF:(a + 1) * HALF], start=c == 0, stop=c == KC - 1)
                        ins.then_inc(hprod.sem, 1)
                    for t in range(T):
                        if t % 4 == 0:
                            pe.wait_ge(added.sem, added.now(b, 1) if t else added.before(b, T))
                        for f in range(FC):
                            if t == 0:
                                pe.wait_ge(gelu.sem, gelu.now(b, f + 1))
                            pe.matmul(PS[0:R, 4 + t % 4, 0:D], h[:, f, t * R:(t + 1) * R], w2[:, f, :], start=f == 0, stop=False)
                        pe.matmul(PS[0:R, 4 + t % 4, 0:D], ones[:, 0:R], b2[:], start=False, stop=True).then_inc(yprod.sem, 1)
                pe.wait_ge(listed_in, 16)
                pe.wait_ge(gelu.sem, gelu.now(B - 1, FC))
                pe.transpose(PS[:, 0, 0:SLOT_TILES], lists[:], k.ident[0:SLOT_TILES, 0:SLOT_TILES]).then_inc(turned, 1)


def chosen_experts(k, A, token_of, expert_of, ones, tokens, outputs):
    nc, PS, ident = k.nc, k.PS, k.ident
    HF = FF // 2
    with ExitStack() as ctx:
        def sb(name, shape, dt=F32):
            return ctx.enter_context(nc.sbuf_tensor("ce_" + name, shape, dt))

        w1 = sb("w1", [C + 1, E1, KC, FF])
        w2 = sb("w2", [128, E1, FC, D])
        b2 = sb("b2", [1, E1, D])
        here = sb("here", [SL, 1], U32)
        x = sb("x", [SL, D])
        xT = sb("xT", [C + 1, KC, SL])
        h = sb("h", [SL, FF])
        hT = sb("hT", [128, FC, SL])
        y = sb("y", [SL, D])
        w_in, ready = nc.alloc_semaphore("ce_w_in"), nc.alloc_semaphore("ce_ready")
        picked = Signal(nc, "ce_picked", 1)
        gathered = Signal(nc, "ce_gathered", 16)
        xturned = Signal(nc, "ce_xturned", 1, primed=True)
        xcopied = Signal(nc, "ce_xcopied", 1, primed=True)
        hprod = Signal(nc, "ce_hprod", 1, primed=True)
        gelu = Signal(nc, "ce_gelu", 1)
        hturned = Signal(nc, "ce_hturned", 1, primed=True)
        hcopied = Signal(nc, "ce_hcopied", 1)
        yprod = Signal(nc, "ce_yprod", 1, primed=True)
        ycopied = Signal(nc, "ce_ycopied", 1, primed=True)
        stored = Signal(nc, "ce_stored", 16, primed=True)
        NW = 16 * (2 * E1 + 2)
        with nc.Block() as block:
            @block.sync
            def _(sp):
                for e in range(E1):
                    sp.dma_start(w1[0:C, e], chunked(A["L1_ffn_W1"][e])).then_inc(w_in, 16)
                    sp.dma_start(w2[:, e], A["L1_ffn_W2"][e].rearrange("(c p) n -> p c n", c=FC)).then_inc(w_in, 16)
                sp.dma_start(w1[C:C + 1, :, KC - 1, :], A["L1_ffn_b1"].rearrange("e (a n) -> a e n", a=1)).then_inc(w_in, 16)
                sp.dma_start(b2[:], A["L1_ffn_b2"].rearrange("e (a n) -> a e n", a=1)).then_inc(w_in, 16)
                stored.prime(sp)
                with sp.Fori(0, SLOT_TILES) as i:
                    sp.wait_ge(ycopied.sem, ycopied.now(i, 1))
                    sp.dma_start(outputs[bass.ds(i * SL, SL), :], y[:]).then_inc(stored.sem, 16)
                sp.wait_ge(stored.sem, stored.now(SLOT_TILES - 1, 16))

            @block.gpsimd
            def _(pool):
                pool.memset(xT[C:C + 1, :, :], 1.0).then_inc(ready, 1)
                pool.wait_ge(ready, 1)
                with pool.Fori(0, SLOT_TILES) as i:
                    pool.tensor_copy(here[:], token_of[:, bass.ds(i, 1)]).then_inc(picked.sem, 1)
                    pool.wait_ge(picked.sem, picked.now(i, 1))
                    pool.wait_ge(xturned.sem, xturned.before(i, 1))
                    stand(k, pool)
                    pool.indirect_dma_start(x[:], None, tokens, bass.IndirectOffsetOnAxis(ap=here[:], axis=0)) \
                        .then_inc(gathered.sem, 16)
                    pool.wait_ge(gathered.sem, gathered.now(i, 16))
                    stand(k, pool)

            def turn_tokens(pe, i):
                pe.wait_ge(gathered.sem, gathered.now(i, 16))
                pe.wait_ge(xcopied.sem, xcopied.before(i, 1))
                for c in range(KC):
                    ins = pe.transpose(PS[0:C, 0, c * SL:(c + 1) * SL], x[:, c * C:(c + 1) * C], ident[:])
                ins.then_inc(xturned.sem, 1)

            def first_product(pe, i):
                e = pe.value_load(expert_of[0:1, bass.ds(i, 1)], min_val=0, max_val=E1 - 1)
                pe.wait_ge(xcopied.sem, xcopied.now(i, 1))
                stand(k, pe)
                for c in range(KC):
                    for a in range(2):
                        ins = pe.matmul(PS[:, 2 + a, 0:HF], xT[0:kin(c), c, :], w1[0:kin(c), e, c, a * HF:(a + 1) * HF],
                                        start=c == 0, stop=c == KC - 1)
                ins.then_inc(hprod.sem, 1)

            def turn_gelu(pe, i):
                pe.wait_ge(gelu.sem, gelu.now(i, 1))
                for f in range(FC):
                    ins = pe.transpose(PS[:, 4 + f // 3, f % 3 * SL:(f % 3 + 1) * SL], h[:, f * 128:(f + 1) * 128], ident[:])
                ins.then_inc(hturned.sem, 1)

            def second_product(pe, i):
                e = pe.value_load(expert_of[0:1, bass.ds(i, 1)], min_val=0, max_val=E1 - 1)
                pe.wait_ge(hcopied.sem, hcopied.now(i, 1))
                pe.wait_ge(ycopied.sem, ycopied.before(i, 1))
                stand(k, pe)
                for f in range(FC):
                    pe.matmul(PS[:, 6, 0:D], hT[:, f, :], w2[:, e, f, :], start=f == 0, stop=False)
                pe.matmul(PS[:, 6, 0:D], ones[:], b2[:, e, :], start=False, stop=True).then_inc(yprod.sem, 1)

            @block.tensor
            def _(pe):
                for s in (xturned, hprod, hturned, yprod):
                    s.prime(pe)
                pe.wait_ge(w_in, NW)
                pe.wait_ge(ready, 1)
                turn_tokens(pe, 0)
                first_product(pe, 0)
                with pe.Fori(0, SLOT_TILES - 1) as j:
                    turn_tokens(pe, j + 1)
                    turn_gelu(pe, j)
                    first_product(pe, j + 1)
                    second_product(pe, j)
                turn_gelu(pe, SLOT_TILES - 1)
                second_product(pe, SLOT_TILES - 1)

            @block.scalar
            def _(act):
                xcopied.prime(act)
                with act.Fori(0, SLOT_TILES) as i:
                    act.wait_ge(xturned.sem, xturned.now(i, 1))
                    act.wait_ge(hprod.sem, hprod.before(i, 1))
                    act.activation(xT[0:C, :, :], PS[0:C, 0, 0:KC * SL].rearrange("p (c n) -> p c n", c=KC), ACT.Copy) \
                       .then_inc(xcopied.sem, 1)
                    act.wait_ge(hprod.sem, hprod.now(i, 1))
                    act.wait_ge(hturned.sem, hturned.before(i, 1))
                    act.activation(h[:].rearrange("p (a n) -> p a n", a=2), PS[:, 2:4, 0:HF], ACT.Gelu).then_inc(gelu.sem, 1)

            @block.vector
            def _(dve):
                ycopied.prime(dve)
                with dve.Fori(0, SLOT_TILES) as i:
                    dve.wait_ge(hturned.sem, hturned.now(i, 1))
                    dve.wait_ge(yprod.sem, yprod.before(i, 1))
                    dve.tensor_copy(hT[:].rearrange("p (a f) n -> p a (f n)", a=2), PS[:, 4:6, 0:FC // 2 * SL]) \
                       .then_inc(hcopied.sem, 1)
                    dve.wait_ge(yprod.sem, yprod.now(i, 1))
                    dve.wait_ge(stored.sem, stored.before(i, 16))
                    dve.tensor_copy(y[:], PS[:, 6, 0:D]).then_inc(ycopied.sem, 1)


def add_chosen(k, prob, slot, outputs):
    nc, X = k.nc, k.X
    with ExitStack() as ctx:
        y = [ctx.enter_context(nc.sbuf_tensor(f"ad_y{t}", [R, D], F32)) for t in range(T)]
        where = ctx.enter_context(nc.sbuf_tensor("ad_where", [R, T], U32))
        picked = Signal(nc, "ad_picked", 1)
        gathered = [Signal(nc, f"ad_gathered{t}", 16) for t in range(T)]
        added = Signal(nc, "ad_added", T, primed=True)
        with nc.Block() as block:
            @block.gpsimd
            def _(pool):
                with pool.Fori(0, B) as b:
                    pool.wait_ge(added.sem, added.before(b, T))
                    stand(k, pool)
                    pool.tensor_copy(where[:], slot[:, bass.ds(b * T, T)]).then_inc(picked.sem, 1)
                    pool.wait_ge(picked.sem, picked.now(b, 1))
                    stand(k, pool)
                    for t in range(T):
                        pool.indirect_dma_start(y[t][:], None, outputs, bass.IndirectOffsetOnAxis(ap=where[:, t:t + 1], axis=0)) \
                            .then_inc(gathered[t].sem, 16)

            @block.vector
            def _(dve):
                added.prime(dve)
                with dve.Fori(0, B) as b:
                    for t in range(T):
                        dve.wait_ge(gathered[t].sem, gathered[t].now(b, 16))
                        stand(k, dve)
                        xt = X[:, b * T + t, :]
                        dve.scalar_tensor_tensor(xt, y[t][:], prob[:, bass.ds(b * T + t, 1)], xt, ALU.mult, ALU.add) \
                           .then_inc(added.sem, 1)


def store(k, out):
    with k.nc.Block() as block:
        stored = k.nc.alloc_semaphore("stored")

        @block.sync
        def _(sp):
            dst = out.rearrange("b n d -> n b d")
            for t in range(T):
                sp.dma_start(dst[t * R:t * R + rows(t)], k.X[0:rows(t), t::T, :]).then_inc(stored, 16)
            sp.wait_ge(stored, 16 * T)


def phase(k, run, *args):
    nc = k.nc
    free = set(nc.free_semaphores)
    run(k, *args)
    nc.clear_and_free_semaphores(sorted(free - set(nc.free_semaphores)))
    nc.all_engine_barrier()


def build(nc, A, out, stages=99):
    k = Core()
    k.nc = nc
    setup(k, A)
    phase(k, patch_tokens, A)
    if stages >= 1:
        phase(k, performer, A)
    if stages >= 2:
        phase(k, gated_attention, A)
    if stages >= 3:
        phase(k, talking_heads, A)
    if stages >= 4:
        experts(k, A)
    store(k, out)


_AS_IS = ["txt", "L0_tok_conv_w", "L0_tok_conv_b", "L0_tok_proj_b", "L0_tok_pos_emb", "L0_attn_W_qkv",
          "L0_attn_W_proj", "L0_attn_b_proj", "L0_ffn_Wqk", "L0_ffn_bqk", "L0_ffn_Wv", "L0_ffn_bv", "L0_ffn_conv_w",
          "L0_ffn_conv_b", "L0_ffn_Wg1", "L0_ffn_bg1", "L0_ffn_Wg2", "L0_ffn_bg2", "L0_ffn_Wp", "L0_ffn_bp",
          "L1_attn_bq", "L1_attn_bk", "L1_attn_bv", "L1_attn_bo", "L1_attn_th1_b", "L1_attn_th2_b", "L1_ffn_Ws",
          "L1_ffn_bs", "L1_ffn_W1", "L1_ffn_b1", "L1_ffn_W2", "L1_ffn_b2"]


def _patches(a):
    lead = a.shape[:-3]
    n = len(lead)
    a = a.reshape(*lead, CH, SIDE, PATCH, SIDE, PATCH)
    return a.transpose(*range(n), n + 1, n + 3, n, n + 2, n + 4).reshape(*lead, NPATCH, PIX)


def layout(inputs):
    laid = {name: inputs[name] for name in _AS_IS}
    laid["x_patches"] = _patches(inputs["x"])
    laid["tok_ln_w_patches"] = _patches(inputs["L0_tok_ln_w"])
    laid["tok_ln_b_patches"] = _patches(inputs["L0_tok_ln_b"])
    laid["tok_proj_wT"] = inputs["L0_tok_proj_w"].T
    laid["attn_proj_matT"] = inputs["L0_attn_proj_mat"].T
    for n in ("wq", "wk", "wv", "wo", "th1_w", "th2_w"):
        laid[f"attn1_{n}T"] = inputs["L1_attn_" + n].T
    return laid


def kernel(**inputs):
    import numpy as _np
    import concourse.bacc as _bacc
    from concourse import mybir as _mybir
    from concourse.bass_utils import run_bass_kernel_spmd as _run

    nc = _bacc.Bacc("TRN2", target_bir_lowering=False, num_devices=1)
    arrays, args = {}, {}
    for name, a in layout({n: _np.asarray(a) for n, a in inputs.items()}).items():
        a = _np.ascontiguousarray(a)
        arrays[f"in_{name}"] = a
        args[name] = nc.dram_tensor(f"in_{name}", a.shape, _mybir.dt.from_np(a.dtype), kind="ExternalInput").ap()
    out = nc.dram_tensor("out_h", (B, N, D), F32, kind="ExternalOutput").ap()
    build(nc, args, out)
    r = _run(nc, [arrays], core_ids=[0])
    return r.results[0]["out_h"]
```
